# Optimizing a Trainium2 kernel written in Bass

```python
import numpy as np
import jax
import jax.numpy as jnp

def _softmax(x, axis=-1):
    return jax.nn.softmax(x, axis=axis)

def _gelu(x):
    return jax.nn.gelu(x, approximate=True)

def _silu(x):
    return jax.nn.silu(x)

def _sigmoid(x):
    return jax.nn.sigmoid(x)

def _layernorm(x, axis=-1, eps=1e-05):
    m = jnp.mean(x, axis=axis, keepdims=True)
    v = jnp.var(x, axis=axis, keepdims=True)
    return (x - m) / jnp.sqrt(v + eps)

def _scatter_add(tgt, idx, src, axis=0):
    return tgt.at[idx].add(src)

def _segment_sum(src, seg, n):
    return jax.ops.segment_sum(src, seg, n)
kernel_name = 'mk_prb_d1_jaxref_r8_ed62f4'

def setup_inputs(seed: int=0):
    np.random.seed(seed)
    _w = jnp.asarray

    def _L0_attn_setup():
        import jax, jax.numpy as jnp
        import numpy as np
        D_MODEL = 128
        D_STATE = 16
        D_CONV = 4
        EXPAND = 2
        D_INNER = EXPAND * D_MODEL
        DT_RANK = (D_MODEL + 15) // 16
        BATCH = 2
        SEQLEN = 128

        def _causal_conv_silu(x, w, b):
            k = w.shape[-1]
            y = jax.lax.conv_general_dilated(x, w, window_strides=(1,), padding=[(k - 1, 0)], dimension_numbers=('NCH', 'OIH', 'NCH'), feature_group_count=x.shape[1])
            return jax.nn.silu(y + b[None, :, None])

        def _ssm_scan(dA, dBx):

            def op(e1, e2):
                a1, b1 = e1
                a2, b2 = e2
                return (a1 * a2, a2 * b1 + b2)
            return jax.lax.associative_scan(op, (dA, dBx), axis=2)[1]

        def _mamba_dir(xz, conv_w, conv_b, xproj_w, dtproj_w, dt_bias, A_log, Dp):
            d_inner = xz.shape[1] // 2
            x, z = (xz[:, :d_inner], xz[:, d_inner:])
            u = _causal_conv_silu(x, conv_w, conv_b)
            x_dbl = jnp.einsum('bdl,kd->bkl', u, xproj_w)
            n = A_log.shape[1]
            r = dtproj_w.shape[1]
            delta = jnp.einsum('dr,brl->bdl', dtproj_w, x_dbl[:, :r])
            Bm = x_dbl[:, r:r + n]
            Cm = x_dbl[:, r + n:]
            delta = jax.nn.softplus(delta + dt_bias[None, :, None])
            A = -jnp.exp(A_log)
            dA = jnp.exp(jnp.einsum('bdl,dn->bdln', delta, A))
            dBx = jnp.einsum('bdl,bnl,bdl->bdln', delta, Bm, u)
            h = _ssm_scan(dA, dBx)
            y = jnp.einsum('bdln,bnl->bdl', h, Cm)
            y = y + Dp[None, :, None] * u
            return y * jax.nn.silu(z)
        key = jax.random.key(seed)
        ks = jax.random.split(key, 16)
        s_in = 1.0 / np.sqrt(D_MODEL)
        s_x = 1.0 / np.sqrt(D_INNER)
        dt_std = DT_RANK ** (-0.5)

        def dt_bias_init(k):
            dt = jnp.exp(jax.random.uniform(k, (D_INNER,)) * (np.log(0.1) - np.log(0.001)) + np.log(0.001))
            dt = jnp.clip(dt, 0.0001, None)
            return dt + jnp.log(-jnp.expm1(-dt))
        A_log = jnp.log(jnp.tile(jnp.arange(1, D_STATE + 1, dtype=jnp.float32)[None, :], (D_INNER, 1)))
        inp = {'hidden_states': jax.random.normal(ks[0], (BATCH, SEQLEN, D_MODEL), jnp.float32), 'in_proj_w': jax.random.normal(ks[1], (2 * D_INNER, D_MODEL), jnp.float32) * s_in, 'conv_w': jax.random.normal(ks[2], (D_INNER, 1, D_CONV), jnp.float32) * 0.3, 'conv_bias': jnp.zeros((D_INNER,), jnp.float32), 'x_proj_w': jax.random.normal(ks[3], (DT_RANK + 2 * D_STATE, D_INNER), jnp.float32) * s_x, 'dt_proj_w': jax.random.uniform(ks[4], (D_INNER, DT_RANK), jnp.float32, -dt_std, dt_std), 'dt_proj_bias': dt_bias_init(ks[5]), 'A_log': A_log, 'D_skip': jnp.ones((D_INNER,), jnp.float32), 'convb_w': jax.random.normal(ks[6], (D_INNER, 1, D_CONV), jnp.float32) * 0.3, 'convb_bias': jnp.zeros((D_INNER,), jnp.float32), 'x_proj_b_w': jax.random.normal(ks[7], (DT_RANK + 2 * D_STATE, D_INNER), jnp.float32) * s_x, 'dt_proj_b_w': jax.random.uniform(ks[8], (D_INNER, DT_RANK), jnp.float32, -dt_std, dt_std), 'dt_proj_b_bias': dt_bias_init(ks[9]), 'A_b_log': A_log, 'D_b_skip': jnp.ones((D_INNER,), jnp.float32), 'out_proj_w': jax.random.normal(ks[10], (D_MODEL, D_INNER), jnp.float32) * s_x}
        return inp
    _L0_attn_in = _L0_attn_setup()

    def _L0_ffn_setup():
        import jax, jax.numpy as jnp
        import numpy as np
        B, L, D = (4, 64, 128)
        E, TOP_K = (16, 4)
        F = 4 * D
        key = jax.random.key(seed)
        ks = jax.random.split(key, 6)
        scale = 0.02
        return {'x': jax.random.normal(ks[0], (B, L, D), jnp.float32), 'keys': jax.random.normal(ks[1], (E, D), jnp.float32), 'w1': jax.random.normal(ks[2], (E, F, D), jnp.float32) * scale, 'b1': jnp.zeros((E, F), jnp.float32), 'w2': jax.random.normal(ks[3], (E, D, F), jnp.float32) * scale, 'b2': jnp.zeros((E, D), jnp.float32), 'rw': jax.random.normal(ks[4], (E, D), jnp.float32) * scale, 'rb': jnp.zeros((E,), jnp.float32)}
    _L0_ffn_in = _L0_ffn_setup()
    _d = {'L0_attn_hidden_states': _L0_attn_in['hidden_states'], 'L0_attn_in_proj_w': _L0_attn_in['in_proj_w'], 'L0_attn_conv_w': _L0_attn_in['conv_w'], 'L0_attn_conv_bias': _L0_attn_in['conv_bias'], 'L0_attn_x_proj_w': _L0_attn_in['x_proj_w'], 'L0_attn_dt_proj_w': _L0_attn_in['dt_proj_w'], 'L0_attn_dt_proj_bias': _L0_attn_in['dt_proj_bias'], 'L0_attn_A_log': _L0_attn_in['A_log'], 'L0_attn_D_skip': _L0_attn_in['D_skip'], 'L0_attn_convb_w': _L0_attn_in['convb_w'], 'L0_attn_convb_bias': _L0_attn_in['convb_bias'], 'L0_attn_x_proj_b_w': _L0_attn_in['x_proj_b_w'], 'L0_attn_dt_proj_b_w': _L0_attn_in['dt_proj_b_w'], 'L0_attn_dt_proj_b_bias': _L0_attn_in['dt_proj_b_bias'], 'L0_attn_A_b_log': _L0_attn_in['A_b_log'], 'L0_attn_D_b_skip': _L0_attn_in['D_b_skip'], 'L0_attn_out_proj_w': _L0_attn_in['out_proj_w'], 'L0_ffn_keys': _L0_ffn_in['keys'], 'L0_ffn_w1': _L0_ffn_in['w1'], 'L0_ffn_b1': _L0_ffn_in['b1'], 'L0_ffn_w2': _L0_ffn_in['w2'], 'L0_ffn_b2': _L0_ffn_in['b2'], 'L0_ffn_rw': _L0_ffn_in['rw'], 'L0_ffn_rb': _L0_ffn_in['rb']}
    _x0 = _d['L0_attn_hidden_states']
    _d['L0_attn_hidden_states'] = jax.random.normal(jax.random.fold_in(jax.random.key(seed), 1), (8, 512, 128), dtype=_x0.dtype)
    del _x0
    return _d

def reference(L0_attn_hidden_states, L0_attn_in_proj_w, L0_attn_conv_w, L0_attn_conv_bias, L0_attn_x_proj_w, L0_attn_dt_proj_w, L0_attn_dt_proj_bias, L0_attn_A_log, L0_attn_D_skip, L0_attn_convb_w, L0_attn_convb_bias, L0_attn_x_proj_b_w, L0_attn_dt_proj_b_w, L0_attn_dt_proj_b_bias, L0_attn_A_b_log, L0_attn_D_b_skip, L0_attn_out_proj_w, L0_ffn_keys, L0_ffn_w1, L0_ffn_b1, L0_ffn_w2, L0_ffn_b2, L0_ffn_rw, L0_ffn_rb):

    def _L0_attn_ref(hidden_states, in_proj_w, conv_w, conv_bias, x_proj_w, dt_proj_w, dt_proj_bias, A_log, D_skip, convb_w, convb_bias, x_proj_b_w, dt_proj_b_w, dt_proj_b_bias, A_b_log, D_b_skip, out_proj_w):
        import jax, jax.numpy as jnp
        import numpy as np
        D_MODEL = 128
        D_STATE = 16
        D_CONV = 4
        EXPAND = 2
        D_INNER = EXPAND * D_MODEL
        DT_RANK = (D_MODEL + 15) // 16
        BATCH = 2
        SEQLEN = 128

        def _causal_conv_silu(x, w, b):
            k = w.shape[-1]
            y = jax.lax.conv_general_dilated(x, w, window_strides=(1,), padding=[(k - 1, 0)], dimension_numbers=('NCH', 'OIH', 'NCH'), feature_group_count=x.shape[1])
            return jax.nn.silu(y + b[None, :, None])

        def _ssm_scan(dA, dBx):

            def op(e1, e2):
                a1, b1 = e1
                a2, b2 = e2
                return (a1 * a2, a2 * b1 + b2)
            return jax.lax.associative_scan(op, (dA, dBx), axis=2)[1]

        def _mamba_dir(xz, conv_w, conv_b, xproj_w, dtproj_w, dt_bias, A_log, Dp):
            d_inner = xz.shape[1] // 2
            x, z = (xz[:, :d_inner], xz[:, d_inner:])
            u = _causal_conv_silu(x, conv_w, conv_b)
            x_dbl = jnp.einsum('bdl,kd->bkl', u, xproj_w)
            n = A_log.shape[1]
            r = dtproj_w.shape[1]
            delta = jnp.einsum('dr,brl->bdl', dtproj_w, x_dbl[:, :r])
            Bm = x_dbl[:, r:r + n]
            Cm = x_dbl[:, r + n:]
            delta = jax.nn.softplus(delta + dt_bias[None, :, None])
            A = -jnp.exp(A_log)
            dA = jnp.exp(jnp.einsum('bdl,dn->bdln', delta, A))
            dBx = jnp.einsum('bdl,bnl,bdl->bdln', delta, Bm, u)
            h = _ssm_scan(dA, dBx)
            y = jnp.einsum('bdln,bnl->bdl', h, Cm)
            y = y + Dp[None, :, None] * u
            return y * jax.nn.silu(z)
        xz = jnp.einsum('ed,bld->bel', in_proj_w, hidden_states)
        out_f = _mamba_dir(xz, conv_w, conv_bias, x_proj_w, dt_proj_w, dt_proj_bias, A_log, D_skip)
        out_b = _mamba_dir(xz[:, :, ::-1], convb_w, convb_bias, x_proj_b_w, dt_proj_b_w, dt_proj_b_bias, A_b_log, D_b_skip)[:, :, ::-1]
        return jnp.einsum('bdl,od->blo', out_f + out_b, out_proj_w)

    def _L0_ffn_ref(x, keys, w1, b1, w2, b2, rw, rb):
        import jax, jax.numpy as jnp
        import numpy as np
        B, L, D = (4, 64, 128)
        E, TOP_K = (16, 4)
        F = 4 * D
        diff = x[:, :, None, :] - keys
        dist2 = jnp.sum(diff * diff, axis=-1)
        logits = -dist2 + jnp.einsum('bld,ed->ble', x, rw) + rb
        topv, topi = jax.lax.top_k(logits, TOP_K)
        w = jax.nn.softmax(topv, axis=-1)
        hidden = jax.nn.gelu(jnp.einsum('bld,efd->blef', x, w1) + b1, approximate=False)
        exp_out = jnp.einsum('blef,edf->bled', hidden, w2) + b2
        sel = jnp.take_along_axis(exp_out, topi[..., None], axis=2)
        fused = jnp.sum(w[..., None] * sel, axis=2)
        return fused
    x = L0_attn_hidden_states
    xn = _layernorm(x, axis=-1)
    x = x + _L0_attn_ref(xn, L0_attn_in_proj_w, L0_attn_conv_w, L0_attn_conv_bias, L0_attn_x_proj_w, L0_attn_dt_proj_w, L0_attn_dt_proj_bias, L0_attn_A_log, L0_attn_D_skip, L0_attn_convb_w, L0_attn_convb_bias, L0_attn_x_proj_b_w, L0_attn_dt_proj_b_w, L0_attn_dt_proj_b_bias, L0_attn_A_b_log, L0_attn_D_b_skip, L0_attn_out_proj_w) + _L0_ffn_ref(xn, L0_ffn_keys, L0_ffn_w1, L0_ffn_b1, L0_ffn_w2, L0_ffn_b2, L0_ffn_rw, L0_ffn_rb)
    return x

_drawn_inputs = setup_inputs


def setup_inputs(seed=0):
    import zlib

    import numpy as np

    out = dict(_drawn_inputs(seed))
    spreads = {'L0_attn_conv_bias': (0.0, 0.1),
     'L0_attn_D_skip': (1.0, 0.6),
     'L0_attn_convb_bias': (0.0, 0.1),
     'L0_attn_D_b_skip': (1.0, 0.6),
     'L0_ffn_b1': (0.0, 2.0),
     'L0_ffn_b2': (0.0, 0.8),
     'L0_ffn_rb': (0.0, 2.0)}
    factors = {'L0_attn_x_proj_w': 6.798,
     'L0_attn_dt_proj_w': 8.0,
     'L0_attn_dt_proj_bias': 8.0,
     'L0_attn_A_log': 8.0,
     'L0_attn_x_proj_b_w': 7.257,
     'L0_attn_dt_proj_b_w': 8.0,
     'L0_attn_dt_proj_b_bias': 8.0,
     'L0_attn_A_b_log': 8.0,
     'L0_ffn_rw': 64.0,
     'L0_ffn_keys': 8.0,
     'L0_ffn_w1': 8.0,
     'L0_ffn_w2': 8.0}
    for name, (base, spread) in spreads.items():
        noise = np.random.default_rng([zlib.crc32(name.encode()), seed]).standard_normal(out[name].shape)
        drawn = base * np.exp(spread * noise) if base else spread * noise
        out[name] = jnp.asarray(drawn.astype(out[name].dtype))
    for name, factor in factors.items():
        out[name] = (out[name] * factor).astype(out[name].dtype)
    return out
```

```python
import numpy as np
import concourse.bass as bass
from concourse import mybir
from contextlib import ExitStack

F32 = mybir.dt.float32
BF16 = mybir.dt.bfloat16
I32 = mybir.dt.int32
U32 = mybir.dt.uint32
ALU = mybir.AluOpType
ACT = mybir.ActivationFunctionType
AXX = mybir.AxisListType.X

P = 128
D = 128
BATCH, L = 8, 512
TOK = BATCH * L
NT = TOK // P
TPB = L // P
DIN = 256
NH = DIN // P
ND = 2
DH = ND * NH
NS = 16
NR = 8
KC = 4
E, TOPK = 16, 4
FF = 512
FC = FF // P
S = 256
SH = S // P
NTILE = TOK * TOPK // S + E
NSLOT = NTILE * S
MPB = NTILE // BATCH
EPS = 1e-5
CH = KC + 3 + NS
BR = 96
W1W = FF + FC

C_ID, C_TRI, C_IOTA, C_THR, C_TILE = 0, 128, 256, 272, 288
C_MASK = C_TILE + NTILE
C_PART = C_MASK + NT * E
C_SEL = C_PART + 2
C_END = C_SEL + NS * P

PAIRS = NS // 2 * DH
DA_RING = 8
H_RING = 8
B_RING = 4
C_RING = 4
CPB = NS // 2 * ND
W_RING = 2
DECAYS = 2 * PAIRS
SUM_LAG = 5
EVAC_LAG = 6

GROUP = MPB // 2
T_STEP = [2 * j for j in range(MPB)]
D_STEP = [2 * GROUP + 2 + 2 * j for j in range(MPB)]
GELU_STEP = [T_STEP[GROUP - 1] + 1 + EVAC_LAG, T_STEP[MPB - 1] + 1 + EVAC_LAG]
GATE_STEP, MIX_STEP = SUM_LAG, 26
EVENTS = {q: [] for q in range(PAIRS)}
for _j in range(MPB):
    EVENTS[T_STEP[_j]].append(("T", _j, 0))
    EVENTS[T_STEP[_j] + 1] += [("U0", _j, 1), ("U1", _j, 0)]
    EVENTS[D_STEP[_j]].append(("D", _j, 1))
EVENTS[21].append(("G", 0, 0))
EVENTS[23].append(("G", 1, 0))
EVENTS[25].append(("O", 0, 0))
USES = [0, 0]
ORDER = {}
for _q in range(PAIRS):
    for _what, _j, _m in EVENTS[_q]:
        ORDER[_what, _j] = USES[_m]
        USES[_m] += 1
FINISH = NH + 1


def uses_before(b, m):
    if isinstance(b, int) and b == 0:
        return 0
    return USES[m] * b - (FINISH if m == 0 else 0)


LAST0 = USES[0] * BATCH - FINISH
ZERO_DMAS = NSLOT * D // (P * 2 * DH * L)
WTS_DMAS = 8
Y_RING = 8
DT_BANKS = (0, 1, 6, 7)
EXP_LN_SET = 6
PREP_LINKS = KC * DH - 1 + 3

SMALL = 1 / 32
LOG_SMALL = float(np.log1p(SMALL))
_nodes = SMALL / 2 * (1 + np.cos(np.pi * (2 * np.arange(3) + 1) / 6))
_c2, _c1, _c0 = (float(c) for c in np.polyfit(_nodes, np.log1p(_nodes) / _nodes, 2))
SQ_SCALE = float(np.sqrt(_c2))
SQ_BIAS = _c1 / (2 * SQ_SCALE)
SQ_REST = _c0 - SQ_BIAS ** 2
PREP_STORES = ("gate_out", "c_out", "parts_out", "skip_out", "delta_out", "du_out")


def wait(eng, semaphore, value):
    if not isinstance(value, int) or value > 0:
        eng.wait_ge(semaphore, value)


def bank_written(eng, sems, b, what, j, m):
    wait(eng, sems[f"m{m}_ready"], uses_before(b, m) + ORDER[what, j] + 1)


def bank_empty(eng, sems, b, what, j, m):
    wait(eng, sems[f"m{m}_free"], uses_before(b, m) + ORDER[what, j])


def build_kernel(nc, x_in, consts_in, chan_in, inw_in, xproj_in, dtw_in, outw_in,
                 route_in, b2_in, w1_in, w2_in, out):
    with ExitStack() as ctx:
        def sb(name, shape, dt=F32):
            return ctx.enter_context(nc.sbuf_tensor(name, shape, dt))

        def sem(name):
            return ctx.enter_context(nc.semaphore(name))

        def dram(name, shape, dt=F32):
            return nc.dram_tensor(name, shape, dt, kind="Internal").ap()

        delta_d = dram("delta_d", (BATCH, P, DH * L))
        du_d = dram("du_d", (BATCH, P, DH * L))
        gate_d = dram("gate_d", (BATCH, P, TPB * DIN))
        skip_d = dram("skip_d", (BATCH, P, TPB * DIN))
        parts_d = dram("parts_d", (BATCH, P, ND * L), BF16)
        c_d = dram("c_d", (BATCH, ND, NS, L))
        base_d = dram("base_d", (BATCH, P, TPB * D))
        mixed_d = dram("mixed_d", (BATCH, P, TPB * D))
        slots_d = dram("slots_d", (NSLOT, D))
        expert_d = dram("expert_d", (NSLOT, D))

        ident = sb("ident", [P, P])
        sel = sb("sel", [P, NS, P], BF16)
        chan = sb("chan", [P, DH, CH])
        half_taps = sb("half_taps", [P, DH, KC + 1])
        a_neg = sb("a_neg", [P, DH, NS])
        outw = sb("outw", [P, NH, D])
        pos = sb("pos", [P, NT * TOPK], I32)
        gates = sb("gates", [P, NT, TOPK])
        fit_bias = sb("fit_bias", [P, 1])
        tile_expert = sb("tile_expert", [P, NTILE], I32)

        delta = sb("delta", [P, 2, DH, L])
        du = sb("du", [P, 2, DH, L])
        gate = sb("gate", [P, 2, NH, TPB, P])
        skip = sb("skip", [P, 2, NH, TPB, P])
        base = sb("base", [P, 2, TPB * D])
        parts = sb("parts", [P, 2, ND, L], BF16)
        gated = sb("gated", [P, NH, TPB, P])
        gatedT = sb("gatedT", [P, NH, L])
        w1 = sb("w1", [P, W_RING, W1W])
        w2 = sb("w2", [P, W_RING, FC, D])
        rows = sb("rows", [P, W_RING, SH, D])
        rowsT = sb("rowsT", [P, S])
        yrows = sb("yrows", [P, W_RING, SH, D])
        mixed = sb("mixed", [P, TPB * D])

        ARENA = 31000
        arena = sb("arena", [P, ARENA])
        top = [0]

        def carve(n):
            at = top[0]
            top[0] += n
            assert top[0] <= ARENA, top[0]
            return arena[:, at:at + n]

        decay = carve(DA_RING * 2 * L).rearrange("p (r j l) -> p r j l", r=DA_RING, j=2)
        state = carve(H_RING * 2 * L).rearrange("p (r j l) -> p r j l", r=H_RING, j=2)
        c_rows = carve(C_RING * 2 * L).rearrange("p (r j l) -> p r j l", r=C_RING, j=2)
        hidden = carve(MPB * FC * S).rearrange("p (t f s) -> p t f s", t=MPB, f=FC)
        acc = state.rearrange("p r j l -> p (r j l)")[:, 0:TOK * D // P]
        y_tok = hidden.rearrange("p t f s -> p (t f s)")[:, 0:Y_RING * TOPK * D].rearrange("p (n d) -> p n d", d=D)
        top[0] = 0
        consts = carve(C_END)
        xnT = carve(TOK)
        inw = carve(2 * DIN)
        xproj = carve(ND * NH * (BR + NR)).rearrange("p (d h m) -> p d h m", d=ND, h=NH)
        dtw = carve(ND * DIN).rearrange("p (d c) -> p d c", d=ND)
        diag = carve(DH * P).rearrange("p (q m) -> p q m", q=DH)
        keys_sq = carve(E)
        route_w = carve(E)
        route_b = carve(E)
        route = carve(4 * E)
        b2 = carve(D)
        xn = carve(NT * D).rearrange("p (t d) -> p t d", t=NT)
        shared = top[0]
        x_all = carve(NT * D).rearrange("p (t d) -> p t d", t=NT)
        stats = carve(NT * 6).rearrange("p (t s) -> p t s", t=NT)
        mv = carve(NT * 2).rearrange("p (t s) -> p t s", t=NT)
        var_eps = carve(NT)
        std = carve(NT)
        rstd = carve(NT)
        logits = carve(NT * E)
        top8 = carve(NT * 8).rearrange("p (t k) -> p t k", t=NT)
        idx8 = carve(NT * 8).bitcast(U32).rearrange("p (t k) -> p t k", t=NT)
        idxf = carve(NT * TOPK)
        onehot = carve(NT * TOPK * E)
        product = carve(NT * TOPK * E)
        chosen = carve(NT * E // 2).bitcast(BF16)
        tri = carve(P // 2).bitcast(BF16)
        ones_b = carve(P // 2).bitcast(BF16)
        ones_f = carve(P)
        totals = carve(NT * E).rearrange("p (e t) -> p e t", e=E)
        upto = carve(NT * E).rearrange("p (e t) -> p e t", e=E)
        place = carve(NT * E)
        n_tiles = carve(E)
        end_tile = carve(E)
        slot0 = carve(E)
        compare = carve(E * NTILE)
        posf = carve(NT * TOPK)
        texp = carve(NTILE)
        gexp = carve(NT * TOPK)
        gsum = carve(NT)
        grec = carve(NT)
        mix_w = carve(NT * E)
        mix_wT = carve(TPB * P)
        base_t = carve(TPB * D)
        routing_end = top[0]
        top[0] = shared
        xb = carve(L)
        PADL = L + 2 * (KC - 1)
        xpad = carve(NH * PADL).rearrange("p (h l) -> p h l", h=NH)
        v = carve(DH * L).rearrange("p (q l) -> p q l", q=DH)
        th = carve(DH * L).rearrange("p (q l) -> p q l", q=DH)
        u = carve(DH * L).rearrange("p (q l) -> p q l", q=DH)
        xdbl = carve(ND * L).rearrange("p (d l) -> p d l", d=ND)
        part1 = carve(ND * L // 2).bitcast(BF16).rearrange("p (d l) -> p d l", d=ND)
        part2 = carve(ND * L // 2).bitcast(BF16).rearrange("p (d l) -> p d l", d=ND)
        rest = carve(ND * L).rearrange("p (d l) -> p d l", d=ND)
        parts_p = carve(ND * L // 2).bitcast(BF16).rearrange("p (d l) -> p d l", d=ND)
        mag = carve(DH * L).rearrange("p (q l) -> p q l", q=DH)
        pos_part = carve(DH * L).rearrange("p (q l) -> p q l", q=DH)
        zhalf = carve(TPB * DIN).rearrange("p (t c) -> p t c", t=TPB)
        zth = carve(TPB * DIN).rearrange("p (t c) -> p t c", t=TPB)
        skip_p = gatedT[:, :, :].rearrange("p h l -> p (h l)").rearrange("p (t c) -> p t c", t=TPB)
        prep_end = top[0]

        ps = ctx.enter_context(nc.psum_tensor("ps", [P, 8, 512], F32))
        b_ps = ps[:, 0:B_RING, :]
        y_ps = ps[:, 4:6, :]
        m_ps = [ps[:, 6, :], ps[:, 7, :]]

        names = """x_ready wts_in a_exp zero_v slots_zeroed var_ready std_ready xn_ready xnT_ps xnT_ready
            kw_ready logit_ps keys_ps chosen_ready rank_ps pos_ready gdiff_ready gexp_ready mix_ready
            mixT_ps mixT_sb base_ps base_sb base_out scattered routed v_chain
            xb_ready xz_ps xpad_ready z_ps z_sb v_ready th_ready u_ready gate_ready xd_ps xd_sb
            part1_ready rest_ready part2_ready parts_ready dt_ps mag_ready a_chain softplus_ready
            small_ready square_ready delta_ready du_ready skip_ps skip_sb gate_out c_out parts_out skip_out delta_out du_out prepared
            early_in0 early_in1 late_in0 late_in1 decay_ready b_ready dbx_done scan_done prod_done summed
            y_free gated_ready m0_ready m0_free m1_ready m1_free gelu_done
            mixed_out sp_step f_chain acc_in acc_ready out_done"""
        s = {n: sem(n) for n in names.split()}
        c_in = [sem(f"c_in{i}") for i in range(C_RING)]
        w1_in_s = [sem(f"w1_in{i}") for i in range(W_RING)]
        w2_in_s = [sem(f"w2_in{i}") for i in range(W_RING)]
        rows_in = [sem(f"rows_in{i}") for i in range(W_RING)]
        y_out = [sem(f"y_out{i}") for i in range(W_RING)]
        y_in = [sem(f"y_in{i}") for i in range(Y_RING)]

        block = ctx.enter_context(nc.Block())

        def bc(ap, shape):
            return ap.to_broadcast(shape)

        def slot_rows(tile):
            return slots_d.rearrange("(t a p) d -> t p a d", a=SH, p=P)[tile]

        @block.sync
        def _(sp):
            sp.dma_start(consts, consts_in).then_inc(s["wts_in"], 16)
            sp.dma_start(x_all, x_in.rearrange("(t p) d -> p t d", p=P)).then_inc(s["x_ready"], 16)
            for dst, src in ((chan[:, :, :], chan_in), (inw, inw_in), (xproj, xproj_in),
                             (dtw[BR:BR + NR], dtw_in), (outw[:, :, :], outw_in), (route[:, 0:3 * E], route_in),
                             (b2[0:E, :], b2_in)):
                sp.dma_start(dst, src).then_inc(s["wts_in"], 16)
            sp.wait_ge(s["zero_v"], 1)
            zeros = delta[:, :, :, :].rearrange("p a q l -> p (a q l)")
            fill = slots_d.rearrange("(k p n) d -> k p (n d)", p=P, n=2 * DH * L // D)
            for k in range(NSLOT // P // (2 * DH * L // D)):
                sp.dma_start(fill[k], zeros).then_inc(s["slots_zeroed"], 16)

            for b in range(BATCH):
                sp.wait_ge(s["base_sb"], b + 1)
                sp.dma_start(base_d[b], base_t).then_inc(s["base_out"], 16)

            for n in PREP_STORES:
                sp.sem_inc(s[n], 16)
            with sp.Fori(0, BATCH) as b:
                def at(t, pattern="e p n -> (e p) n"):
                    return t[bass.ds(b, 1)].rearrange(pattern)
                sp.wait_ge(s["gate_ready"], b + 1)
                sp.sem_inc(s["sp_step"], 1)
                sp.dma_start(at(gate_d), zth.rearrange("p t c -> p (t c)")).then_inc(s["gate_out"], 16)
                sp.wait_ge(s["xd_sb"], b + 1)
                sp.sem_inc(s["sp_step"], 1)
                sp.dma_start(c_d[bass.ds(b, 1)].rearrange("e d n l -> n (e d) l"),
                             xdbl[NS:2 * NS]).then_inc(s["c_out"], 16)
                sp.wait_ge(s["parts_ready"], b + 1)
                sp.sem_inc(s["sp_step"], 1)
                sp.dma_start(at(parts_d), parts_p.rearrange("p d l -> p (d l)")).then_inc(s["parts_out"], 16)
                sp.wait_ge(s["skip_sb"], b + 2)
                sp.sem_inc(s["sp_step"], 1)
                sp.dma_start(at(skip_d), skip_p.rearrange("p t c -> p (t c)")).then_inc(s["skip_out"], 16)
                sp.wait_ge(s["delta_ready"], b + 1)
                sp.sem_inc(s["sp_step"], 1)
                sp.dma_start(at(delta_d), pos_part.rearrange("p q l -> p (q l)")).then_inc(s["delta_out"], 16)
                sp.wait_ge(s["du_ready"], b + 1)
                sp.sem_inc(s["sp_step"], 1)
                sp.dma_start(at(du_d), v.rearrange("p q l -> p (q l)")).then_inc(s["du_out"], 16)
            sp.wait_ge(s["prepared"], 1)

            def one(t, b):
                return t[bass.ds(b, 1)].rearrange("e p n -> (e p) n")

            def read_early(b, par):
                sp.dma_start(delta[:, par, :, :].rearrange("p q l -> p (q l)"), one(delta_d, b)).then_inc(s[f"early_in{par}"], 16)
                sp.dma_start(du[:, par, :, :].rearrange("p q l -> p (q l)"), one(du_d, b)).then_inc(s[f"early_in{par}"], 16)
                sp.dma_start(parts[:, par, :, :].rearrange("p d l -> p (d l)"), one(parts_d, b)).then_inc(s[f"early_in{par}"], 16)

            def read_late(b, par):
                for h in range(NH):
                    for dst, src in ((gate, gate_d), (skip, skip_d)):
                        sp.dma_start(dst[:, par, h, :, :],
                                     src[bass.ds(b, 1)].rearrange("e p (t h c) -> (e p) h t c", t=TPB, h=NH)[:, h])\
                            .then_inc(s[f"late_in{par}"], 16)
                sp.dma_start(base[:, par, :], one(base_d, b)).then_inc(s[f"late_in{par}"], 16)

            def read_c(b, r):
                g, d = r // ND, r % ND
                src = c_d[bass.ds(b, 1), d, 2 * g:2 * g + 2, :].rearrange("e j l -> e (j l)")
                sp.dma_start(c_rows[:, r % C_RING, :, :].rearrange("p j l -> p (j l)"),
                             src.to_broadcast([P, 2 * L])).then_inc(c_in[r % C_RING], 16)

            def expert_of(tile):
                return sp.value_load(tile_expert[0:1, bass.ds(tile, 1)], min_val=0, max_val=E - 1)

            def read_up(tile, slot):
                e = expert_of(tile)
                sp.dma_start(w1[:, slot, :], w1_in[bass.ds(e, 1)].rearrange("e p n -> (e p) n")).then_inc(w1_in_s[slot], 16)
                sp.dma_start(rows[:, slot, :, :],
                             slots_d.rearrange("(t a p) d -> t p a d", a=SH, p=P)[bass.ds(tile, 1)]
                             .rearrange("t p a d -> (t p) a d")).then_inc(rows_in[slot], 16)

            def read_down(tile, slot):
                e = expert_of(tile)
                sp.dma_start(w2[:, slot, :, :].rearrange("p f d -> p (f d)"),
                             w2_in[bass.ds(e, 1)].rearrange("e p n -> (e p) n")).then_inc(w2_in_s[slot], 16)

            def batch(b, par):
                first = isinstance(b, int) and b == 0
                nxt = (b + 1) % BATCH
                todo = []

                def early():
                    wait(sp, s["decay_ready"], DECAYS * b)
                    wait(sp, s["dbx_done"], DECAYS * b)
                    wait(sp, s["b_ready"], DECAYS * b)
                    sp.sem_inc(s["sp_step"], 1)
                    read_early(nxt, 1 - par)
                todo.append((0.5, early))

                def late():
                    if not first:
                        sp.wait_ge(s["m0_free"], uses_before(b, 0) + ORDER["O", 0] + 1)
                        sp.sem_inc(s["sp_step"], 1)
                        sp.dma_start(one(mixed_d, b - 1), mixed[:, :]).then_inc(s["mixed_out"], 16)
                    read_late(nxt, 1 - par)
                todo.append((27.5, late))
                for r in range(CPB):
                    def c(r=r):
                        sp.wait_ge(s["prod_done"], PAIRS * b + 2 * (r + 1))
                        sp.sem_inc(s["sp_step"], 1)
                        rn = r + C_RING
                        read_c(b if rn < CPB else nxt, rn % CPB)
                    todo.append((2 * r + 3, c))
                for j in range(MPB):
                    def up(j=j):
                        sp.wait_ge(s["m0_free"], uses_before(b, 0) + ORDER["U1", j] + 1)
                        sp.sem_inc(s["sp_step"], 1)
                        read_up((b * MPB + (j + W_RING)) % NTILE, j % W_RING)
                    todo.append((T_STEP[j] + 2.5, up))

                    def down(j=j):
                        sp.wait_ge(s["m1_ready"], uses_before(b, 1) + ORDER["D", j] + 1)
                        sp.sem_inc(s["sp_step"], 1)
                        read_down((b * MPB + (j + W_RING)) % NTILE, j % W_RING)
                    todo.append((D_STEP[j] + 1.2, down))

                    def store(j=j):
                        sp.wait_ge(s["m1_free"], uses_before(b, 1) + ORDER["D", j] + 1)
                        sp.sem_inc(s["sp_step"], 1)
                        sp.dma_start(expert_d.rearrange("(t a p) d -> t p a d", a=SH, p=P)[bass.ds(b * MPB + j, 1)]
                                     .rearrange("t p a d -> (t p) a d"),
                                     yrows[:, j % W_RING, :, :]).then_inc(y_out[j % W_RING], 16)
                    todo.append((D_STEP[j] + 1.6, store))
                for _, f in sorted(todo, key=lambda x: x[0]):
                    f()

            read_early(0, 0)
            for r in range(C_RING):
                read_c(0, r)
            for j in range(W_RING):
                read_up(j, j)
                read_down(j, j)
            read_late(0, 0)
            batch(0, 0)
            batch(1, 1)
            with sp.Fori(1, BATCH // 2) as i:
                batch(2 * i, 0)
                batch(2 * i + 1, 1)
            sp.wait_ge(s["m0_free"], LAST0 + FINISH)
            sp.dma_start(mixed_d[BATCH - 1], mixed[:, :]).then_inc(s["mixed_out"], 16)
            sp.wait_ge(s["mixed_out"], 16 * BATCH)
            sp.wait_ge(s["summed"], PAIRS * BATCH)
            sp.dma_start(acc.rearrange("p (b n) -> p b n", b=BATCH), mixed_d.rearrange("b p n -> p b n")).then_inc(s["acc_in"], 16)
            for b in range(BATCH):
                sp.wait_ge(s["acc_ready"], TPB * (b + 1))
                sp.dma_start(out.rearrange("(t p) d -> p t d", p=P)[:, TPB * b:TPB * (b + 1), :],
                             acc[:, TPB * b * D:TPB * (b + 1) * D].rearrange("p (t d) -> p t d", t=TPB))\
                    .then_inc(s["out_done"], 16)
            sp.wait_ge(s["out_done"], 16 * BATCH)
            for par in range(2):
                sp.wait_ge(s[f"early_in{par}"], 16 * 3 * (BATCH // 2 + (1 - par)))
                sp.wait_ge(s[f"late_in{par}"], 16 * 5 * (BATCH // 2 + (1 - par)))
            for i in range(C_RING):
                sp.wait_ge(c_in[i], 16 * (BATCH * CPB // C_RING + 1))
            for i in range(W_RING):
                sp.wait_ge(w1_in_s[i], 16 * (NTILE // W_RING + 1))
                sp.wait_ge(w2_in_s[i], 16 * (NTILE // W_RING + 1))
                sp.wait_ge(rows_in[i], 16 * (NTILE // W_RING + 1))
                sp.wait_ge(y_out[i], 16 * (NTILE // W_RING))

        @block.gpsimd
        def _(pool):
            nc.gpsimd.memset(delta[:, :, :, :], 0.0).then_inc(s["zero_v"], 1)
            pool.wait_ge(s["slots_zeroed"], 16 * ZERO_DMAS)
            pool.wait_ge(s["xn_ready"], NT)
            pool.wait_ge(s["pos_ready"], 1)
            for t in range(NT):
                for k in range(TOPK):
                    pool.indirect_dma_start(slots_d, bass.IndirectOffsetOnAxis(
                        ap=pos[:, t * TOPK + k:t * TOPK + k + 1], axis=0), xn[:, t, :], None).then_inc(s["scattered"], 16)
            pool.wait_ge(s["prepared"], 1)

            def batch(b):
                for q in range(PAIRS):
                    r, h = q // NH, q % NH
                    wait(pool, s["scan_done"], DECAYS * b + 2 * q + 2)
                    if h == 0:
                        pool.wait_ge(c_in[r % C_RING], 16 * (CPB // C_RING * b + r // C_RING + 1))
                    nc.gpsimd.tensor_tensor(state[:, q % H_RING], state[:, q % H_RING], c_rows[:, r % C_RING],
                                            ALU.mult).then_inc(s["prod_done"], 1)

            batch(0)
            batch(1)
            with pool.Fori(1, BATCH // 2) as i:
                batch(2 * i)
                batch(2 * i + 1)
            for i in range(W_RING):
                pool.wait_ge(y_out[i], 16 * (NTILE // W_RING))
            for t in range(NT):
                wait(pool, s["acc_ready"], t - Y_RING + 1)
                for k in range(TOPK):
                    pool.indirect_dma_start(y_tok[:, (t % Y_RING) * TOPK + k, :], None, expert_d, bass.IndirectOffsetOnAxis(
                        ap=pos[:, t * TOPK + k:t * TOPK + k + 1], axis=0)).then_inc(y_in[t % Y_RING], 16)

        @block.scalar
        def _(act):
            act.wait_ge(s["wts_in"], 16 * WTS_DMAS)
            nc.scalar.activation(a_neg[:, :, :], chan[:, :, KC + 3:CH], ACT.Exp).then_inc(s["a_exp"], 1)
            act.wait_ge(s["var_ready"], 1)
            nc.scalar.activation(std, var_eps, ACT.Sqrt).then_inc(s["std_ready"], 1)
            for g in range(BATCH):
                act.wait_ge(s["xnT_ps"], g + 1)
                nc.scalar.copy(xnT[:, g * L:(g + 1) * L], ps[:, 2 + g % 4, :]).then_inc(s["xnT_ready"], 1)
            act.wait_ge(s["gdiff_ready"], 1)
            nc.scalar.activation(gexp, idxf, ACT.Exp).then_inc(s["gexp_ready"], 1)
            for g in range(BATCH):
                act.wait_ge(s["mixT_ps"], g + 1)
                wait(act, s["base_ps"], g)
                nc.scalar.copy(mix_wT[0:E, :], ps[0:E, 2 + g % 2, :]).then_inc(s["mixT_sb"], 1)

            act.wait_ge(s["routed"], 1)
            act.sem_inc(s["mag_ready"], 1)
            act.sem_inc(s["skip_sb"], 1)
            with act.Fori(0, BATCH) as b:
                act.wait_ge(s["xz_ps"], b + 1)
                act.wait_ge(s["v_ready"], b + 1)
                nc.scalar.copy(xpad[:, :, KC - 1:KC - 1 + L], ps[:, 0:2, :]).then_inc(s["xpad_ready"], 1)
                act.wait_ge(s["z_ps"], b + 1)
                act.wait_ge(s["gate_out"], 16 * b + 16)
                nc.scalar.mul(zhalf.rearrange("p t c -> p (t c)"), ps[:, 2:4, :].rearrange("p a n -> p (a n)"), 0.5)
                nc.scalar.activation(zth.rearrange("p t c -> p (t c)"), ps[:, 2:4, :].rearrange("p a n -> p (a n)"),
                                     ACT.Tanh, scale=0.5).then_inc(s["z_sb"], 1)
                act.wait_ge(s["v_ready"], b + 2)
                nc.scalar.activation(th, v, ACT.Tanh).then_inc(s["th_ready"], 1)
                act.wait_ge(s["xd_ps"], b + 1)
                act.wait_ge(s["c_out"], 16 * b + 16)
                nc.scalar.copy(xdbl[0:BR + NR], ps[0:BR + NR, 4:6, :]).then_inc(s["xd_sb"], 1)
                nc.scalar.copy(part1[0:BR], ps[0:BR, 4:6, :]).then_inc(s["part1_ready"], 1)
                act.wait_ge(s["rest_ready"], b + 1)
                nc.scalar.copy(part2[0:BR], rest[0:BR]).then_inc(s["part2_ready"], 1)
                act.wait_ge(s["dt_ps"], b + 1)
                act.wait_ge(s["delta_out"], 16 * b + 16)
                for q in range(DH):
                    bank = DT_BANKS[q]
                    nc.scalar.activation(mag[:, q, :], ps[:, bank, :], ACT.Abs, bias=chan[:, q, KC + 1:KC + 2])
                    last = nc.scalar.activation(pos_part[:, q, :], ps[:, bank, :], ACT.Relu, bias=chan[:, q, KC + 1:KC + 2])
                last.then_inc(s["mag_ready"], 1)
                nc.scalar.add_instruction(mybir.InstLoadActFuncSet(name=nc.get_next_instruction_name(), act_func_set_id=EXP_LN_SET))
                act.wait_ge(s["mag_ready"], b + 2)
                nc.scalar.activation(mag, mag, ACT.Exp, scale=-1.0).then_inc(s["a_chain"], 1)
                act.wait_ge(s["a_chain"], b + 1)
                nc.scalar.activation(th, mag, ACT.Ln, bias=1.0).then_inc(s["softplus_ready"], 1)
                act.wait_ge(s["small_ready"], b + 1)
                nc.scalar.activation(v, mag, ACT.Square, scale=SQ_SCALE, bias=fit_bias[:, 0:1]).then_inc(s["square_ready"], 1)
                act.wait_ge(s["skip_ps"], b + 2)
                act.wait_ge(s["skip_out"], 16 * b + 16)
                nc.scalar.copy(skip_p.rearrange("p t c -> p (t c)"), ps[:, 2:4, :].rearrange("p a n -> p (a n)")).then_inc(s["skip_sb"], 1)
            act.wait_ge(s["prepared"], 1)

            def empty(b, q):
                for what, j, m in EVENTS[q]:
                    bank = m_ps[m]
                    if what in "GO" and isinstance(b, int) and b == 0 or what == "O":
                        continue
                    bank_written(act, s, b, what, j, m)
                    if what == "T":
                        nc.scalar.copy(rowsT[:, :], bank[:, 0:S]).then_inc(s["m0_free"], 1)
                    elif what in ("U0", "U1"):
                        for f in range(2):
                            c = 2 * (what == "U1") + f
                            last = nc.scalar.activation(hidden[:, j, c, :], bank[:, f * S:(f + 1) * S], ACT.Identity,
                                                        bias=w1[:, j % W_RING, FF + c:FF + c + 1])
                        last.then_inc(s[f"m{m}_free"], 1)
                    elif what == "D":
                        wait(act, y_out[j % W_RING], 16 * (MPB // W_RING * b + j // W_RING))
                        nc.scalar.copy(yrows[:, j % W_RING, :, :].rearrange("p a d -> p (a d)"), bank[:, 0:S]).then_inc(s["m1_free"], 1)
                    elif what == "G":
                        nc.scalar.copy(gatedT[:, j, :], bank).then_inc(s["m0_free"], 1)

            def batch(b, par, i):
                first = isinstance(b, int) and b == 0
                act.wait_ge(s[f"early_in{par}"], 48 * i + 48)
                for q in range(PAIRS):
                    g, dh = q // DH, q % DH
                    wait(act, s["scan_done"], DECAYS * b + 2 * (q - DA_RING) + 2)
                    lo = 1 if dh < NH else 0
                    for j in range(2):
                        nc.scalar.activation(decay[:, q % DA_RING, j, lo:lo + L - 1], delta[:, par, dh, lo:lo + L - 1], ACT.Exp,
                                             scale=a_neg[:, dh, 2 * g + j:2 * g + j + 1]).then_inc(s["decay_ready"], 1)
                    if q >= EVAC_LAG:
                        empty(b, q - EVAC_LAG)
                    elif not first:
                        empty(b - 1, PAIRS + q - EVAC_LAG)
                    if q in GELU_STEP:
                        n = GELU_STEP.index(q)
                        act.wait_ge(s["m0_free"], uses_before(b, 0) + ORDER["U1", GROUP * (n + 1) - 1] + 1)
                        act.wait_ge(s["m1_free"], uses_before(b, 1) + ORDER["U0", GROUP * (n + 1) - 1] + 1)
                        for j in range(GROUP * n, GROUP * (n + 1)):
                            h = hidden[:, j, :, :].rearrange("p f s -> p (f s)")
                            nc.scalar.activation(h, h, ACT.Gelu).then_inc(s["gelu_done"], 1)

            batch(0, 0, 0)
            batch(1, 1, 0)
            with act.Fori(1, BATCH // 2) as i:
                batch(2 * i, 0, i)
                batch(2 * i + 1, 1, i)
            for q in range(PAIRS - EVAC_LAG, PAIRS):
                empty(BATCH - 1, q)
            for j in range(NH):
                act.wait_ge(s["m0_ready"], LAST0 + j + 1)
                nc.scalar.copy(gatedT[:, j, :], m_ps[0]).then_inc(s["m0_free"], 1)

        @block.tensor
        def _(pe):
            for g in range(BATCH):
                pe.wait_ge(s["xn_ready"], TPB * (g + 1))
                wait(pe, s["xnT_ready"], g - 3)
                for t in range(TPB):
                    last = nc.tensor.transpose(ps[:, 2 + g % 4, t * P:(t + 1) * P], xn[:, g * TPB + t, :], ident[:, :])
                last.then_inc(s["xnT_ps"], 1)
            pe.wait_ge(s["kw_ready"], 1)
            nc.tensor.matmul(ps[:, 6, 0:E], ones_f, keys_sq, start=True, stop=True).then_inc(s["keys_ps"], 1)
            for g in range(BATCH):
                pe.wait_ge(s["xnT_ready"], g + 1)
                for t in range(g * TPB, (g + 1) * TPB):
                    last = nc.tensor.matmul(ps[:, 7, t * E:(t + 1) * E], xnT[:, t * P:(t + 1) * P], route_w,
                                            start=True, stop=True)
            last.then_inc(s["logit_ps"], 1)
            pe.wait_ge(s["chosen_ready"], 1)
            nc.tensor.matmul(ps[:, 0, :], tri, chosen, start=True, stop=True)
            nc.tensor.matmul(ps[:, 1, :], ones_b, chosen, start=True, stop=True).then_inc(s["rank_ps"], 1)
            pe.wait_ge(s["mix_ready"], 1)
            for g in range(BATCH):
                wait(pe, s["mixT_sb"], g - 1)
                for t in range(TPB):
                    tt = g * TPB + t
                    last = nc.tensor.transpose(ps[0:E, 2 + g % 2, t * P:(t + 1) * P], mix_w[:, tt * E:(tt + 1) * E], ident[:, :])
                last.then_inc(s["mixT_ps"], 1)
                pe.wait_ge(s["mixT_sb"], g + 1)
                wait(pe, s["base_sb"], g - 1)
                for t in range(TPB):
                    last = nc.tensor.matmul(ps[:, 4 + g % 2, t * P:(t + 1) * P], mix_wT[0:E, t * P:(t + 1) * P], b2[0:E, :],
                                            start=True, stop=True)
                last.then_inc(s["base_ps"], 1)

            pe.wait_ge(s["routed"], 1)
            pe.sem_inc(s["skip_ps"], 1)
            with pe.Fori(0, BATCH) as b:
                pe.wait_ge(s["xb_ready"], b + 1)
                pe.wait_ge(s["mag_ready"], b + 1)
                for h in range(NH):
                    last = nc.tensor.matmul(ps[:, h, :], inw[:, h * P:(h + 1) * P], xb, start=True, stop=True)
                last.then_inc(s["xz_ps"], 1)
                pe.wait_ge(s["skip_sb"], b + 1)
                for t in range(TPB):
                    last = nc.tensor.matmul(ps[:, 2 + t // 2, t % 2 * DIN:(t % 2 + 1) * DIN], xb[:, t * P:(t + 1) * P],
                                            inw[:, DIN:2 * DIN], start=True, stop=True)
                last.then_inc(s["z_ps"], 1)
                pe.wait_ge(s["u_ready"], b + 1)
                for d in range(ND):
                    for h in range(NH):
                        last = nc.tensor.matmul(ps[0:BR + NR, 4 + d, :], xproj[:, d, h, :], u[:, d * NH + h, :],
                                                start=h == 0, stop=h == NH - 1)
                last.then_inc(s["xd_ps"], 1)
                for t in range(TPB):
                    for h in range(NH):
                        for d in range(ND):
                            o = t % 2 * DIN + h * P
                            last = nc.tensor.matmul(ps[:, 2 + t // 2, o:o + P], u[:, d * NH + h, t * P:(t + 1) * P],
                                                    diag[:, d * NH + h, :], start=d == 0, stop=d == ND - 1)
                last.then_inc(s["skip_ps"], 1)
                pe.wait_ge(s["xd_sb"], b + 1)
                for d in range(ND):
                    for h in range(NH):
                        last = nc.tensor.matmul(ps[:, DT_BANKS[d * NH + h], :], dtw[BR:BR + NR, d, h * P:(h + 1) * P],
                                                xdbl[BR:BR + NR, d, :], start=True, stop=True)
                last.then_inc(s["dt_ps"], 1)
            pe.wait_ge(s["prepared"], 1)

            def sum_states(b, q):
                g, d, h = q // DH, q // NH % ND, q % NH
                pe.wait_ge(s["prod_done"], PAIRS * b + q + 1)
                if q < NH:
                    wait(pe, s["y_free"], NH * (b - 1) + h + 1)
                for j in range(2):
                    for t in range(TPB):
                        last = nc.tensor.matmul(y_ps[:, h, t * P:(t + 1) * P], state[:, q % H_RING, j, t * P:(t + 1) * P], ident[:, :],
                                                is_transpose=True, start=q < NH and j == 0 and t == 0,
                                                stop=q >= PAIRS - NH and j == 1, skip_group_check=True)
                last.then_inc(s["summed"], 1)

            def extra(b, q, par):
                for what, j, m in EVENTS[q]:
                    if what in "GO" and isinstance(b, int) and b == 0:
                        continue
                    bank, slot, turn = m_ps[m], j % W_RING, j // W_RING
                    bank_empty(pe, s, b, what, j, m)
                    if what == "T":
                        pe.wait_ge(rows_in[slot], 16 * (MPB // W_RING * b + turn + 1))
                        for a in range(SH):
                            last = nc.tensor.transpose(bank[:, a * P:(a + 1) * P], rows[:, slot, a, :], ident[:, :])
                    elif what in ("U0", "U1"):
                        if what == "U0":
                            bank_empty(pe, s, b, "U1", j, 0)
                            pe.wait_ge(w1_in_s[slot], 16 * (MPB // W_RING * b + turn + 1))
                        for f in range(2):
                            c = 2 * (what == "U1") + f
                            last = nc.tensor.matmul(bank[:, f * S:(f + 1) * S], w1[:, slot, c * P:(c + 1) * P], rowsT[:, :],
                                                    start=True, stop=True)
                    elif what == "D":
                        pe.wait_ge(w2_in_s[slot], 16 * (MPB // W_RING * b + turn + 1))
                        pe.wait_ge(s["gelu_done"], MPB * b + j + 1)
                        for a in range(SH):
                            for c in range(FC):
                                last = nc.tensor.matmul(bank[:, a * P:(a + 1) * P], hidden[:, j, c, a * P:(a + 1) * P], w2[:, slot, c, :],
                                                        start=c == 0, stop=c == FC - 1)
                    elif what == "G":
                        transpose_gated(bank, j, b)
                        continue
                    else:
                        last = project(bank)
                    last.then_inc(s[f"m{m}_ready"], 1)

            def transpose_gated(bank, h, b):
                pe.wait_ge(s["gated_ready"], NH * (b - 1) + h + 1)
                for t in range(TPB):
                    last = nc.tensor.transpose(bank[:, t * P:(t + 1) * P], gated[:, h, t, :], ident[:, :])
                last.then_inc(s["m0_ready"], 1)

            def project(bank):
                for t in range(TPB):
                    for h in range(NH):
                        last = nc.tensor.matmul(bank[:, t * P:(t + 1) * P], gatedT[:, h, t * P:(t + 1) * P], outw[:, h, :],
                                                start=h == 0, stop=h == NH - 1)
                return last

            def batch(b, par, i):
                first = isinstance(b, int) and b == 0
                pe.wait_ge(s[f"early_in{par}"], 48 * i + 48)
                for q in range(PAIRS):
                    g, d = q // DH, q // NH % ND
                    for j in range(2):
                        tau = 2 * q + j
                        wait(pe, s["scan_done"], DECAYS * b + tau - B_RING + 1)
                        nc.tensor.matmul(b_ps[:, tau % B_RING, :], sel[:, 2 * g + j, :], parts[:, par, d, :],
                                         start=True, stop=True).then_inc(s["b_ready"], 1)
                    extra(b, q, par)
                    if q >= SUM_LAG:
                        sum_states(b, q - SUM_LAG)
                    elif not first:
                        sum_states(b - 1, PAIRS + q - SUM_LAG)

            batch(0, 0, 0)
            batch(1, 1, 0)
            with pe.Fori(1, BATCH // 2) as i:
                batch(2 * i, 0, i)
                batch(2 * i + 1, 1, i)
            for q in range(PAIRS - SUM_LAG, PAIRS):
                sum_states(BATCH - 1, q)
            for h in range(NH):
                pe.wait_ge(s["m0_free"], LAST0 + h)
                transpose_gated(m_ps[0], h, BATCH)
            pe.wait_ge(s["m0_free"], LAST0 + NH)
            project(m_ps[0]).then_inc(s["m0_ready"], 1)

        @block.vector
        def _(dve):
            done = [0]

            def link(ins):
                done[0] += 1
                ins.then_inc(s["v_chain"], 1)
                dve.wait_ge(s["v_chain"], done[0])

            dve.wait_ge(s["x_ready"], 16)
            for t in range(NT):
                last = nc.vector.bn_stats(stats[:, t, :], x_all[:, t, :])
            link(last)
            for t in range(NT):
                last = nc.vector.bn_aggr(mv[:, t, :], stats[:, t, :])
            link(last)
            nc.vector.tensor_scalar(var_eps, mv[:, :, 1], EPS, None, ALU.add).then_inc(s["var_ready"], 1)
            dve.wait_ge(s["wts_in"], 16 * WTS_DMAS)
            keysT, rwT, rb = (route[:, k * E:(k + 1) * E] for k in range(3))
            nc.vector.tensor_copy(ident[:, :], consts[:, C_ID:C_ID + P])
            nc.vector.memset(ones_f, 1.0)
            nc.vector.memset(ones_b, 1.0)
            nc.vector.memset(fit_bias[:, :], SQ_BIAS)
            nc.vector.tensor_copy(tri, consts[:, C_TRI:C_TRI + P])
            nc.vector.scalar_tensor_tensor(route_w, keysT, 2.0, rwT, ALU.mult, ALU.add)
            nc.vector.tensor_tensor(keys_sq, keysT, keysT, ALU.mult).then_inc(s["kw_ready"], 1)
            dve.wait_ge(s["std_ready"], 1)
            link(nc.vector.reciprocal(rstd, std))
            for t in range(NT):
                nc.vector.tensor_scalar(xn[:, t, :], x_all[:, t, :], mv[:, t, 0:1], rstd[:, t:t + 1],
                                        ALU.subtract, ALU.mult).then_inc(s["xn_ready"], 1)
            nc.vector.tensor_copy(sel[:, :, :].rearrange("p n m -> p (n m)"), consts[:, C_SEL:C_END])
            nc.vector.tensor_scalar(half_taps[:, :, :], chan[:, :, 0:KC + 1], 0.5, None, ALU.mult)
            dve.wait_ge(s["a_exp"], 1)
            nc.vector.tensor_scalar(a_neg[:, :, :], a_neg[:, :, :], -1.0, None, ALU.mult)
            for q in range(DH):
                nc.vector.tensor_scalar(diag[:, q, :], consts[:, C_ID:C_ID + P], chan[:, q, KC + 2:KC + 3], None, ALU.mult)
            dve.wait_ge(s["keys_ps"], 1)
            link(nc.vector.tensor_tensor(route_b, rb, ps[:, 6, 0:E], ALU.subtract))
            dve.wait_ge(s["logit_ps"], 1)
            te = lambda ap: ap.rearrange("p (t e) -> p t e", e=E)
            link(nc.vector.tensor_tensor(te(logits), te(ps[:, 7, :]), bc(route_b.unsqueeze(1), [P, NT, E]), ALU.add))
            for t in range(NT):
                last = nc.vector.max(top8[:, t, :], te(logits)[:, t, :])
            link(last)
            for t in range(NT):
                last = nc.vector.max_index(idx8[:, t, :], top8[:, t, :], te(logits)[:, t, :])
            link(last)
            tk = lambda ap: ap.rearrange("p (t k) -> p t k", k=TOPK)
            link(nc.vector.tensor_copy(tk(idxf), idx8[:, :, 0:TOPK]))
            iota = consts[:, C_IOTA:C_IOTA + E]
            tke = lambda ap: ap.rearrange("p (n e) -> p n e", e=E)
            link(nc.vector.tensor_tensor(tke(onehot), bc(idxf.unsqueeze(2), [P, NT * TOPK, E]),
                                         bc(iota.unsqueeze(1), [P, NT * TOPK, E]), ALU.is_equal))
            oh4 = onehot.rearrange("p (t k e) -> p t k e", k=TOPK, e=E)
            with nc.allow_low_precision(reason="zeros and ones"):
                nc.vector.tensor_reduce(te(chosen), oh4.rearrange("p t k e -> p t e k"), AXX, ALU.add).then_inc(s["chosen_ready"], 1)
            dve.wait_ge(s["rank_ps"], 1)
            link(nc.vector.tensor_copy(totals, ps[:, 1, :].rearrange("p (t e) -> p e t", e=E)))
            flat = lambda ap: ap.rearrange("p e t -> p (e t)")
            link(nc.vector.tensor_tensor_scan(flat(upto), consts[:, C_MASK:C_MASK + NT * E], flat(totals), 0.0, ALU.mult, ALU.add))
            cmp1 = compare[:, 0:E * E].rearrange("p (e j) -> p e j", j=E)
            link(nc.vector.tensor_tensor(cmp1, bc(upto[:, :, NT - 1:NT], [P, E, E]),
                                         bc(consts[:, C_THR:C_THR + E].unsqueeze(1), [P, E, E]), ALU.is_gt))
            link(nc.vector.tensor_reduce(n_tiles, cmp1, AXX, ALU.add))
            link(nc.vector.tensor_tensor_scan(end_tile, ones_f[:, 0:E], n_tiles, 0.0, ALU.mult, ALU.add))
            link(nc.vector.tensor_tensor(slot0, end_tile, n_tiles, ALU.subtract))
            link(nc.vector.tensor_scalar(slot0, slot0, float(S), None, ALU.mult))
            link(nc.vector.tensor_tensor(upto, upto, totals, ALU.subtract))
            link(nc.vector.tensor_tensor(upto, upto, bc(slot0.unsqueeze(2), [P, E, NT]), ALU.add))
            link(nc.vector.tensor_tensor(te(place), te(ps[:, 0, :]), upto.rearrange("p e t -> p t e"), ALU.add))
            pr4 = product.rearrange("p (t k e) -> p t k e", k=TOPK, e=E)
            link(nc.vector.tensor_tensor(pr4, oh4, bc(te(place).unsqueeze(2), [P, NT, TOPK, E]), ALU.mult))
            link(nc.vector.tensor_reduce(posf, tke(product), AXX, ALU.add))
            nc.vector.tensor_copy(pos[:, :], posf).then_inc(s["pos_ready"], 1)
            nc.vector.tensor_tensor(tk(idxf), top8[:, :, 0:TOPK], bc(top8[:, :, 0:1], [P, NT, TOPK]),
                                    ALU.subtract).then_inc(s["gdiff_ready"], 1)
            cmp2 = compare.rearrange("p (t e) -> p t e", e=E)
            link(nc.vector.tensor_tensor(cmp2, bc(end_tile.unsqueeze(1), [P, NTILE, E]),
                                         bc(consts[:, C_TILE:C_TILE + NTILE].unsqueeze(2), [P, NTILE, E]), ALU.is_le))
            link(nc.vector.tensor_reduce(texp, cmp2, AXX, ALU.add))
            link(nc.vector.tensor_scalar(tile_expert[:, :], texp, float(E - 1), None, ALU.min))
            dve.wait_ge(s["gexp_ready"], 1)
            link(nc.vector.tensor_reduce(gsum, tk(gexp), AXX, ALU.add))
            link(nc.vector.reciprocal(grec, gsum))
            link(nc.vector.tensor_tensor(gates[:, :, :], tk(gexp), bc(grec.unsqueeze(2), [P, NT, TOPK]), ALU.mult))
            link(nc.vector.tensor_tensor(tke(product), tke(onehot),
                                         bc(gates[:, :, :].rearrange("p t k -> p (t k)").unsqueeze(2), [P, NT * TOPK, E]), ALU.mult))
            nc.vector.tensor_reduce(te(mix_w), pr4.rearrange("p t k e -> p t e k"), AXX, ALU.add).then_inc(s["mix_ready"], 1)
            for g in range(BATCH):
                dve.wait_ge(s["base_ps"], g + 1)
                wait(dve, s["base_out"], 16 * g)
                nc.vector.tensor_tensor(base_t, ps[:, 4 + g % 2, :], x_all[:, g * TPB:(g + 1) * TPB, :].rearrange("p t d -> p (t d)"),
                                        ALU.add).then_inc(s["base_sb"], 1)
            dve.wait_ge(s["base_out"], 16 * BATCH)
            nc.vector.memset(xpad[:, :, :], 0.0).then_inc(s["v_chain"], 1)
            done[0] += 1
            link(nc.vector.memset(parts_p[BR:P], 0.0))
            dve.sem_inc(s["routed"], 1)
            dve.sem_inc(s["v_ready"], 1)

            start = done[0]
            per = [0]
            with dve.Fori(0, BATCH) as b:
                def linked(ins):
                    per[0] += 1
                    ins.then_inc(s["v_chain"], 1)

                def since(n):
                    dve.wait_ge(s["v_chain"], start + PREP_LINKS * b + n)

                nc.vector.tensor_copy(xb, xnT[:, bass.ds(b * L, L)]).then_inc(s["xb_ready"], 1)
                dve.wait_ge(s["xpad_ready"], b + 1)
                dve.wait_ge(s["du_out"], 16 * b + 16)
                for k in range(KC):
                    for q in range(DH):
                        d, h = q // NH, q % NH
                        o = k if d == 0 else 2 * (KC - 1) - k
                        src = xpad[:, h, o:o + L]
                        if k == 0:
                            linked(nc.vector.tensor_scalar(v[:, q, :], src, half_taps[:, q, 0:1], half_taps[:, q, KC:KC + 1],
                                                           ALU.mult, ALU.add))
                        else:
                            since(per[0] - DH + 1)
                            ins = nc.vector.scalar_tensor_tensor(v[:, q, :], src, half_taps[:, q, k:k + 1], v[:, q, :],
                                                                 ALU.mult, ALU.add)
                            if k < KC - 1 or q < DH - 1:
                                linked(ins)
                            else:
                                ins.then_inc(s["v_ready"], 1)
                dve.wait_ge(s["z_sb"], b + 1)
                nc.vector.scalar_tensor_tensor(zth, zth, 1.0, zhalf, ALU.add, ALU.mult).then_inc(s["gate_ready"], 1)
                dve.wait_ge(s["th_ready"], b + 1)
                dve.wait_ge(s["v_ready"], b + 2)
                dve.wait_ge(s["skip_ps"], b + 1)
                nc.vector.scalar_tensor_tensor(u, th, 1.0, v, ALU.add, ALU.mult).then_inc(s["u_ready"], 1)
                dve.wait_ge(s["part1_ready"], b + 1)
                nc.vector.scalar_tensor_tensor(rest[0:BR], part1[0:BR], consts[0:BR, C_PART:C_PART + 1], xdbl[0:BR],
                                               ALU.mult, ALU.add).then_inc(s["rest_ready"], 1)
                dve.wait_ge(s["part2_ready"], b + 1)
                dve.wait_ge(s["rest_ready"], b + 1)
                dve.wait_ge(s["parts_out"], 16 * b + 16)
                nc.vector.scalar_tensor_tensor(parts_p[0:BR], part2[0:BR], consts[0:BR, C_PART + 1:C_PART + 2], rest[0:BR],
                                               ALU.mult, ALU.add).then_inc(s["parts_ready"], 1)
                dve.wait_ge(s["softplus_ready"], b + 1)
                nc.vector.tensor_scalar(mag, mag, SMALL, None, ALU.min).then_inc(s["small_ready"], 1)
                linked(nc.vector.tensor_scalar(th, th, -LOG_SMALL, 0.0, ALU.add, ALU.max))
                since(per[0])
                linked(nc.vector.tensor_tensor(pos_part, pos_part, th, ALU.add))
                dve.wait_ge(s["square_ready"], b + 1)
                linked(nc.vector.scalar_tensor_tensor(v, v, SQ_REST, mag, ALU.add, ALU.mult))
                since(per[0])
                nc.vector.tensor_tensor(pos_part, pos_part, v, ALU.add).then_inc(s["delta_ready"], 1)
                dve.wait_ge(s["delta_ready"], b + 1)
                dve.wait_ge(s["u_ready"], b + 1)
                nc.vector.tensor_tensor(v, pos_part, u, ALU.mult).then_inc(s["du_ready"], 1)
            assert per[0] == PREP_LINKS, per[0]

            for n in PREP_STORES:
                dve.wait_ge(s[n], 16 * (BATCH + 1))
            dve.wait_ge(s["scattered"], 16 * NT * TOPK)
            dve.wait_ge(s["skip_sb"], BATCH + 1)
            for r in range(DA_RING):
                at = 0 if r % DH < NH else L - 1
                last = nc.vector.memset(decay[:, r, :, at:at + 1], 0.0)
            last.then_inc(s["prepared"], 1)
            dve.wait_ge(s["prepared"], 1)

            def gate_batch(b, par, i):
                dve.wait_ge(s[f"late_in{par}"], 80 * i + 80)
                for h in range(NH):
                    dve.wait_ge(s["summed"], PAIRS * b + PAIRS - NH + h + 1)
                    nc.vector.tensor_tensor(gated[:, h], y_ps[:, h, :].rearrange("p (t c) -> p t c", t=TPB), skip[:, par, h],
                                            ALU.add).then_inc(s["y_free"], 1)
                for h in range(NH):
                    dve.wait_ge(s["y_free"], NH * b + h + 1)
                    nc.vector.tensor_tensor(gated[:, h], gated[:, h], gate[:, par, h], ALU.mult).then_inc(s["gated_ready"], 1)

            def mix_batch(b, par):
                wait(dve, s["mixed_out"], 16 * b)
                nc.vector.tensor_tensor(mixed[:, :], m_ps[0], base[:, par, :], ALU.add).then_inc(s["m0_free"], 1)

            def batch(b, par, i):
                first = isinstance(b, int) and b == 0
                dve.wait_ge(s[f"early_in{par}"], 48 * i + 48)

                def dbx(tau):
                    dve.wait_ge(s["b_ready"], DECAYS * b + tau + 1)
                    bank = b_ps[:, tau % B_RING, :]
                    nc.vector.tensor_tensor(bank, du[:, par, tau // 2 % DH, :], bank, ALU.mult).then_inc(s["dbx_done"], 1)

                dbx(0)
                for q in range(PAIRS):
                    if q == GATE_STEP and not first:
                        gate_batch(b - 1, 1 - par, i if par else i - 1)
                    if q == MIX_STEP and not first:
                        bank_written(dve, s, b, "O", 0, 0)
                        mix_batch(b - 1, 1 - par)
                    for j in range(2):
                        tau = 2 * q + j
                        if tau + 1 < DECAYS:
                            dbx(tau + 1)
                        if j == 0:
                            wait(dve, s["summed"], PAIRS * b + q - H_RING + 1)
                        dve.wait_ge(s["decay_ready"], DECAYS * b + tau + 1)
                        dve.wait_ge(s["dbx_done"], DECAYS * b + tau + 1)
                        way = slice(None) if q % DH < NH else slice(None, None, -1)
                        nc.vector.tensor_tensor_scan(state[:, q % H_RING, j, way], decay[:, q % DA_RING, j, way],
                                                     b_ps[:, tau % B_RING, way], 0.0, ALU.mult, ALU.add).then_inc(s["scan_done"], 1)

            batch(0, 0, 0)
            batch(1, 1, 0)
            with dve.Fori(1, BATCH // 2) as i:
                batch(2 * i, 0, i)
                batch(2 * i + 1, 1, i)
            gate_batch(BATCH - 1, 1, BATCH // 2 - 1)
            dve.wait_ge(s["m0_ready"], LAST0 + FINISH)
            mix_batch(BATCH - 1, 1)
            dve.wait_ge(s["acc_in"], 16)
            for t in range(NT):
                dve.wait_ge(y_in[t % Y_RING], 16 * TOPK * (t // Y_RING + 1))
                for k in range(TOPK):
                    ins = nc.vector.scalar_tensor_tensor(acc[:, t * D:(t + 1) * D], y_tok[:, (t % Y_RING) * TOPK + k, :],
                                                         gates[:, t, k:k + 1], acc[:, t * D:(t + 1) * D], ALU.mult, ALU.add)
                    if k < TOPK - 1:
                        ins.then_inc(s["f_chain"], 1)
                        dve.wait_ge(s["f_chain"], (TOPK - 1) * t + k + 1)
                    else:
                        ins.then_inc(s["acc_ready"], 1)


def kernel(**inputs):
    import numpy as np
    import concourse.bacc as bacc
    from concourse.bass_utils import run_bass_kernel_spmd

    a = {k[3:]: np.asarray(v) for k, v in inputs.items()}
    f = lambda n: a["attn_" + n]

    def by_channel(m):
        return np.stack([w.reshape(NH, P, -1) for w in m]).transpose(2, 0, 1, 3).reshape(P, DH, -1)

    consts = np.zeros((P, C_END), np.float32)
    p = np.arange(P)
    consts[:, C_ID:C_ID + P] = np.eye(P)
    consts[:, C_TRI:C_TRI + P] = p[:, None] < p[None, :]
    consts[:, C_IOTA:C_IOTA + E] = np.arange(E)
    consts[:, C_THR:C_THR + E] = S * np.arange(E)
    consts[:, C_TILE:C_TILE + NTILE] = np.arange(NTILE)
    consts[:, C_MASK:C_MASK + NT * E] = np.tile(np.arange(NT) > 0, E)
    consts[:, C_PART] = -1.0 * (p >= BR // 3)
    consts[:, C_PART + 1] = -1.0 * (p >= 2 * BR // 3)
    sel = (p[:, None] % (2 * NS) == np.arange(NS)[None, :]) & (p[:, None] < BR)
    consts[:, C_SEL:C_END] = np.repeat(sel, P, axis=1)

    chan = np.concatenate([by_channel([f("conv_w")[:, 0], f("convb_w")[:, 0]]),
                           by_channel([f("conv_bias"), f("convb_bias")]),
                           by_channel([f("dt_proj_bias"), f("dt_proj_b_bias")]),
                           by_channel([f("D_skip"), f("D_b_skip")]),
                           by_channel([f("A_log"), f("A_b_log")])], axis=2)
    xproj = []
    for w in (f("x_proj_w"), f("x_proj_b_w")):
        rows = np.concatenate([w[NR:]] * 3 + [w[:NR]])
        xproj.append(rows.T.reshape(NH, P, BR + NR).transpose(1, 0, 2))
    w1 = a["ffn_w1"].transpose(0, 2, 1)
    b1 = a["ffn_b1"].reshape(E, FC, P).transpose(0, 2, 1)
    arrays = {
        "x": f("hidden_states").reshape(TOK, D),
        "consts": consts,
        "chan": chan,
        "in_w": f("in_proj_w").T,
        "xproj": np.stack(xproj, axis=1),
        "dt_w": np.stack([f("dt_proj_w").T, f("dt_proj_b_w").T], axis=1),
        "out_w": f("out_proj_w").T.reshape(NH, P, D).transpose(1, 0, 2),
        "route": np.concatenate([a["ffn_keys"].T, a["ffn_rw"].T, np.broadcast_to(a["ffn_rb"], (P, E))], axis=1),
        "b2": a["ffn_b2"],
        "w1": np.concatenate([w1, b1], axis=2),
        "w2": a["ffn_w2"].transpose(0, 2, 1).reshape(E, FC, P, D).transpose(0, 2, 1, 3).reshape(E, P, FC * D),
    }
    arrays = {k: np.ascontiguousarray(v) for k, v in arrays.items()}
    nc = bacc.Bacc("TRN2", target_bir_lowering=False, num_devices=1)
    aps = [nc.dram_tensor(k + "_dram", v.shape, mybir.dt.from_np(v.dtype), kind="ExternalInput").ap()
           for k, v in arrays.items()]
    out = nc.dram_tensor("out_dram", (TOK, D), F32, kind="ExternalOutput").ap()
    build_kernel(nc, *aps, out)
    r = run_bass_kernel_spmd(nc, [{k + "_dram": v for k, v in arrays.items()}], core_ids=[0])
    return r.results[0]["out_dram"].reshape(BATCH, L, D)
```

```python
import numpy as np
import concourse.bass as bass
from concourse import mybir
from contextlib import ExitStack

F32 = mybir.dt.float32
BF16 = mybir.dt.bfloat16
I32 = mybir.dt.int32
U32 = mybir.dt.uint32
ALU = mybir.AluOpType
ACT = mybir.ActivationFunctionType
AXX = mybir.AxisListType.X

P = 128
D = 128
BATCH, L = 8, 512
TOK = BATCH * L
NT = TOK // P
TPB = L // P
DIN = 256
NH = DIN // P
ND = 2
DH = ND * NH
NS = 16
NR = 8
KC = 4
E, TOPK = 16, 4
FF = 512
FC = FF // P
S = 256
SH = S // P
NTILE = TOK * TOPK // S + E
NSLOT = NTILE * S
MPB = NTILE // BATCH
EPS = 1e-5
CH = KC + 3 + NS
BR = 96
W1W = FF + FC

C_ID, C_TRI, C_IOTA, C_THR, C_TILE = 0, 128, 256, 272, 288
C_MASK = C_TILE + NTILE
C_PART = C_MASK + NT * E
C_SEL = C_PART + 2
C_END = C_SEL + NS * P

PAIRS = NS // 2 * DH
DA_RING = 8
H_RING = 8
B_RING = 4
C_RING = 4
CPB = NS // 2 * ND
W_RING = 2
DECAYS = 2 * PAIRS

SUM_LAG = 4
SUM_STEP = [k + SUM_LAG for k in range(PAIRS)]
SUMS = [[k for k in range(PAIRS) if SUM_STEP[k] == q] for q in range(PAIRS)]
SUMS_AFTER = [[k for k in range(PAIRS) if SUM_STEP[k] == PAIRS + q] for q in range(PAIRS)]

GROUP = MPB // 2
T_STEP = [0, 3, 6, 9, 12, 17, 20, 23, 26, 29]
EVENTS = [[] for _ in range(PAIRS)]
for _j, _q in enumerate(T_STEP):
    EVENTS[_q].append(("T", _j, 0, False))
    EVENTS[_q + 1].append(("D", (_j + GROUP) % MPB, 1, _j < GROUP))
    EVENTS[_q + 2] += [("U0", _j, 1, False), ("U1", _j, 0, False)]
EVENTS[15] += [("G", 0, 0, True), ("G", 1, 1, True)]
EVENTS[16].append(("O", 0, 1, True))
GATE_STEP, MIX_STEP = 3, 16

EMPTY_LAG = 6
HALF = PAIRS // 2
GELU_STEP = [HALF - 1 + EMPTY_LAG, 2 * HALF - 1 + EMPTY_LAG - PAIRS]
BURST_STEPS = [[HALF, HALF + 1], [0, 1]]
EMPTY_STEP = [q + (EMPTY_LAG - 1 - q % HALF if q % HALF < 2 else EMPTY_LAG - 2 if q % HALF < 6 else
                   EMPTY_LAG - 1 if q % HALF < 9 else EMPTY_LAG) for q in range(PAIRS)]
EMPTY = [[p for p in range(PAIRS) if EMPTY_STEP[p] == q and p % HALF > 1] for q in range(PAIRS)]
EMPTY_AFTER = [[p for p in range(PAIRS) if EMPTY_STEP[p] == PAIRS + q and p % HALF > 1] for q in range(PAIRS)]


def events(b, q):
    if isinstance(b, int) and b in (0, BATCH):
        return [e for e in EVENTS[q] if e[3] == (b == BATCH)]
    return EVENTS[q]


def uses(b, m, what, j):
    n = 0
    for q in range(PAIRS):
        for e in events(b, q):
            if e[:2] == (what, j):
                return uses_before(b, m) + n
            n += e[2] == m
    raise ValueError(what)


def uses_before(b, m):
    if isinstance(b, int) and b == 0:
        return 0
    return sum(e[2] == m for q in EVENTS for e in q) * b - sum(e[2] == m and e[3] for q in EVENTS for e in q)


def tiles_before(b, before):
    return MPB * (b - 1) if before else MPB * b


ZERO_DMAS = NSLOT * D // (P * 2 * DH * L)
WTS_DMAS = 6
XQ = 4
Y_RING = 8
DT_BANKS = (0, 1, 6, 7)
EXP_LN_SET = 6

SMALL = 1 / 32
LOG_SMALL = float(np.log1p(SMALL))
_nodes = SMALL / 2 * (1 + np.cos(np.pi * (2 * np.arange(3) + 1) / 6))
_c2, _c1, _c0 = (float(c) for c in np.polyfit(_nodes, np.log1p(_nodes) / _nodes, 2))
SQ_SCALE = float(np.sqrt(_c2))
SQ_BIAS = _c1 / (2 * SQ_SCALE)
SQ_REST = _c0 - SQ_BIAS ** 2
PREP_STORES = ("gate_out", "c_out", "parts_out", "skip_out", "delta_out", "du_out")


def wait(eng, semaphore, value):
    if not isinstance(value, int) or value > 0:
        eng.wait_ge(semaphore, value)


def bank_written(eng, sems, b, what, j, m):
    wait(eng, sems[f"m{m}_ready"], uses(b, m, what, j) + 1)


def bank_empty(eng, sems, b, what, j, m):
    wait(eng, sems[f"m{m}_free"], uses(b, m, what, j))


def bank_emptied(eng, sems, b, what, j, m):
    wait(eng, sems[f"m{m}_free"], uses(b, m, what, j) + 1)


def build_kernel(nc, x_in, consts_in, chan_in, inw_in, xproj_in, dtw_in, outw_in,
                 route_in, b2_in, w1_in, w2_in, out):
    with ExitStack() as ctx:
        def sb(name, shape, dt=F32):
            return ctx.enter_context(nc.sbuf_tensor(name, shape, dt))

        def sem(name):
            return ctx.enter_context(nc.semaphore(name))

        def dram(name, shape, dt=F32):
            return nc.dram_tensor(name, shape, dt, kind="Internal").ap()

        delta_d = dram("delta_d", (BATCH, P, DH * L))
        du_d = dram("du_d", (BATCH, P, DH * L))
        gate_d = dram("gate_d", (BATCH, P, TPB * DIN))
        skip_d = dram("skip_d", (BATCH, P, TPB * DIN))
        parts_d = dram("parts_d", (BATCH, P, ND * L), BF16)
        c_d = dram("c_d", (BATCH, ND, NS, L))
        base_d = dram("base_d", (BATCH, P, TPB * D))
        mixed_d = dram("mixed_d", (BATCH, P, TPB * D))
        slots_d = dram("slots_d", (NSLOT, D))
        expert_d = dram("expert_d", (NSLOT, D))

        ident = sb("ident", [P, P])
        sel = sb("sel", [P, NS, P], BF16)
        chan = sb("chan", [P, DH, CH])
        half_taps = sb("half_taps", [P, DH, KC + 1])
        a_neg = sb("a_neg", [P, DH, NS])
        outw = sb("outw", [P, NH, D])
        pos = sb("pos", [P, NT * TOPK], I32)
        gates = sb("gates", [P, NT, TOPK])
        fit_bias = sb("fit_bias", [P, 1])
        tile_expert = sb("tile_expert", [P, NTILE], I32)

        delta = sb("delta", [P, 2, DH, L])
        du = sb("du", [P, 2, DH, L])
        gate = sb("gate", [P, 2, NH, TPB, P])
        skip = sb("skip", [P, 2, NH, TPB, P])
        base = sb("base", [P, 2, TPB * D])
        parts = sb("parts", [P, 2, ND, L], BF16)
        gated = sb("gated", [P, NH, TPB, P])
        gatedT = sb("gatedT", [P, NH, L])
        w1 = sb("w1", [P, W_RING, W1W])
        w2 = sb("w2", [P, W_RING, FC, D])
        rows = sb("rows", [P, W_RING, SH, D])
        rowsT = sb("rowsT", [P, S])
        yrows = sb("yrows", [P, W_RING, SH, D])
        mixed = sb("mixed", [P, TPB * D])

        ARENA = 31000
        arena = sb("arena", [P, ARENA])
        top = [0]

        def carve(n):
            at = top[0]
            top[0] += n
            assert top[0] <= ARENA, top[0]
            return arena[:, at:at + n]

        decay = carve(DA_RING * 2 * L).rearrange("p (r j l) -> p r j l", r=DA_RING, j=2)
        state = carve(H_RING * 2 * L).rearrange("p (r j l) -> p r j l", r=H_RING, j=2)
        c_rows = carve(C_RING * 2 * L).rearrange("p (r j l) -> p r j l", r=C_RING, j=2)
        hidden = carve(MPB * FC * S).rearrange("p (t f s) -> p t f s", t=MPB, f=FC)
        acc = state.rearrange("p r j l -> p (r j l)")[:, 0:TOK * D // P]
        y_tok = hidden.rearrange("p t f s -> p (t f s)")[:, 0:Y_RING * TOPK * D].rearrange("p (n d) -> p n d", d=D)
        top[0] = 0
        consts = carve(C_END)
        xnT = carve(TOK)
        inw = carve(2 * DIN)
        xproj = carve(ND * NH * (BR + NR)).rearrange("p (d h m) -> p d h m", d=ND, h=NH)
        dtw = carve(ND * DIN).rearrange("p (d c) -> p d c", d=ND)
        diag = carve(DH * P).rearrange("p (q m) -> p q m", q=DH)
        keys_sq = carve(E)
        route_w = carve(E)
        route_b = carve(E)
        route = carve(4 * E)
        b2 = carve(D)
        xn = carve(NT * D).rearrange("p (t d) -> p t d", t=NT)
        shared = top[0]
        x_all = carve(NT * D).rearrange("p (t d) -> p t d", t=NT)
        stats = carve(NT * 6).rearrange("p (t s) -> p t s", t=NT)
        mv = carve(NT * 2).rearrange("p (t s) -> p t s", t=NT)
        var_eps = carve(NT)
        std = carve(NT)
        rstd = carve(NT)
        logits = carve(NT * E)
        top8 = carve(NT * 8).rearrange("p (t k) -> p t k", t=NT)
        idx8 = carve(NT * 8).bitcast(U32).rearrange("p (t k) -> p t k", t=NT)
        idxf = carve(NT * TOPK)
        onehot = carve(NT * TOPK * E)
        product = carve(NT * TOPK * E)
        chosen = carve(NT * E // 2).bitcast(BF16)
        tri = carve(P // 2).bitcast(BF16)
        ones_b = carve(P // 2).bitcast(BF16)
        ones_f = carve(P)
        totals = carve(NT * E).rearrange("p (e t) -> p e t", e=E)
        upto = carve(NT * E).rearrange("p (e t) -> p e t", e=E)
        place = carve(NT * E)
        n_tiles = carve(E)
        end_tile = carve(E)
        slot0 = carve(E)
        compare = carve(E * NTILE)
        posf = carve(NT * TOPK)
        texp = carve(NTILE)
        gexp = carve(NT * TOPK)
        gsum = carve(NT)
        grec = carve(NT)
        mix_w = carve(NT * E)
        mix_wT = carve(2 * TPB * P).rearrange("p (a n) -> p a n", a=2)
        base_lo, base_hi = (ap.rearrange("p a h t c -> p (a h t c)").rearrange("p (b n) -> p b n", b=BATCH // 2)
                            for ap in (gate[:, :, :, :, :], skip[:, :, :, :, :]))
        routing_end = top[0]
        top[0] = shared
        PADL = L + 2 * (KC - 1)
        by_q = lambda ap: ap.rearrange("p (q l) -> p q l", q=DH)
        by_d = lambda ap: ap.rearrange("p (d l) -> p d l", d=ND)
        mag = by_q(carve(DH * L))
        pos_part = by_q(carve(DH * L))
        xpad = carve(NH * PADL).rearrange("p (h l) -> p h l", h=NH)
        v = by_q(carve(DH * L))
        th = by_q(carve(DH * L))
        u = by_q(carve(DH * L))
        xdbl = by_d(carve(ND * L))
        rest = by_d(carve(ND * L))
        part1 = by_d(carve(ND * L // 2).bitcast(BF16))
        part2 = by_d(carve(ND * L // 2).bitcast(BF16))
        parts_p = by_d(carve(ND * L // 2).bitcast(BF16))
        fit = by_q(carve(DH * L))
        ln1p = by_q(consts[:, C_SEL:C_END])
        small, du_p = du[:, 1], delta[:, 1]
        xb = mixed[:, :]
        zhalf = w2[:, :, :, :].rearrange("p r f d -> p (r f d)").rearrange("p (t c) -> p t c", t=TPB)
        zth = w1[:, :, :].rearrange("p r n -> p (r n)")[:, 0:TPB * DIN].rearrange("p (t c) -> p t c", t=TPB)
        skip_p = gatedT[:, :, :].rearrange("p h l -> p (h l)").rearrange("p (t c) -> p t c", t=TPB)
        prep_end = top[0]

        ps = ctx.enter_context(nc.psum_tensor("ps", [P, 8, 512], F32))
        b_ps = ps[:, 0:B_RING, :]
        y_ps = ps[:, 4:6, :]
        m_ps = [ps[:, 6, :], ps[:, 7, :]]

        names = """consts_in route_in wts_in a_exp zero_v slots_zeroed var_ready std_ready xn_ready xnT_ps xnT_ready
            kw_ready logit_ps keys_ps chosen_ready rank_ps pos_ready gdiff_ready gexp_ready mix_ready
            mixT_ps mixT_sb base_ps base_sb base_out scattered v_chain
            xb_ready xz_ps xpad_ready z_ps z_sb v_ready th_ready u_ready gate_ready xd_ps xd_sb
            part1_ready rest_ready part2_ready parts_ready dt_ps mag_ready
            small_ready square_ready exp_ready relu_ready ln_ready large_ready
            sum_ready fit_ready delta_ready du_ready skip_ps skip_sb gate_out c_out parts_out skip_out delta_out du_out decay_free prepared
            early_in0 early_in1 late_in0 late_in1 decay_ready b_ready dbx_done scan_done prod_done summed
            y_free gated_ready m0_ready m0_free m1_ready m1_free gelu_done
            mixed_out sp_step f_chain acc_in acc_ready out_done"""
        s = {n: sem(n) for n in names.split()}
        x_loaded = [sem(f"x_in{i}") for i in range(XQ)]
        c_in = [sem(f"c_in{i}") for i in range(C_RING)]
        w1_in_s = [sem(f"w1_in{i}") for i in range(W_RING)]
        w2_in_s = [sem(f"w2_in{i}") for i in range(W_RING)]
        rows_in = [sem(f"rows_in{i}") for i in range(W_RING)]
        y_out = [sem(f"y_out{i}") for i in range(W_RING)]
        y_in = [sem(f"y_in{i}") for i in range(Y_RING)]

        block = ctx.enter_context(nc.Block())

        def bc(ap, shape):
            return ap.to_broadcast(shape)

        def slot_rows(tile):
            return slots_d.rearrange("(t a p) d -> t p a d", a=SH, p=P)[tile]

        @block.sync
        def _(sp):
            sp.dma_start(consts[:, 0:C_SEL], consts_in[:, 0:C_SEL]).then_inc(s["consts_in"], 16)
            for k in range(XQ):
                own = slice(k * NT // XQ, (k + 1) * NT // XQ)
                sp.dma_start(x_all[:, own], x_in.rearrange("(t p) d -> p t d", p=P)[:, own]).then_inc(x_loaded[k], 16)
                if k == 0:
                    for dst, src in ((route[:, 0:3 * E], route_in), (b2[0:E, :], b2_in)):
                        sp.dma_start(dst, src).then_inc(s["route_in"], 16)
            for dst, src in ((chan[:, :, :], chan_in), (inw, inw_in), (xproj, xproj_in), (dtw[BR:BR + NR], dtw_in),
                             (outw[:, :, :], outw_in), (consts[:, C_SEL:C_END], consts_in[:, C_SEL:C_END])):
                sp.dma_start(dst, src).then_inc(s["wts_in"], 16)
            sp.wait_ge(s["zero_v"], 1)
            zeros = delta[:, :, :, :].rearrange("p a q l -> p (a q l)")
            fill = slots_d.rearrange("(k p n) d -> k p (n d)", p=P, n=2 * DH * L // D)
            for k in range(NSLOT // P // (2 * DH * L // D)):
                sp.dma_start(fill[k], zeros).then_inc(s["slots_zeroed"], 16)

            def one(t, b):
                return t[bass.ds(b, 1)].rearrange("e p n -> (e p) n")

            for k, held in enumerate((base_lo, base_hi)):
                half = slice(k * BATCH // 2, (k + 1) * BATCH // 2)
                sp.wait_ge(s["base_sb"], (k + 1) * BATCH // 2)
                sp.dma_start(base_d[half].rearrange("b p n -> p b n"), held).then_inc(s["base_out"], 16)

            def read_early(b, par):
                sp.dma_start(delta[:, par, :, :].rearrange("p q l -> p (q l)"), one(delta_d, b)).then_inc(s[f"early_in{par}"], 16)
                sp.dma_start(du[:, par, :, :].rearrange("p q l -> p (q l)"), one(du_d, b)).then_inc(s[f"early_in{par}"], 16)
                sp.dma_start(parts[:, par, :, :].rearrange("p d l -> p (d l)"), one(parts_d, b)).then_inc(s[f"early_in{par}"], 16)

            def read_late(b, par):
                for h in range(NH):
                    for dst, src in ((gate, gate_d), (skip, skip_d)):
                        sp.dma_start(dst[:, par, h, :, :],
                                     src[bass.ds(b, 1)].rearrange("e p (t h c) -> (e p) h t c", t=TPB, h=NH)[:, h])\
                            .then_inc(s[f"late_in{par}"], 16)
                sp.dma_start(base[:, par, :], one(base_d, b)).then_inc(s[f"late_in{par}"], 16)

            def expert_of(tile):
                return sp.value_load(tile_expert[0:1, bass.ds(tile, 1)], min_val=0, max_val=E - 1)

            def read_up(tile, slot):
                e = expert_of(tile)
                sp.dma_start(w1[:, slot, :], w1_in[bass.ds(e, 1)].rearrange("e p n -> (e p) n")).then_inc(w1_in_s[slot], 16)
                sp.dma_start(rows[:, slot, :, :],
                             slots_d.rearrange("(t a p) d -> t p a d", a=SH, p=P)[bass.ds(tile, 1)]
                             .rearrange("t p a d -> (t p) a d")).then_inc(rows_in[slot], 16)

            def read_down(tile, slot):
                e = expert_of(tile)
                sp.dma_start(w2[:, slot, :, :].rearrange("p f d -> p (f d)"),
                             w2_in[bass.ds(e, 1)].rearrange("e p n -> (e p) n")).then_inc(w2_in_s[slot], 16)

            def read_ahead():
                for n in PREP_STORES:
                    sp.wait_ge(s[n], 16)
                sp.wait_ge(s["slots_zeroed"], 16 * ZERO_DMAS)
                sp.wait_ge(s["base_out"], 32)
                read_early(0, 0)
                sp.wait_ge(s["scattered"], 16 * NT * TOPK)
                sp.wait_ge(s["gate_out"], 16 * BATCH)
                for j in range(W_RING):
                    read_up(j, j)
                    read_down(j, j)
                read_late(0, 0)

            def store(b, dst, src, ready, stored):
                sp.wait_ge(s[ready], b + 1)
                sp.sem_inc(s["sp_step"], 1)
                sp.dma_start(one(dst, b), src).then_inc(s[stored], 16)

            def store_gate(b):
                store(b, gate_d, zth.rearrange("p t c -> p (t c)"), "gate_ready", "gate_out")

            def store_prepared(b):
                sp.wait_ge(s["xd_sb"], ND * b + ND)
                sp.sem_inc(s["sp_step"], 1)
                sp.dma_start(c_d[bass.ds(b, 1)].rearrange("e d n l -> n (e d) l"),
                             xdbl[NS:2 * NS]).then_inc(s["c_out"], 16)
                if not isinstance(b, int) or b < BATCH - 1:
                    store_gate(b + 1)
                store(b, skip_d, skip_p.rearrange("p t c -> p (t c)"), "skip_sb", "skip_out")
                store(b, delta_d, pos_part.rearrange("p q l -> p (q l)"), "delta_ready", "delta_out")
                store(b, parts_d, parts_p.rearrange("p d l -> p (d l)"), "parts_ready", "parts_out")
                store(b, du_d, du_p.rearrange("p q l -> p (q l)"), "du_ready", "du_out")

            store_gate(0)
            store_prepared(0)
            with sp.Fori(1, BATCH - 2) as b:
                store_prepared(b)
            store_prepared(BATCH - 2)
            read_ahead()
            store_prepared(BATCH - 1)
            sp.wait_ge(s["prepared"], 1)
            sp.wait_ge(s["du_out"], 16 * BATCH)
            sp.wait_ge(s["skip_out"], 16 * BATCH)

            def read_c(b, r):
                g, d = r // ND, r % ND
                src = c_d[bass.ds(b, 1), d, 2 * g:2 * g + 2, :].rearrange("e j l -> e (j l)")
                sp.dma_start(c_rows[:, r % C_RING, :, :].rearrange("p j l -> p (j l)"),
                             src.to_broadcast([P, 2 * L])).then_inc(c_in[r % C_RING], 16)

            def batch(b, par):
                first = isinstance(b, int) and b == 0
                nxt = (b + 1) % BATCH
                todo = []

                def early():
                    wait(sp, s["decay_ready"], DECAYS * b)
                    wait(sp, s["dbx_done"], DECAYS * b)
                    wait(sp, s["b_ready"], DECAYS * b)
                    sp.sem_inc(s["sp_step"], 1)
                    read_early(nxt, 1 - par)
                todo.append((0.5, early))

                todo.append((23.5, lambda: read_late(nxt, 1 - par)))
                for r in range(CPB):
                    def c(r=r):
                        sp.wait_ge(s["prod_done"], PAIRS * b + 2 * (r + 1))
                        sp.sem_inc(s["sp_step"], 1)
                        rn = r + C_RING
                        read_c(b if rn < CPB else nxt, rn % CPB)
                    todo.append((2 * r + 3, c))
                todo += tile_traffic(b)
                for _, f in sorted(todo, key=lambda x: x[0]):
                    f()

            def tile_traffic(b):
                todo = []
                for q in range(PAIRS):
                    for what, j, m, before in events(b, q):
                        tiles = tiles_before(b, before)

                        def up(j=j, m=m, tiles=tiles):
                            bank_emptied(sp, s, b, "U1", j, m)
                            sp.sem_inc(s["sp_step"], 1)
                            read_up((tiles + j + W_RING) % NTILE, j % W_RING)

                        def down(j=j, m=m, tiles=tiles):
                            bank_written(sp, s, b, "D", j, m)
                            sp.sem_inc(s["sp_step"], 1)
                            read_down((tiles + j + W_RING) % NTILE, j % W_RING)

                        def store(j=j, m=m, tiles=tiles):
                            bank_emptied(sp, s, b, "D", j, m)
                            sp.sem_inc(s["sp_step"], 1)
                            sp.dma_start(expert_d.rearrange("(t a p) d -> t p a d", a=SH, p=P)[bass.ds(tiles + j, 1)]
                                         .rearrange("t p a d -> (t p) a d"),
                                         yrows[:, j % W_RING, :, :]).then_inc(y_out[j % W_RING], 16)

                        def mix(m=m):
                            bank_emptied(sp, s, b, "O", 0, m)
                            sp.sem_inc(s["sp_step"], 1)
                            sp.dma_start(one(mixed_d, b - 1), mixed[:, :]).then_inc(s["mixed_out"], 16)

                        if what == "U1":
                            todo.append((q + 1.5, up))
                        elif what == "D":
                            todo += [(q + 1.2, down), (q + 1.6, store)]
                        elif what == "O":
                            todo.append((q + 1.8, mix))
                return todo

            for r in range(C_RING):
                read_c(0, r)
            batch(0, 0)
            batch(1, 1)
            with sp.Fori(1, BATCH // 2) as i:
                batch(2 * i, 0)
                batch(2 * i + 1, 1)
            for _, f in tile_traffic(BATCH):
                f()
            sp.wait_ge(s["mixed_out"], 16 * BATCH)
            sp.wait_ge(s["summed"], PAIRS * BATCH)
            sp.dma_start(acc.rearrange("p (b n) -> p b n", b=BATCH), mixed_d.rearrange("b p n -> p b n")).then_inc(s["acc_in"], 16)
            for b in range(BATCH):
                sp.wait_ge(s["acc_ready"], TPB * (b + 1))
                sp.dma_start(out.rearrange("(t p) d -> p t d", p=P)[:, TPB * b:TPB * (b + 1), :],
                             acc[:, TPB * b * D:TPB * (b + 1) * D].rearrange("p (t d) -> p t d", t=TPB))\
                    .then_inc(s["out_done"], 16)
            sp.wait_ge(s["out_done"], 16 * BATCH)
            for par in range(2):
                sp.wait_ge(s[f"early_in{par}"], 16 * 3 * (BATCH // 2 + (1 - par)))
                sp.wait_ge(s[f"late_in{par}"], 16 * 5 * (BATCH // 2 + (1 - par)))
            for i in range(C_RING):
                sp.wait_ge(c_in[i], 16 * (BATCH * CPB // C_RING + 1))
            for i in range(W_RING):
                sp.wait_ge(w1_in_s[i], 16 * (NTILE // W_RING + 1))
                sp.wait_ge(w2_in_s[i], 16 * (NTILE // W_RING + 1))
                sp.wait_ge(rows_in[i], 16 * (NTILE // W_RING + 1))
                sp.wait_ge(y_out[i], 16 * (NTILE // W_RING))

        @block.gpsimd
        def _(pool):
            nc.gpsimd.memset(delta[:, :, :, :], 0.0).then_inc(s["zero_v"], 1)
            pool.wait_ge(s["slots_zeroed"], 16 * ZERO_DMAS)
            pool.wait_ge(s["xn_ready"], NT)
            pool.wait_ge(s["pos_ready"], 1)
            for t in range(NT):
                for k in range(TOPK):
                    pool.indirect_dma_start(slots_d, bass.IndirectOffsetOnAxis(
                        ap=pos[:, t * TOPK + k:t * TOPK + k + 1], axis=0), xn[:, t, :], None).then_inc(s["scattered"], 16)
            pool.wait_ge(s["prepared"], 1)

            def batch(b):
                for q in range(PAIRS):
                    r, h = q // NH, q % NH
                    wait(pool, s["scan_done"], DECAYS * b + 2 * q + 2)
                    if h == 0:
                        pool.wait_ge(c_in[r % C_RING], 16 * (CPB // C_RING * b + r // C_RING + 1))
                    nc.gpsimd.tensor_tensor(state[:, q % H_RING], state[:, q % H_RING], c_rows[:, r % C_RING],
                                            ALU.mult).then_inc(s["prod_done"], 1)

            batch(0)
            batch(1)
            with pool.Fori(1, BATCH // 2) as i:
                batch(2 * i)
                batch(2 * i + 1)
            for i in range(W_RING):
                pool.wait_ge(y_out[i], 16 * (NTILE // W_RING))
            for t in range(NT):
                wait(pool, s["acc_ready"], t - Y_RING + 1)
                for k in range(TOPK):
                    pool.indirect_dma_start(y_tok[:, (t % Y_RING) * TOPK + k, :], None, expert_d, bass.IndirectOffsetOnAxis(
                        ap=pos[:, t * TOPK + k:t * TOPK + k + 1], axis=0)).then_inc(y_in[t % Y_RING], 16)

        @block.scalar
        def _(act):
            per = NT // XQ
            for k in range(XQ + 1):
                if k < XQ:
                    act.wait_ge(s["var_ready"], k + 1)
                    nc.scalar.activation(std[:, k * per:(k + 1) * per], var_eps[:, k * per:(k + 1) * per], ACT.Sqrt)\
                        .then_inc(s["std_ready"], 1)
                if k > 0:
                    for g in range((k - 1) * per // TPB, k * per // TPB):
                        act.wait_ge(s["xnT_ps"], g + 1)
                        nc.scalar.copy(xnT[:, g * L:(g + 1) * L], ps[:, 2 + g % 4, :]).then_inc(s["xnT_ready"], 1)
            act.wait_ge(s["wts_in"], 16 * WTS_DMAS)
            nc.scalar.activation(a_neg[:, :, :], chan[:, :, KC + 3:CH], ACT.Exp).then_inc(s["a_exp"], 1)
            act.wait_ge(s["gdiff_ready"], 1)
            nc.scalar.activation(gexp, idxf, ACT.Exp).then_inc(s["gexp_ready"], 1)
            def take_projected(b):
                act.wait_ge(s["xz_ps"], b + 1)
                wait(act, s["v_ready"], b)
                nc.scalar.copy(xpad[:, :, KC - 1:KC - 1 + L], ps[:, 0:2, :]).then_inc(s["xpad_ready"], 1)
                act.wait_ge(s["z_ps"], b + 1)
                wait(act, s["gate_out"], 16 * b)
                z_ps = ps[:, 4:6, :].rearrange("p a n -> p (a n)")
                nc.scalar.mul(zhalf.rearrange("p t c -> p (t c)"), z_ps, 0.5)
                nc.scalar.activation(zth.rearrange("p t c -> p (t c)"), z_ps, ACT.Tanh, scale=0.5).then_inc(s["z_sb"], 1)

            def take_tanh(b):
                act.wait_ge(s["v_ready"], b + 1)
                nc.scalar.activation(th, v, ACT.Tanh).then_inc(s["th_ready"], 1)

            def prepare(b):
                last_but = lambda n: not isinstance(b, int) or b < BATCH - n
                wait(act, s["c_out"], 16 * b)
                for d in range(ND):
                    act.wait_ge(s["xd_ps"], ND * b + d + 1)
                    nc.scalar.copy(xdbl[0:BR + NR, d], ps[0:BR + NR, 4 + d, :]).then_inc(s["xd_sb"], 1)
                nc.scalar.copy(part1[0:BR], ps[0:BR, 4:6, :]).then_inc(s["part1_ready"], 1)
                wait(act, s["fit_ready"], b)
                for q in range(DH):
                    act.wait_ge(s["dt_ps"], ND * b + q // NH + 1)
                    last = nc.scalar.activation(mag[:, q, :], ps[:, DT_BANKS[q], :], ACT.Abs, bias=chan[:, q, KC + 1:KC + 2])
                last.then_inc(s["mag_ready"], 1)
                nc.scalar.add_instruction(mybir.InstLoadActFuncSet(name=nc.get_next_instruction_name(), act_func_set_id=EXP_LN_SET))
                act.wait_ge(s["mag_ready"], b + 1)
                nc.scalar.activation(mag, mag, ACT.Exp, scale=-1.0).then_inc(s["exp_ready"], 1)
                act.wait_ge(s["exp_ready"], b + 1)
                nc.scalar.activation(ln1p, mag, ACT.Ln, bias=1.0).then_inc(s["ln_ready"], 1)
                wait(act, s["delta_out"], 16 * b)
                for q in range(DH):
                    last = nc.scalar.activation(pos_part[:, q, :], ps[:, DT_BANKS[q], :], ACT.Relu, bias=chan[:, q, KC + 1:KC + 2])
                last.then_inc(s["relu_ready"], 1)
                act.wait_ge(s["small_ready"], b + 1)
                nc.scalar.activation(fit, small, ACT.Square, scale=SQ_SCALE, bias=fit_bias[:, 0:1]).then_inc(s["square_ready"], 1)
                act.wait_ge(s["rest_ready"], b + 1)
                nc.scalar.copy(part2[0:BR], rest[0:BR]).then_inc(s["part2_ready"], 1)
                act.wait_ge(s["skip_ps"], b + 1)
                wait(act, s["skip_out"], 16 * b)
                nc.scalar.copy(skip_p.rearrange("p t c -> p (t c)"), ps[:, 2:4, :].rearrange("p a n -> p (a n)")).then_inc(s["skip_sb"], 1)
                if last_but(1):
                    take_tanh(b + 1)
                if last_but(2):
                    take_projected(b + 2)

            take_projected(0)
            for g in range(BATCH):
                act.wait_ge(s["mixT_ps"], g + 1)
                wait(act, s["base_ps"], g - 1)
                nc.scalar.copy(mix_wT[0:E, g % 2, :], ps[0:E, 2 + g % 2, :]).then_inc(s["mixT_sb"], 1)
            take_tanh(0)
            take_projected(1)
            act.wait_ge(s["base_sb"], BATCH)
            prepare(0)
            with act.Fori(1, BATCH - 2) as b:
                prepare(b)
            for b in range(BATCH - 2, BATCH):
                prepare(b)
            act.wait_ge(s["decay_free"], 1)

            def empty(b, q):
                for what, j, m, before in events(b, q):
                    bank = m_ps[m]
                    if what == "O":
                        continue
                    bank_written(act, s, b, what, j, m)
                    if what == "T":
                        last = nc.scalar.copy(rowsT[:, :], bank[:, 0:S])
                    elif what in ("U0", "U1"):
                        for f in range(2):
                            c = 2 * (what == "U1") + f
                            last = nc.scalar.activation(hidden[:, j, c, :], bank[:, f * S:(f + 1) * S], ACT.Identity,
                                                        bias=w1[:, j % W_RING, FF + c:FF + c + 1])
                    elif what == "D":
                        wait(act, y_out[j % W_RING], 16 * (tiles_before(b, before) // W_RING + j // W_RING)
                             if isinstance(b, int) else 16 * (MPB // W_RING * (b - before) + j // W_RING))
                        last = nc.scalar.copy(yrows[:, j % W_RING, :, :].rearrange("p a d -> p (a d)"), bank[:, 0:S])
                    elif what == "G":
                        last = nc.scalar.copy(gatedT[:, j, :], bank)
                    last.then_inc(s[f"m{m}_free"], 1)

            def gelus(b, n, now):
                for k in range(GROUP):
                    if isinstance(b, int) and not 0 <= b < BATCH:
                        pass
                    else:
                        if k == 0:
                            for what, m in (("U0", 1), ("U1", 0)):
                                bank_emptied(act, s, b, what, GROUP * (n + 1) - 1, m)
                        h = hidden[:, GROUP * n + k, :, :].rearrange("p f s -> p (f s)")
                        nc.scalar.activation(h, h, ACT.Gelu).then_inc(s["gelu_done"], 1)
                    if k in (1, 3):
                        empty(now, BURST_STEPS[n][k // 2])

            def besides(b, q):
                if not (isinstance(b, int) and b == 0):
                    for p in EMPTY_AFTER[q]:
                        empty(b - 1, p)
                for p in EMPTY[q]:
                    empty(b, p)
                if q in GELU_STEP:
                    n = GELU_STEP.index(q)
                    gelus(b - n, n, b)

            def batch(b, par, i):
                act.wait_ge(s[f"early_in{par}"], 48 * i + 48)
                for q in range(PAIRS):
                    g, dh = q // DH, q % DH
                    wait(act, s["scan_done"], DECAYS * b + 2 * (q - DA_RING) + 2)
                    lo = 1 if dh < NH else 0
                    for j in range(2):
                        nc.scalar.activation(decay[:, q % DA_RING, j, lo:lo + L - 1], delta[:, par, dh, lo:lo + L - 1], ACT.Exp,
                                             scale=a_neg[:, dh, 2 * g + j:2 * g + j + 1]).then_inc(s["decay_ready"], 1)
                    if isinstance(b, int) and b == 0 and q == EMPTY_LAG - 1:
                        act.wait_ge(s["prepared"], 1)
                    besides(b, q)

            batch(0, 0, 0)
            batch(1, 1, 0)
            with act.Fori(1, BATCH // 2) as i:
                batch(2 * i, 0, i)
                batch(2 * i + 1, 1, i)
            for q in range(PAIRS):
                besides(BATCH, q)

        @block.tensor
        def _(pe):
            for g in range(BATCH + 1):
                if g < BATCH:
                    pe.wait_ge(s["xn_ready"], TPB * (g + 1))
                    wait(pe, s["xnT_ready"], g - 3)
                    for t in range(TPB):
                        last = nc.tensor.transpose(ps[:, 2 + g % 4, t * P:(t + 1) * P], xn[:, g * TPB + t, :], ident[:, :])
                    last.then_inc(s["xnT_ps"], 1)
                if g == 1:
                    pe.wait_ge(s["kw_ready"], 1)
                    nc.tensor.matmul(ps[:, 6, 0:E], ones_f, keys_sq, start=True, stop=True).then_inc(s["keys_ps"], 1)
                if g > 0:
                    pe.wait_ge(s["xnT_ready"], g)
                    for t in range((g - 1) * TPB, g * TPB):
                        last = nc.tensor.matmul(ps[:, 7, t * E:(t + 1) * E], xnT[:, t * P:(t + 1) * P], route_w,
                                                start=True, stop=True)
            last.then_inc(s["logit_ps"], 1)
            pe.wait_ge(s["chosen_ready"], 1)
            nc.tensor.matmul(ps[:, 0, :], tri, chosen, start=True, stop=True)
            nc.tensor.matmul(ps[:, 1, :], ones_b, chosen, start=True, stop=True).then_inc(s["rank_ps"], 1)

            def project_in(b):
                pe.wait_ge(s["xb_ready"], b + 1)
                wait(pe, s["relu_ready"], b - 1)
                wait(pe, s["xpad_ready"], b)
                for h in range(NH):
                    last = nc.tensor.matmul(ps[:, h, :], inw[:, h * P:(h + 1) * P], xb, start=True, stop=True)
                last.then_inc(s["xz_ps"], 1)
                wait(pe, s["part1_ready"], b - 1)
                wait(pe, s["z_sb"], b)
                for t in range(TPB):
                    last = nc.tensor.matmul(ps[:, 4 + t // 2, t % 2 * DIN:(t % 2 + 1) * DIN], xb[:, t * P:(t + 1) * P],
                                            inw[:, DIN:2 * DIN], start=True, stop=True)
                last.then_inc(s["z_ps"], 1)

            def prepare(b):
                ahead = min(b + 2, BATCH) if isinstance(b, int) else b + 2
                pe.wait_ge(s["z_sb"], ahead)
                for d in range(ND):
                    pe.wait_ge(s["u_ready"], ND * b + d + 1)
                    for h in range(NH):
                        last = nc.tensor.matmul(ps[0:BR + NR, 4 + d, :], xproj[:, d, h, :], u[:, d * NH + h, :],
                                                start=h == 0, stop=h == NH - 1)
                    last.then_inc(s["xd_ps"], 1)
                wait(pe, s["skip_sb"], b)
                def skip_tile(t):
                    for h in range(NH):
                        for d in range(ND):
                            o = t % 2 * DIN + h * P
                            last = nc.tensor.matmul(ps[:, 2 + t // 2, o:o + P], u[:, d * NH + h, t * P:(t + 1) * P],
                                                    diag[:, d * NH + h, :], start=d == 0, stop=d == ND - 1)
                    return last
                wait(pe, s["relu_ready"], b)
                pe.wait_ge(s["xpad_ready"], ahead)
                for d in range(ND):
                    pe.wait_ge(s["xd_sb"], ND * b + d + 1)
                    for h in range(NH):
                        last = nc.tensor.matmul(ps[:, DT_BANKS[d * NH + h], :], dtw[BR:BR + NR, d, h * P:(h + 1) * P],
                                                xdbl[BR:BR + NR, d, :], start=True, stop=True)
                    last.then_inc(s["dt_ps"], 1)
                for t in range(TPB):
                    last = skip_tile(t)
                last.then_inc(s["skip_ps"], 1)
                if not isinstance(b, int) or b < BATCH - 2:
                    project_in(b + 2)

            project_in(0)
            pe.wait_ge(s["mix_ready"], 1)
            for g in range(BATCH + 1):
                if g < BATCH:
                    wait(pe, s["mixT_sb"], g - 1)
                    for t in range(TPB):
                        tt = g * TPB + t
                        last = nc.tensor.transpose(ps[0:E, 2 + g % 2, t * P:(t + 1) * P], mix_w[:, tt * E:(tt + 1) * E], ident[:, :])
                    last.then_inc(s["mixT_ps"], 1)
                if g > 0:
                    k = g - 1
                    pe.wait_ge(s["mixT_sb"], k + 1)
                    wait(pe, s["base_sb"], k - 1)
                    for t in range(TPB):
                        last = nc.tensor.matmul(ps[:, 6 + k % 2, t * P:(t + 1) * P], mix_wT[0:E, k % 2, t * P:(t + 1) * P], b2[0:E, :],
                                                start=True, stop=True)
                    last.then_inc(s["base_ps"], 1)
                if g == 3:
                    project_in(1)
            prepare(0)
            with pe.Fori(1, BATCH - 2) as b:
                prepare(b)
            for b in range(BATCH - 2, BATCH):
                prepare(b)
            for n in ("skip_sb", "part1_ready", "relu_ready"):
                pe.wait_ge(s[n], BATCH)

            def sum_states(b, q):
                g, d, h = q // DH, q // NH % ND, q % NH
                pe.wait_ge(s["prod_done"], PAIRS * b + q + 1)
                if q < NH:
                    wait(pe, s["y_free"], NH * (b - 1) + h + 1)
                for j in range(2):
                    for t in range(TPB):
                        last = nc.tensor.matmul(y_ps[:, h, t * P:(t + 1) * P], state[:, q % H_RING, j, t * P:(t + 1) * P], ident[:, :],
                                                is_transpose=True, start=q < NH and j == 0 and t == 0,
                                                stop=q >= PAIRS - NH and j == 1, skip_group_check=True)
                last.then_inc(s["summed"], 1)

            def besides(b, q):
                for what, j, m, before in events(b, q):
                    bank, slot = m_ps[m], j % W_RING
                    loads = MPB // W_RING * (b - before) + j // W_RING + 1
                    bank_empty(pe, s, b, what, j, m)
                    if what == "T":
                        pe.wait_ge(rows_in[slot], 16 * loads)
                        for a in range(SH):
                            last = nc.tensor.transpose(bank[:, a * P:(a + 1) * P], rows[:, slot, a, :], ident[:, :])
                    elif what in ("U0", "U1"):
                        if what == "U0":
                            bank_emptied(pe, s, b, "T", j, 0)
                            pe.wait_ge(w1_in_s[slot], 16 * loads)
                        for f in range(2):
                            c = 2 * (what == "U1") + f
                            last = nc.tensor.matmul(bank[:, f * S:(f + 1) * S], w1[:, slot, c * P:(c + 1) * P], rowsT[:, :],
                                                    start=True, stop=True)
                    elif what == "D":
                        pe.wait_ge(w2_in_s[slot], 16 * loads)
                        pe.wait_ge(s["gelu_done"], MPB * (b - before) + j + 1)
                        for a in range(SH):
                            for c in range(FC):
                                last = nc.tensor.matmul(bank[:, a * P:(a + 1) * P], hidden[:, j, c, a * P:(a + 1) * P], w2[:, slot, c, :],
                                                        start=c == 0, stop=c == FC - 1)
                    elif what == "G":
                        pe.wait_ge(s["gated_ready"], NH * (b - 1) + j + 1)
                        for t in range(TPB):
                            last = nc.tensor.transpose(bank[:, t * P:(t + 1) * P], gated[:, j, t, :], ident[:, :])
                    else:
                        for k in range(NH):
                            bank_emptied(pe, s, b, "G", k, k)
                        for t in range(TPB):
                            for h in range(NH):
                                last = nc.tensor.matmul(bank[:, t * P:(t + 1) * P], gatedT[:, h, t * P:(t + 1) * P], outw[:, h, :],
                                                        start=h == 0, stop=h == NH - 1)
                    last.then_inc(s[f"m{m}_ready"], 1)

            def batch(b, par, i):
                first = isinstance(b, int) and b == 0
                pe.wait_ge(s[f"early_in{par}"], 48 * i + 48)
                for q in range(PAIRS):
                    g, d = q // DH, q // NH % ND
                    for j in range(2):
                        tau = 2 * q + j
                        wait(pe, s["scan_done"], DECAYS * b + tau - B_RING + 1)
                        nc.tensor.matmul(b_ps[:, tau % B_RING, :], sel[:, 2 * g + j, :], parts[:, par, d, :],
                                         start=True, stop=True).then_inc(s["b_ready"], 1)
                    besides(b, q)
                    if not first:
                        for k in SUMS_AFTER[q]:
                            sum_states(b - 1, k)
                    for k in SUMS[q]:
                        sum_states(b, k)

            batch(0, 0, 0)
            batch(1, 1, 0)
            with pe.Fori(1, BATCH // 2) as i:
                batch(2 * i, 0, i)
                batch(2 * i + 1, 1, i)
            for q in range(PAIRS):
                for k in SUMS_AFTER[q]:
                    sum_states(BATCH - 1, k)
                besides(BATCH, q)

        @block.vector
        def _(dve):
            done = [0]

            def link(ins):
                done[0] += 1
                ins.then_inc(s["v_chain"], 1)
                dve.wait_ge(s["v_chain"], done[0])

            dve.wait_ge(s["consts_in"], 16)
            nc.vector.tensor_copy(ident[:, :], consts[:, C_ID:C_ID + P])
            nc.vector.tensor_copy(tri, consts[:, C_TRI:C_TRI + P])
            nc.vector.memset(ones_f, 1.0)
            nc.vector.memset(ones_b, 1.0)
            nc.vector.memset(fit_bias[:, :], SQ_BIAS)
            per = NT // XQ
            for k in range(XQ + 1):
                if k < XQ:
                    own = slice(k * per, (k + 1) * per)
                    dve.wait_ge(x_loaded[k], 16)
                    for t in range(k * per, (k + 1) * per):
                        last = nc.vector.bn_stats(stats[:, t, :], x_all[:, t, :])
                    link(last)
                    for t in range(k * per, (k + 1) * per):
                        last = nc.vector.bn_aggr(mv[:, t, :], stats[:, t, :])
                    link(last)
                    nc.vector.tensor_scalar(var_eps[:, own], mv[:, own, 1], EPS, None, ALU.add).then_inc(s["var_ready"], 1)
                if k > 0:
                    own = slice((k - 1) * per, k * per)
                    dve.wait_ge(s["std_ready"], k)
                    link(nc.vector.reciprocal(rstd[:, own], std[:, own]))
                    for t in range((k - 1) * per, k * per):
                        nc.vector.tensor_scalar(xn[:, t, :], x_all[:, t, :], mv[:, t, 0:1], rstd[:, t:t + 1],
                                                ALU.subtract, ALU.mult).then_inc(s["xn_ready"], 1)
                if k == 1:
                    dve.wait_ge(s["route_in"], 32)
                    keysT, rwT, rb = (route[:, n * E:(n + 1) * E] for n in range(3))
                    nc.vector.scalar_tensor_tensor(route_w, keysT, 2.0, rwT, ALU.mult, ALU.add)
                    nc.vector.tensor_tensor(keys_sq, keysT, keysT, ALU.mult).then_inc(s["kw_ready"], 1)
            dve.wait_ge(s["keys_ps"], 1)
            link(nc.vector.tensor_tensor(route_b, rb, ps[:, 6, 0:E], ALU.subtract))
            dve.wait_ge(s["logit_ps"], 1)
            te = lambda ap: ap.rearrange("p (t e) -> p t e", e=E)
            link(nc.vector.tensor_tensor(te(logits), te(ps[:, 7, :]), bc(route_b.unsqueeze(1), [P, NT, E]), ALU.add))
            for t in range(NT):
                last = nc.vector.max(top8[:, t, :], te(logits)[:, t, :])
            link(last)
            for t in range(NT):
                last = nc.vector.max_index(idx8[:, t, :], top8[:, t, :], te(logits)[:, t, :])
            link(last)
            tk = lambda ap: ap.rearrange("p (t k) -> p t k", k=TOPK)
            link(nc.vector.tensor_copy(tk(idxf), idx8[:, :, 0:TOPK]))
            iota = consts[:, C_IOTA:C_IOTA + E]
            tke = lambda ap: ap.rearrange("p (n e) -> p n e", e=E)
            link(nc.vector.tensor_tensor(tke(onehot), bc(idxf.unsqueeze(2), [P, NT * TOPK, E]),
                                         bc(iota.unsqueeze(1), [P, NT * TOPK, E]), ALU.is_equal))
            oh4 = onehot.rearrange("p (t k e) -> p t k e", k=TOPK, e=E)
            with nc.allow_low_precision(reason="zeros and ones"):
                nc.vector.tensor_reduce(te(chosen), oh4.rearrange("p t k e -> p t e k"), AXX, ALU.add).then_inc(s["chosen_ready"], 1)
            dve.wait_ge(s["rank_ps"], 1)
            link(nc.vector.tensor_copy(totals, ps[:, 1, :].rearrange("p (t e) -> p e t", e=E)))
            flat = lambda ap: ap.rearrange("p e t -> p (e t)")
            link(nc.vector.tensor_tensor_scan(flat(upto), consts[:, C_MASK:C_MASK + NT * E], flat(totals), 0.0, ALU.mult, ALU.add))
            cmp1 = compare[:, 0:E * E].rearrange("p (e j) -> p e j", j=E)
            link(nc.vector.tensor_tensor(cmp1, bc(upto[:, :, NT - 1:NT], [P, E, E]),
                                         bc(consts[:, C_THR:C_THR + E].unsqueeze(1), [P, E, E]), ALU.is_gt))
            link(nc.vector.tensor_reduce(n_tiles, cmp1, AXX, ALU.add))
            link(nc.vector.tensor_tensor_scan(end_tile, ones_f[:, 0:E], n_tiles, 0.0, ALU.mult, ALU.add))
            link(nc.vector.tensor_tensor(slot0, end_tile, n_tiles, ALU.subtract))
            link(nc.vector.tensor_scalar(slot0, slot0, float(S), None, ALU.mult))
            link(nc.vector.tensor_tensor(upto, upto, totals, ALU.subtract))
            link(nc.vector.tensor_tensor(upto, upto, bc(slot0.unsqueeze(2), [P, E, NT]), ALU.add))
            link(nc.vector.tensor_tensor(te(place), te(ps[:, 0, :]), upto.rearrange("p e t -> p t e"), ALU.add))
            pr4 = product.rearrange("p (t k e) -> p t k e", k=TOPK, e=E)
            link(nc.vector.tensor_tensor(pr4, oh4, bc(te(place).unsqueeze(2), [P, NT, TOPK, E]), ALU.mult))
            link(nc.vector.tensor_reduce(posf, tke(product), AXX, ALU.add))
            nc.vector.tensor_copy(pos[:, :], posf).then_inc(s["pos_ready"], 1)
            nc.vector.tensor_tensor(tk(idxf), top8[:, :, 0:TOPK], bc(top8[:, :, 0:1], [P, NT, TOPK]),
                                    ALU.subtract).then_inc(s["gdiff_ready"], 1)
            cmp2 = compare.rearrange("p (t e) -> p t e", e=E)
            link(nc.vector.tensor_tensor(cmp2, bc(end_tile.unsqueeze(1), [P, NTILE, E]),
                                         bc(consts[:, C_TILE:C_TILE + NTILE].unsqueeze(2), [P, NTILE, E]), ALU.is_le))
            link(nc.vector.tensor_reduce(texp, cmp2, AXX, ALU.add))
            link(nc.vector.tensor_scalar(tile_expert[:, :], texp, float(E - 1), None, ALU.min))
            dve.wait_ge(s["gexp_ready"], 1)
            link(nc.vector.tensor_reduce(gsum, tk(gexp), AXX, ALU.add))
            link(nc.vector.reciprocal(grec, gsum))
            link(nc.vector.tensor_tensor(gates[:, :, :], tk(gexp), bc(grec.unsqueeze(2), [P, NT, TOPK]), ALU.mult))
            link(nc.vector.tensor_tensor(tke(product), tke(onehot),
                                         bc(gates[:, :, :].rearrange("p t k -> p (t k)").unsqueeze(2), [P, NT * TOPK, E]), ALU.mult))
            nc.vector.tensor_reduce(te(mix_w), pr4.rearrange("p t k e -> p t e k"), AXX, ALU.add).then_inc(s["mix_ready"], 1)
            link(nc.vector.memset(xpad[:, :, :], 0.0))
            nc.vector.tensor_copy(xb, xnT[:, 0:L]).then_inc(s["xb_ready"], 1)
            dve.wait_ge(s["wts_in"], 16 * WTS_DMAS)
            nc.vector.tensor_copy(sel[:, :, :].rearrange("p n m -> p (n m)"), consts[:, C_SEL:C_END])
            nc.vector.tensor_scalar(half_taps[:, :, :], chan[:, :, 0:KC + 1], 0.5, None, ALU.mult)
            dve.wait_ge(s["a_exp"], 1)
            nc.vector.tensor_scalar(a_neg[:, :, :], a_neg[:, :, :], -1.0, None, ALU.mult)
            for q in range(DH):
                nc.vector.tensor_scalar(diag[:, q, :], consts[:, C_ID:C_ID + P], chan[:, q, KC + 2:KC + 3], None, ALU.mult)
            def residual(g):
                dve.wait_ge(s["base_ps"], g + 1)
                held = (base_lo, base_hi)[g * 2 // BATCH][:, g % (BATCH // 2)]
                nc.vector.tensor_tensor(held, ps[:, 6 + g % 2, :], x_all[:, g * TPB:(g + 1) * TPB, :].rearrange("p t d -> p (t d)"),
                                        ALU.add).then_inc(s["base_sb"], 1)

            def copy_x(b):
                wait(dve, s["z_ps"], b)
                nc.vector.tensor_copy(xb, xnT[:, bass.ds(b * L, L)]).then_inc(s["xb_ready"], 1)

            def convolve(b):
                dve.wait_ge(s["xpad_ready"], b + 1)
                wait(dve, s["u_ready"], ND * b)
                for k in range(KC):
                    for q in range(DH):
                        d, h = q // NH, q % NH
                        o = k if d == 0 else 2 * (KC - 1) - k
                        src = xpad[:, h, o:o + L]
                        if k == 0:
                            ins = nc.vector.tensor_scalar(v[:, q, :], src, half_taps[:, q, 0:1], half_taps[:, q, KC:KC + 1],
                                                          ALU.mult, ALU.add)
                        else:
                            dve.wait_ge(s["v_chain"], start + (KC - 1) * DH * b + (k - 1) * DH + q + 1)
                            ins = nc.vector.scalar_tensor_tensor(v[:, q, :], src, half_taps[:, q, k:k + 1], v[:, q, :],
                                                                 ALU.mult, ALU.add)
                        if k < KC - 1:
                            ins.then_inc(s["v_chain"], 1)
                ins.then_inc(s["v_ready"], 1)

            def gate_z(b):
                dve.wait_ge(s["z_sb"], b + 1)
                nc.vector.scalar_tensor_tensor(zth, zth, 1.0, zhalf, ALU.add, ALU.mult).then_inc(s["gate_ready"], 1)

            def prepare(b):
                last_but = lambda n: not isinstance(b, int) or b < BATCH - n
                dve.wait_ge(s["th_ready"], b + 1)
                dve.wait_ge(s["v_ready"], b + 1)
                wait(dve, s["skip_ps"], b)
                wait(dve, s["du_ready"], b)
                for d in range(ND):
                    way = slice(d * NH, (d + 1) * NH)
                    nc.vector.scalar_tensor_tensor(u[:, way], th[:, way], 1.0, v[:, way], ALU.add, ALU.mult).then_inc(s["u_ready"], 1)
                if last_but(1):
                    convolve(b + 1)
                if last_but(2):
                    copy_x(b + 2)
                dve.wait_ge(s["part1_ready"], b + 1)
                nc.vector.scalar_tensor_tensor(rest[0:BR], part1[0:BR], consts[0:BR, C_PART:C_PART + 1], xdbl[0:BR],
                                               ALU.mult, ALU.add).then_inc(s["rest_ready"], 1)
                if last_but(1):
                    gate_z(b + 1)
                dve.wait_ge(s["exp_ready"], b + 1)
                nc.vector.tensor_scalar(small, mag, SMALL, None, ALU.min).then_inc(s["small_ready"], 1)
                dve.wait_ge(s["ln_ready"], b + 1)
                nc.vector.tensor_scalar(ln1p, ln1p, -LOG_SMALL, 0.0, ALU.add, ALU.max).then_inc(s["large_ready"], 1)
                dve.wait_ge(s["large_ready"], b + 1)
                dve.wait_ge(s["relu_ready"], b + 1)
                nc.vector.tensor_tensor(pos_part, pos_part, ln1p, ALU.add).then_inc(s["sum_ready"], 1)
                dve.wait_ge(s["square_ready"], b + 1)
                dve.wait_ge(s["small_ready"], b + 1)
                nc.vector.scalar_tensor_tensor(fit, fit, SQ_REST, small, ALU.add, ALU.mult).then_inc(s["fit_ready"], 1)
                dve.wait_ge(s["fit_ready"], b + 1)
                dve.wait_ge(s["sum_ready"], b + 1)
                nc.vector.tensor_tensor(pos_part, pos_part, fit, ALU.add).then_inc(s["delta_ready"], 1)
                dve.wait_ge(s["part2_ready"], b + 1)
                dve.wait_ge(s["rest_ready"], b + 1)
                wait(dve, s["parts_out"], 16 * b)
                nc.vector.scalar_tensor_tensor(parts_p[0:BR], part2[0:BR], consts[0:BR, C_PART + 1:C_PART + 2], rest[0:BR],
                                               ALU.mult, ALU.add).then_inc(s["parts_ready"], 1)
                if not last_but(1):
                    dve.wait_ge(s["parts_ready"], BATCH)
                    for r in range(DA_RING):
                        at = 0 if r % DH < NH else L - 1
                        last = nc.vector.memset(decay[:, r, :, at:at + 1], 0.0)
                    last.then_inc(s["decay_free"], 1)
                dve.wait_ge(s["delta_ready"], b + 1)
                dve.wait_ge(s["u_ready"], ND * b + ND)
                wait(dve, s["du_out"], 16 * b)
                nc.vector.tensor_tensor(du_p, pos_part, u, ALU.mult).then_inc(s["du_ready"], 1)

            start = done[0]
            for g in range(2):
                residual(g)
            copy_x(1)
            residual(2)
            convolve(0)
            gate_z(0)
            for g in range(3, BATCH):
                residual(g)
            dve.wait_ge(s["base_sb"], BATCH)
            nc.vector.memset(parts_p[BR:P], 0.0)
            prepare(0)
            with dve.Fori(1, BATCH - 2) as b:
                prepare(b)
            for b in range(BATCH - 2, BATCH):
                prepare(b)

            for n in ("gate_out", "c_out", "parts_out", "delta_out"):
                dve.wait_ge(s[n], 16 * BATCH)
            dve.wait_ge(s["scattered"], 16 * NT * TOPK)
            dve.wait_ge(s["skip_sb"], BATCH)
            dve.wait_ge(s["du_ready"], BATCH)
            dve.sem_inc(s["prepared"], 1)

            def gate_batch(b, par, i):
                dve.wait_ge(s[f"late_in{par}"], 80 * i + 80)
                for h in range(NH):
                    dve.wait_ge(s["summed"], PAIRS * b + PAIRS - NH + h + 1)
                    nc.vector.tensor_tensor(gated[:, h], y_ps[:, h, :].rearrange("p (t c) -> p t c", t=TPB), skip[:, par, h],
                                            ALU.add).then_inc(s["y_free"], 1)
                for h in range(NH):
                    dve.wait_ge(s["y_free"], NH * b + h + 1)
                    nc.vector.tensor_tensor(gated[:, h], gated[:, h], gate[:, par, h], ALU.mult).then_inc(s["gated_ready"], 1)

            def mix_batch(b, par):
                bank_written(dve, s, b + 1, "O", 0, 1)
                wait(dve, s["mixed_out"], 16 * b)
                nc.vector.tensor_tensor(mixed[:, :], m_ps[1], base[:, par, :], ALU.add).then_inc(s["m1_free"], 1)

            def batch(b, par, i):
                first = isinstance(b, int) and b == 0
                dve.wait_ge(s[f"early_in{par}"], 48 * i + 48)

                def dbx(tau):
                    dve.wait_ge(s["b_ready"], DECAYS * b + tau + 1)
                    bank = b_ps[:, tau % B_RING, :]
                    nc.vector.tensor_tensor(bank, du[:, par, tau // 2 % DH, :], bank, ALU.mult).then_inc(s["dbx_done"], 1)

                dbx(0)
                for q in range(PAIRS):
                    if q == GATE_STEP and not first:
                        gate_batch(b - 1, 1 - par, i if par else i - 1)
                    if q == MIX_STEP and not first:
                        mix_batch(b - 1, 1 - par)
                    for j in range(2):
                        tau = 2 * q + j
                        if tau + 1 < DECAYS:
                            dbx(tau + 1)
                        if j == 0:
                            wait(dve, s["summed"], PAIRS * b + q - H_RING + 1)
                        dve.wait_ge(s["decay_ready"], DECAYS * b + tau + 1)
                        dve.wait_ge(s["dbx_done"], DECAYS * b + tau + 1)
                        way = slice(None) if q % DH < NH else slice(None, None, -1)
                        nc.vector.tensor_tensor_scan(state[:, q % H_RING, j, way], decay[:, q % DA_RING, j, way],
                                                     b_ps[:, tau % B_RING, way], 0.0, ALU.mult, ALU.add).then_inc(s["scan_done"], 1)

            batch(0, 0, 0)
            batch(1, 1, 0)
            with dve.Fori(1, BATCH // 2) as i:
                batch(2 * i, 0, i)
                batch(2 * i + 1, 1, i)
            gate_batch(BATCH - 1, 1, BATCH // 2 - 1)
            mix_batch(BATCH - 1, 1)
            dve.wait_ge(s["acc_in"], 16)
            for t in range(NT):
                dve.wait_ge(y_in[t % Y_RING], 16 * TOPK * (t // Y_RING + 1))
                for k in range(TOPK):
                    ins = nc.vector.scalar_tensor_tensor(acc[:, t * D:(t + 1) * D], y_tok[:, (t % Y_RING) * TOPK + k, :],
                                                         gates[:, t, k:k + 1], acc[:, t * D:(t + 1) * D], ALU.mult, ALU.add)
                    if k < TOPK - 1:
                        ins.then_inc(s["f_chain"], 1)
                        dve.wait_ge(s["f_chain"], (TOPK - 1) * t + k + 1)
                    else:
                        ins.then_inc(s["acc_ready"], 1)


def kernel(**inputs):
    import numpy as np
    import concourse.bacc as bacc
    from concourse.bass_utils import run_bass_kernel_spmd

    a = {k[3:]: np.asarray(v) for k, v in inputs.items()}
    f = lambda n: a["attn_" + n]

    def by_channel(m):
        return np.stack([w.reshape(NH, P, -1) for w in m]).transpose(2, 0, 1, 3).reshape(P, DH, -1)

    consts = np.zeros((P, C_END), np.float32)
    p = np.arange(P)
    consts[:, C_ID:C_ID + P] = np.eye(P)
    consts[:, C_TRI:C_TRI + P] = p[:, None] < p[None, :]
    consts[:, C_IOTA:C_IOTA + E] = np.arange(E)
    consts[:, C_THR:C_THR + E] = S * np.arange(E)
    consts[:, C_TILE:C_TILE + NTILE] = np.arange(NTILE)
    consts[:, C_MASK:C_MASK + NT * E] = np.tile(np.arange(NT) > 0, E)
    consts[:, C_PART] = -1.0 * (p >= BR // 3)
    consts[:, C_PART + 1] = -1.0 * (p >= 2 * BR // 3)
    sel = (p[:, None] % (2 * NS) == np.arange(NS)[None, :]) & (p[:, None] < BR)
    consts[:, C_SEL:C_END] = np.repeat(sel, P, axis=1)

    chan = np.concatenate([by_channel([f("conv_w")[:, 0], f("convb_w")[:, 0]]),
                           by_channel([f("conv_bias"), f("convb_bias")]),
                           by_channel([f("dt_proj_bias"), f("dt_proj_b_bias")]),
                           by_channel([f("D_skip"), f("D_b_skip")]),
                           by_channel([f("A_log"), f("A_b_log")])], axis=2)
    xproj = []
    for w in (f("x_proj_w"), f("x_proj_b_w")):
        rows = np.concatenate([w[NR:]] * 3 + [w[:NR]])
        xproj.append(rows.T.reshape(NH, P, BR + NR).transpose(1, 0, 2))
    w1 = a["ffn_w1"].transpose(0, 2, 1)
    b1 = a["ffn_b1"].reshape(E, FC, P).transpose(0, 2, 1)
    arrays = {
        "x": f("hidden_states").reshape(TOK, D),
        "consts": consts,
        "chan": chan,
        "in_w": f("in_proj_w").T,
        "xproj": np.stack(xproj, axis=1),
        "dt_w": np.stack([f("dt_proj_w").T, f("dt_proj_b_w").T], axis=1),
        "out_w": f("out_proj_w").T.reshape(NH, P, D).transpose(1, 0, 2),
        "route": np.concatenate([a["ffn_keys"].T, a["ffn_rw"].T, np.broadcast_to(a["ffn_rb"], (P, E))], axis=1),
        "b2": a["ffn_b2"],
        "w1": np.concatenate([w1, b1], axis=2),
        "w2": a["ffn_w2"].transpose(0, 2, 1).reshape(E, FC, P, D).transpose(0, 2, 1, 3).reshape(E, P, FC * D),
    }
    arrays = {k: np.ascontiguousarray(v) for k, v in arrays.items()}
    nc = bacc.Bacc("TRN2", target_bir_lowering=False, num_devices=1)
    aps = [nc.dram_tensor(k + "_dram", v.shape, mybir.dt.from_np(v.dtype), kind="ExternalInput").ap()
           for k, v in arrays.items()]
    out = nc.dram_tensor("out_dram", (TOK, D), F32, kind="ExternalOutput").ap()
    build_kernel(nc, *aps, out)
    r = run_bass_kernel_spmd(nc, [{k + "_dram": v for k, v in arrays.items()}], core_ids=[0])
    return r.results[0]["out_dram"].reshape(BATCH, L, D)
```

```python
import numpy as np
import concourse.bass as bass
from concourse import mybir
from contextlib import ExitStack

F32 = mybir.dt.float32
BF16 = mybir.dt.bfloat16
I32 = mybir.dt.int32
U32 = mybir.dt.uint32
ALU = mybir.AluOpType
ACT = mybir.ActivationFunctionType
AXX = mybir.AxisListType.X

P = 128
D = 128
BATCH, L = 8, 512
TOK = BATCH * L
NT = TOK // P
TPB = L // P
DIN = 256
NH = DIN // P
ND = 2
DH = ND * NH
NS = 16
NR = 8
KC = 4
E, TOPK = 16, 4
FF = 512
FC = FF // P
S = 256
SH = S // P
NTILE = TOK * TOPK // S + E
NSLOT = NTILE * S
MPB = NTILE // BATCH
EPS = 1e-5
CH = KC + 3 + NS
BR = 96
W1W = FF + FC

C_ID, C_TRI, C_IOTA, C_THR, C_TILE = 0, 128, 256, 272, 288
C_MASK = C_TILE + NTILE
C_PART = C_MASK + NT * E
C_DEST = C_PART + 2
C_UNUSED = C_DEST + NT
C_SEL = C_UNUSED + MPB * SH
C_END = C_SEL + NS * P

PAIRS = NS // 2 * DH
DA_RING = 8
H_RING = 8
B_RING = 4
C_RING = 4
CPB = NS // 2 * ND
W_RING = 2
VECTOR_PAIRS = (14, 26)
DECAYS = 2 * PAIRS

SUM_LAG = 4
SUM_STEP = [k + SUM_LAG for k in range(PAIRS)]
SUMS = [[k for k in range(PAIRS) if SUM_STEP[k] == q] for q in range(PAIRS)]
SUMS_AFTER = [[k for k in range(PAIRS) if SUM_STEP[k] == PAIRS + q] for q in range(PAIRS)]

GROUP = MPB // 2
T_STEP = [0, 3, 6, 9, 12, 17, 20, 23, 26, 29]
EVENTS = [[] for _ in range(PAIRS)]
for _j, _q in enumerate(T_STEP):
    EVENTS[_q].append(("T", _j, 0, False))
    EVENTS[_q + 1].append(("D", (_j + GROUP) % MPB, 1, _j < GROUP))
    EVENTS[_q + 2] += [("U0", _j, 1, False), ("U1", _j, 0, False)]
EVENTS[15] += [("G", 0, 0, True), ("G", 1, 1, True)]
EVENTS[16].append(("O", 0, 1, True))
GATE_STEP, MIX_STEP = 3, 16

EMPTY_LAG = 6
HALF = PAIRS // 2
GELU_STEP = [HALF - 1 + EMPTY_LAG, 2 * HALF - 1 + EMPTY_LAG - PAIRS]
BURST_STEPS = [[HALF, HALF + 1], [0, 1]]
EMPTY_STEP = [q + (EMPTY_LAG - 1 - q % HALF if q % HALF < 2 else EMPTY_LAG - 2 if q % HALF < 6 else
                   EMPTY_LAG - 1 if q % HALF < 9 else EMPTY_LAG) for q in range(PAIRS)]
EMPTY = [[p for p in range(PAIRS) if EMPTY_STEP[p] == q and p % HALF > 1] for q in range(PAIRS)]
EMPTY_AFTER = [[p for p in range(PAIRS) if EMPTY_STEP[p] == PAIRS + q and p % HALF > 1] for q in range(PAIRS)]


def events(b, q):
    if isinstance(b, int) and b in (0, BATCH):
        return [e for e in EVENTS[q] if e[3] == (b == BATCH)]
    return EVENTS[q]


def uses(b, m, what, j):
    n = 0
    for q in range(PAIRS):
        for e in events(b, q):
            if e[:2] == (what, j):
                return uses_before(b, m) + n
            n += e[2] == m
    raise ValueError(what)


def uses_before(b, m):
    if isinstance(b, int) and b == 0:
        return 0
    return sum(e[2] == m for q in EVENTS for e in q) * b - sum(e[2] == m and e[3] for q in EVENTS for e in q)


def tiles_before(b, before):
    return MPB * (b - 1) if before else MPB * b


UNUSED = MPB * S
RW = D + 1
ZEROS = 2 * DH * L
FILL = [(at, min(ZEROS, NSLOT * RW // P - at)) for at in range(0, NSLOT * RW // P, ZEROS)]
ZERO_DMAS = len(FILL)
WTS_DMAS = 6
XQ = 4
DEST_LAG = 1
DT_BANKS = (0, 1, 6, 7)
EXP_LN_SET = 6

SMALL = 1 / 32
LOG_SMALL = float(np.log1p(SMALL))
_nodes = SMALL / 2 * (1 + np.cos(np.pi * (2 * np.arange(3) + 1) / 6))
_c2, _c1, _c0 = (float(c) for c in np.polyfit(_nodes, np.log1p(_nodes) / _nodes, 2))
SQ_SCALE = float(np.sqrt(_c2))
SQ_BIAS = _c1 / (2 * SQ_SCALE)
SQ_REST = _c0 - SQ_BIAS ** 2
PREP_STORES = ("gate_out", "c_out", "parts_out", "skip_out", "delta_out", "du_out")


def wait(eng, semaphore, value):
    if not isinstance(value, int) or value > 0:
        eng.wait_ge(semaphore, value)


def bank_written(eng, sems, b, what, j, m):
    wait(eng, sems[f"m{m}_ready"], uses(b, m, what, j) + 1)


def bank_empty(eng, sems, b, what, j, m):
    wait(eng, sems[f"m{m}_free"], uses(b, m, what, j))


def bank_emptied(eng, sems, b, what, j, m):
    wait(eng, sems[f"m{m}_free"], uses(b, m, what, j) + 1)


def build_kernel(nc, x_in, consts_in, chan_in, inw_in, xproj_in, dtw_in, outw_in,
                 route_in, b2_in, w1_in, w2_in, out):
    with ExitStack() as ctx:
        def sb(name, shape, dt=F32):
            return ctx.enter_context(nc.sbuf_tensor(name, shape, dt))

        def sem(name):
            return ctx.enter_context(nc.semaphore(name))

        def dram(name, shape, dt=F32):
            return nc.dram_tensor(name, shape, dt, kind="Internal").ap()

        delta_d = dram("delta_d", (BATCH, P, DH * L))
        du_d = dram("du_d", (BATCH, P, DH * L))
        gate_d = dram("gate_d", (BATCH, P, TPB * DIN))
        skip_d = dram("skip_d", (BATCH, P, TPB * DIN))
        parts_d = dram("parts_d", (BATCH, P, ND * L), BF16)
        c_d = dram("c_d", (BATCH, ND, NS, L))
        base_d = dram("base_d", (BATCH, P, TPB * D))
        mixed_d = dram("mixed_d", (BATCH, P, TPB * D))
        slots_d = dram("slots_d", (NSLOT, RW))
        chosen_d = dram("chosen_d", (UNUSED + TOK * TOPK, D))

        ident = sb("ident", [P, P])
        sel = sb("sel", [P, NS, P], BF16)
        chan = sb("chan", [P, DH, CH])
        half_taps = sb("half_taps", [P, DH, KC + 1])
        a_neg = sb("a_neg", [P, DH, NS])
        outw = sb("outw", [P, NH, D])
        pos = sb("pos", [P, NT * TOPK], I32)
        gates = sb("gates", [P, NT, TOPK])
        fit_bias = sb("fit_bias", [P, 1])
        tile_expert = sb("tile_expert", [P, NTILE], I32)

        delta = sb("delta", [P, 2, DH, L])
        du = sb("du", [P, 2, DH, L])
        gate = sb("gate", [P, 2, NH, TPB, P])
        skip = sb("skip", [P, 2, NH, TPB, P])
        base = sb("base", [P, 2, TPB * D])
        parts = sb("parts", [P, 2, ND, L], BF16)
        gated = sb("gated", [P, NH, TPB, P])
        gatedT = sb("gatedT", [P, NH, L])
        w1 = sb("w1", [P, W_RING, W1W])
        w2 = sb("w2", [P, W_RING, FC, D])
        rows = sb("rows", [P, W_RING, SH, RW])
        dest = sb("dest", [P, MPB, SH], I32)
        unused = sb("unused", [P, MPB, SH])
        rowsT = sb("rowsT", [P, S])
        yrows = sb("yrows", [P, W_RING, SH, D])
        mixed = sb("mixed", [P, TPB * D])

        ARENA = 30720
        arena = sb("arena", [P, ARENA])
        top = [0]

        def carve(n):
            at = top[0]
            top[0] += n
            assert top[0] <= ARENA, top[0]
            return arena[:, at:at + n]

        decay = carve(DA_RING * 2 * L).rearrange("p (r j l) -> p r j l", r=DA_RING, j=2)
        state = carve(H_RING * 2 * L).rearrange("p (r j l) -> p r j l", r=H_RING, j=2)
        c_rows = carve(C_RING * 2 * L).rearrange("p (r j l) -> p r j l", r=C_RING, j=2)
        hidden = carve(MPB * FC * S).rearrange("p (t f s) -> p t f s", t=MPB, f=FC)
        acc = state.rearrange("p r j l -> p (r j l)")[:, 0:TOK * D // P]
        Y_GROUP = TPB * TOPK * D
        y_tok = [ring[:, k * Y_GROUP:(k + 1) * Y_GROUP].rearrange("p (t k d) -> p t k d", t=TPB, k=TOPK)
                 for ring in (decay.rearrange("p r j l -> p (r j l)"), hidden.rearrange("p t f s -> p (t f s)"))
                 for k in range(BATCH // 2)]
        top[0] = 0
        consts = carve(C_END)
        xnT = carve(TOK)
        inw = carve(2 * DIN)
        xproj = carve(ND * NH * (BR + NR)).rearrange("p (d h m) -> p d h m", d=ND, h=NH)
        dtw = carve(ND * DIN).rearrange("p (d c) -> p d c", d=ND)
        diag = carve(DH * P).rearrange("p (q m) -> p q m", q=DH)
        keys_sq = carve(E)
        route_w = carve(E)
        route_b = carve(E)
        route = carve(4 * E)
        b2 = carve(D)
        xn = carve(NT * RW).rearrange("p (t d) -> p t d", t=NT)
        shared = top[0]
        x_all = carve(NT * D).rearrange("p (t d) -> p t d", t=NT)
        stats = carve(NT * 6).rearrange("p (t s) -> p t s", t=NT)
        mv = carve(NT * 2).rearrange("p (t s) -> p t s", t=NT)
        var_eps = carve(NT)
        std = carve(NT)
        rstd = carve(NT)
        logits = carve(NT * E)
        top8 = carve(NT * 8).rearrange("p (t k) -> p t k", t=NT)
        idx8 = carve(NT * 8).bitcast(U32).rearrange("p (t k) -> p t k", t=NT)
        idxf = carve(NT * TOPK)
        onehot = carve(NT * TOPK * E)
        product = carve(NT * TOPK * E)
        chosen = carve(NT * E // 2).bitcast(BF16)
        tri = carve(P // 2).bitcast(BF16)
        ones_b = carve(P // 2).bitcast(BF16)
        ones_f = carve(P)
        totals = carve(NT * E).rearrange("p (e t) -> p e t", e=E)
        upto = carve(NT * E).rearrange("p (e t) -> p e t", e=E)
        place = carve(NT * E)
        n_tiles = carve(E)
        end_tile = carve(E)
        slot0 = carve(E)
        compare = carve(E * NTILE)
        posf = carve(NT * TOPK)
        texp = carve(NTILE)
        gexp = carve(NT * TOPK)
        gsum = carve(NT)
        grec = carve(NT)
        mix_w = carve(NT * E)
        mix_wT = carve(2 * TPB * P).rearrange("p (a n) -> p a n", a=2)
        base_lo, base_hi = (ap.rearrange("p a h t c -> p (a h t c)").rearrange("p (b n) -> p b n", b=BATCH // 2)
                            for ap in (gate[:, :, :, :, :], skip[:, :, :, :, :]))
        routing_end = top[0]
        top[0] = shared
        PADL = L + 2 * (KC - 1)
        by_q = lambda ap: ap.rearrange("p (q l) -> p q l", q=DH)
        by_d = lambda ap: ap.rearrange("p (d l) -> p d l", d=ND)
        mag = by_q(carve(DH * L))
        pos_part = by_q(carve(DH * L))
        xpad = carve(NH * PADL).rearrange("p (h l) -> p h l", h=NH)
        v = by_q(carve(DH * L))
        th = by_q(carve(DH * L))
        u = by_q(carve(DH * L))
        xdbl = by_d(carve(ND * L))
        rest = by_d(carve(ND * L))
        part1 = by_d(carve(ND * L // 2).bitcast(BF16))
        part2 = by_d(carve(ND * L // 2).bitcast(BF16))
        parts_p = by_d(carve(ND * L // 2).bitcast(BF16))
        fit = by_q(carve(DH * L))
        ln1p = by_q(consts[:, C_SEL:C_END])
        small, du_p = du[:, 1], delta[:, 1]
        xb = mixed[:, :]
        zhalf = w2[:, :, :, :].rearrange("p r f d -> p (r f d)").rearrange("p (t c) -> p t c", t=TPB)
        zth = w1[:, :, :].rearrange("p r n -> p (r n)")[:, 0:TPB * DIN].rearrange("p (t c) -> p t c", t=TPB)
        skip_p = gatedT[:, :, :].rearrange("p h l -> p (h l)").rearrange("p (t c) -> p t c", t=TPB)
        prep_end = top[0]

        ps = ctx.enter_context(nc.psum_tensor("ps", [P, 8, 512], F32))
        b_ps = ps[:, 0:B_RING, :]
        y_ps = ps[:, 4:6, :]
        m_ps = [ps[:, 6, :], ps[:, 7, :]]

        names = """consts_in route_in wts_in a_exp zero_v slots_zeroed var_ready std_ready xn_ready xnT_ps xnT_ready
            kw_ready logit_ps keys_ps chosen_ready rank_ps pos_ready gdiff_ready gexp_ready mix_ready
            mixT_ps mixT_sb base_ps base_sb base_out scattered v_chain
            xb_ready xz_ps xpad_ready z_ps z_sb v_ready th_ready u_ready gate_ready xd_ps xd_sb
            part1_ready rest_ready part2_ready parts_ready dt_ps mag_ready
            small_ready square_ready exp_ready relu_ready
            sum_ready fit_ready delta_ready du_ready skip_ps skip_sb gate_out c_out parts_out skip_out delta_out du_out decay_free prepared
            early_in0 early_in1 late_in0 late_in1 decay_ready b_ready dbx_done scan_done prod_done v_prod_done dest_free dest_saved summed
            y_free gated_ready m0_ready m0_free m1_ready m1_free gelu_done
            mixed_out sp_step pool_step f_chain acc_in acc_ready out_done"""
        s = {n: sem(n) for n in names.split()}
        x_loaded = [sem(f"x_in{i}") for i in range(XQ)]
        c_in = [sem(f"c_in{i}") for i in range(C_RING)]
        w1_in_s = [sem(f"w1_in{i}") for i in range(W_RING)]
        w2_in_s = [sem(f"w2_in{i}") for i in range(W_RING)]
        rows_in = [sem(f"rows_in{i}") for i in range(W_RING)]
        y_out = [sem(f"y_out{i}") for i in range(W_RING)]
        y_in = [sem(f"y_in{i}") for i in range(BATCH)]

        block = ctx.enter_context(nc.Block())

        def bc(ap, shape):
            return ap.to_broadcast(shape)

        def product_done(eng, b, q):
            mine = q in VECTOR_PAIRS
            n = sum(k <= q and (k in VECTOR_PAIRS) == mine for k in range(PAIRS))
            per = len(VECTOR_PAIRS) if mine else PAIRS - len(VECTOR_PAIRS)
            eng.wait_ge(s["v_prod_done" if mine else "prod_done"], per * b + n)

        @block.sync
        def _(sp):
            sp.dma_start(consts[:, 0:C_SEL], consts_in[:, 0:C_SEL]).then_inc(s["consts_in"], 16)
            for k in range(XQ):
                own = slice(k * NT // XQ, (k + 1) * NT // XQ)
                sp.dma_start(x_all[:, own], x_in.rearrange("(t p) d -> p t d", p=P)[:, own]).then_inc(x_loaded[k], 16)
                if k == 0:
                    for dst, src in ((route[:, 0:3 * E], route_in), (b2[0:E, :], b2_in)):
                        sp.dma_start(dst, src).then_inc(s["route_in"], 16)
            for dst, src in ((chan[:, :, :], chan_in), (inw, inw_in), (xproj, xproj_in), (dtw[BR:BR + NR], dtw_in),
                             (outw[:, :, :], outw_in), (consts[:, C_SEL:C_END], consts_in[:, C_SEL:C_END])):
                sp.dma_start(dst, src).then_inc(s["wts_in"], 16)
            sp.wait_ge(s["zero_v"], 1)
            zeros = delta[:, :, :, :].rearrange("p a q l -> p (a q l)")
            fill = slots_d.rearrange("s d -> (s d)").rearrange("(p n) -> p n", p=P)
            for at, n in FILL:
                sp.dma_start(fill[:, at:at + n], zeros[:, 0:n]).then_inc(s["slots_zeroed"], 16)

            def one(t, b):
                return t[bass.ds(b, 1)].rearrange("e p n -> (e p) n")

            for k, held in enumerate((base_lo, base_hi)):
                half = slice(k * BATCH // 2, (k + 1) * BATCH // 2)
                sp.wait_ge(s["base_sb"], (k + 1) * BATCH // 2)
                sp.dma_start(base_d[half].rearrange("b p n -> p b n"), held).then_inc(s["base_out"], 16)

            def early_reads(par):
                return ((delta[:, par, :, :].rearrange("p q l -> p (q l)"), delta_d),
                        (du[:, par, :, :].rearrange("p q l -> p (q l)"), du_d),
                        (parts[:, par, :, :].rearrange("p d l -> p (d l)"), parts_d))

            def read_early(b, par, k):
                dst, src = early_reads(par)[k]
                sp.dma_start(dst, one(src, b)).then_inc(s[f"early_in{par}"], 16)

            def read_late(b, par, k):
                if k < 2 * NH:
                    dst, src = ((gate, gate_d), (skip, skip_d))[k % 2]
                    sp.dma_start(dst[:, par, k // 2, :, :], src[bass.ds(b, 1)].rearrange("e p (t h c) -> (e p) h t c", t=TPB, h=NH)[:, k // 2])\
                        .then_inc(s[f"late_in{par}"], 16)
                else:
                    sp.dma_start(base[:, par, :], one(base_d, b)).then_inc(s[f"late_in{par}"], 16)

            def expert_of(tile):
                return sp.value_load(tile_expert[0:1, bass.ds(tile, 1)], min_val=0, max_val=E - 1)

            def read_up(tile, slot):
                e = expert_of(tile)
                sp.dma_start(w1[:, slot, :], w1_in[bass.ds(e, 1)].rearrange("e p n -> (e p) n")).then_inc(w1_in_s[slot], 16)
                sp.dma_start(rows[:, slot, :, :],
                             slots_d.rearrange("(t a p) d -> t p a d", a=SH, p=P)[bass.ds(tile, 1)]
                             .rearrange("t p a d -> (t p) a d")).then_inc(rows_in[slot], 16)

            def read_down(tile, slot):
                e = expert_of(tile)
                sp.dma_start(w2[:, slot, :, :].rearrange("p f d -> p (f d)"),
                             w2_in[bass.ds(e, 1)].rearrange("e p n -> (e p) n")).then_inc(w2_in_s[slot], 16)

            def read_ahead():
                for n in PREP_STORES:
                    sp.wait_ge(s[n], 16)
                sp.wait_ge(s["slots_zeroed"], 16 * ZERO_DMAS)
                sp.wait_ge(s["base_out"], 32)
                for k in range(3):
                    read_early(0, 0, k)
                sp.wait_ge(s["scattered"], 16 * NT * TOPK)
                sp.wait_ge(s["gate_out"], 16 * BATCH)
                for j in range(W_RING):
                    read_up(j, j)
                    read_down(j, j)
                for k in range(2 * NH + 1):
                    read_late(0, 0, k)

            def store(b, dst, src, ready, stored, per=1):
                sp.wait_ge(s[ready], per * b + per)
                sp.sem_inc(s["sp_step"], 1)
                sp.dma_start(one(dst, b), src).then_inc(s[stored], 16)

            def store_gate(b):
                store(b, gate_d, zth.rearrange("p t c -> p (t c)"), "gate_ready", "gate_out")

            def store_prepared(b):
                sp.wait_ge(s["xd_sb"], ND * b + ND)
                sp.sem_inc(s["sp_step"], 1)
                sp.dma_start(c_d[bass.ds(b, 1)].rearrange("e d n l -> n (e d) l"),
                             xdbl[NS:2 * NS]).then_inc(s["c_out"], 16)
                if not isinstance(b, int) or b < BATCH - 1:
                    store_gate(b + 1)
                store(b, skip_d, skip_p.rearrange("p t c -> p (t c)"), "skip_sb", "skip_out")
                store(b, delta_d, pos_part.rearrange("p q l -> p (q l)"), "delta_ready", "delta_out", ND)
                store(b, parts_d, parts_p.rearrange("p d l -> p (d l)"), "parts_ready", "parts_out")
                store(b, du_d, du_p.rearrange("p q l -> p (q l)"), "du_ready", "du_out", ND)

            store_gate(0)
            store_prepared(0)
            with sp.Fori(1, BATCH - 2) as b:
                store_prepared(b)
            store_prepared(BATCH - 2)
            read_ahead()
            store_prepared(BATCH - 1)
            sp.wait_ge(s["prepared"], 1)
            sp.wait_ge(s["du_out"], 16 * BATCH)
            sp.wait_ge(s["skip_out"], 16 * BATCH)

            def read_c(b, r):
                g, d = r // ND, r % ND
                src = c_d[bass.ds(b, 1), d, 2 * g:2 * g + 2, :].rearrange("e j l -> e (j l)")
                sp.dma_start(c_rows[:, r % C_RING, :, :].rearrange("p j l -> p (j l)"),
                             src.to_broadcast([P, 2 * L])).then_inc(c_in[r % C_RING], 16)

            def batch(b, par):
                first = isinstance(b, int) and b == 0
                nxt = (b + 1) % BATCH
                todo = []

                def early():
                    wait(sp, s["decay_ready"], DECAYS * b)
                    wait(sp, s["dbx_done"], DECAYS * b)
                    wait(sp, s["b_ready"], DECAYS * b)
                    sp.sem_inc(s["sp_step"], 1)
                    read_early(nxt, 1 - par, 2)
                todo.append((0.5, early))
                for k in range(2):
                    todo.append((4.4 + 6 * k, lambda k=k: read_early(nxt, 1 - par, k)))

                for k in range(2 * NH + 1):
                    todo.append((18.4 + 2 * k, lambda k=k: read_late(nxt, 1 - par, k)))
                for r in range(CPB):
                    def c(r=r):
                        for q in range(NH * r, NH * r + NH):
                            product_done(sp, b, q)
                            sp.sem_inc(s["sp_step"], 1)
                        sp.sem_inc(s["sp_step"], 1)
                        rn = r + C_RING
                        read_c(b if rn < CPB else nxt, rn % CPB)
                    todo.append((2 * r + 3, c))
                todo += tile_traffic(b)
                for _, f in sorted(todo, key=lambda x: x[0]):
                    f()

            def tile_traffic(b):
                todo = []
                for q in range(PAIRS):
                    for what, j, m, before in events(b, q):
                        tiles = tiles_before(b, before)

                        def up(j=j, m=m, tiles=tiles):
                            bank_emptied(sp, s, b, "U1", j, m)
                            sp.sem_inc(s["sp_step"], 1)
                            sp.wait_ge(s["dest_saved"], tiles + j + 1)
                            sp.sem_inc(s["sp_step"], 1)
                            read_up((tiles + j + W_RING) % NTILE, j % W_RING)

                        def down(j=j, m=m, tiles=tiles):
                            bank_written(sp, s, b, "D", j, m)
                            sp.sem_inc(s["sp_step"], 1)
                            read_down((tiles + j + W_RING) % NTILE, j % W_RING)

                        def mix(m=m):
                            bank_emptied(sp, s, b, "O", 0, m)
                            sp.sem_inc(s["sp_step"], 1)
                            sp.dma_start(one(mixed_d, b - 1), mixed[:, :]).then_inc(s["mixed_out"], 16)

                        if what == "U1":
                            todo.append((q + 1.5, up))
                        elif what == "D":
                            todo.append((q + 1.2, down))
                        elif what == "O" and not (isinstance(b, int) and b == BATCH):
                            todo.append((q + 1.8, mix))
                return todo

            for r in range(C_RING):
                read_c(0, r)
            batch(0, 0)
            batch(1, 1)
            with sp.Fori(1, BATCH // 2) as i:
                batch(2 * i, 0)
                batch(2 * i + 1, 1)
            sp.wait_ge(s["mixed_out"], 16 * (BATCH - 1))
            sp.wait_ge(s["summed"], PAIRS * BATCH)
            sp.dma_start(acc[:, 0:(BATCH - 1) * TPB * D].rearrange("p (b n) -> p b n", b=BATCH - 1),
                         mixed_d[0:BATCH - 1].rearrange("b p n -> p b n")).then_inc(s["acc_in"], 16)
            for _, f in tile_traffic(BATCH):
                f()
            for i in range(W_RING):
                sp.wait_ge(y_out[i], 16 * SH * (NTILE // W_RING))
            for g in range(BATCH):
                sp.dma_start(y_tok[g], chosen_d[UNUSED:UNUSED + TOK * TOPK].rearrange("(g t p k) d -> g p t (k d)", g=BATCH, p=P, k=TOPK)[g]
                             .rearrange("p t (k d) -> p t k d", k=TOPK)).then_inc(y_in[g], 16)
            for b in range(BATCH):
                sp.wait_ge(s["acc_ready"], TPB * (b + 1))
                sp.dma_start(out.rearrange("(t p) d -> p t d", p=P)[:, TPB * b:TPB * (b + 1), :],
                             acc[:, TPB * b * D:TPB * (b + 1) * D].rearrange("p (t d) -> p t d", t=TPB))\
                    .then_inc(s["out_done"], 16)
            sp.wait_ge(s["out_done"], 16 * BATCH)
            for par in range(2):
                sp.wait_ge(s[f"early_in{par}"], 16 * 3 * (BATCH // 2 + (1 - par)))
                sp.wait_ge(s[f"late_in{par}"], 16 * 5 * (BATCH // 2 + (1 - par)))
            for i in range(C_RING):
                sp.wait_ge(c_in[i], 16 * (BATCH * CPB // C_RING + 1))
            for i in range(W_RING):
                sp.wait_ge(w1_in_s[i], 16 * (NTILE // W_RING + 1))
                sp.wait_ge(w2_in_s[i], 16 * (NTILE // W_RING + 1))
                sp.wait_ge(rows_in[i], 16 * (NTILE // W_RING + 1))

        @block.gpsimd
        def _(pool):
            nc.gpsimd.memset(delta[:, :, :, :], 0.0).then_inc(s["zero_v"], 1)
            pool.wait_ge(s["slots_zeroed"], 16 * ZERO_DMAS)
            pool.wait_ge(s["xn_ready"], NT)
            pool.wait_ge(s["pos_ready"], 1)
            for k in range(TOPK):
                wait(pool, s["scattered"], 16 * NT * k)
                nc.gpsimd.tensor_scalar(xn[:, :, D], consts[:, C_DEST:C_DEST + NT], float(k), None, ALU.add).then_inc(s["dest_free"], 1)
                pool.wait_ge(s["dest_free"], k + 1)
                for t in range(NT):
                    pool.indirect_dma_start(slots_d, bass.IndirectOffsetOnAxis(
                        ap=pos[:, t * TOPK + k:t * TOPK + k + 1], axis=0), xn[:, t, :], None).then_inc(s["scattered"], 16)
            pool.wait_ge(s["prepared"], 1)

            def send(b, before, j, m):
                bank_emptied(pool, s, b, "D", j, m)
                pool.sem_inc(s["pool_step"], 1)
                pool.wait_ge(s["dest_saved"], MPB * (b - before) + j + 1)
                pool.sem_inc(s["pool_step"], 1)
                for a in range(SH):
                    pool.indirect_dma_start(chosen_d, bass.IndirectOffsetOnAxis(ap=dest[:, j, a:a + 1], axis=0),
                                            yrows[:, j % W_RING, a, :], None).then_inc(y_out[j % W_RING], 16)

            def besides(b, q):
                if q >= DEST_LAG:
                    for what, j, m, before in events(b, q - DEST_LAG):
                        if what == "D":
                            send(b, before, j, m)

            def batch(b):
                for q in range(PAIRS):
                    r, h = q // NH, q % NH
                    if q not in VECTOR_PAIRS:
                        wait(pool, s["scan_done"], DECAYS * b + 2 * q + 2)
                        pool.wait_ge(c_in[r % C_RING], 16 * (CPB // C_RING * b + r // C_RING + 1))
                        nc.gpsimd.tensor_tensor(state[:, q % H_RING], state[:, q % H_RING], c_rows[:, r % C_RING],
                                                ALU.mult).then_inc(s["prod_done"], 1)
                    besides(b, q)

            batch(0)
            batch(1)
            with pool.Fori(1, BATCH // 2) as i:
                batch(2 * i)
                batch(2 * i + 1)
            for q in range(PAIRS):
                besides(BATCH, q)

        @block.scalar
        def _(act):
            per = NT // XQ
            for k in range(XQ + 1):
                if k < XQ:
                    act.wait_ge(s["var_ready"], k + 1)
                    nc.scalar.activation(std[:, k * per:(k + 1) * per], var_eps[:, k * per:(k + 1) * per], ACT.Sqrt)\
                        .then_inc(s["std_ready"], 1)
                if k > 0:
                    for g in range((k - 1) * per // TPB, k * per // TPB):
                        act.wait_ge(s["xnT_ps"], g + 1)
                        nc.scalar.copy(xnT[:, g * L:(g + 1) * L], ps[:, 2 + g % 4, :]).then_inc(s["xnT_ready"], 1)
            act.wait_ge(s["wts_in"], 16 * WTS_DMAS)
            nc.scalar.activation(a_neg[:, :, :], chan[:, :, KC + 3:CH], ACT.Exp).then_inc(s["a_exp"], 1)
            act.wait_ge(s["gdiff_ready"], 1)
            nc.scalar.activation(gexp, idxf, ACT.Exp).then_inc(s["gexp_ready"], 1)
            def take_projected(b):
                act.wait_ge(s["xz_ps"], b + 1)
                wait(act, s["v_ready"], b)
                nc.scalar.copy(xpad[:, :, KC - 1:KC - 1 + L], ps[:, 0:2, :]).then_inc(s["xpad_ready"], 1)
                act.wait_ge(s["z_ps"], b + 1)
                wait(act, s["gate_out"], 16 * b)
                z_ps = ps[:, 4:6, :].rearrange("p a n -> p (a n)")
                nc.scalar.mul(zhalf.rearrange("p t c -> p (t c)"), z_ps, 0.5)
                nc.scalar.activation(zth.rearrange("p t c -> p (t c)"), z_ps, ACT.Tanh, scale=0.5).then_inc(s["z_sb"], 1)

            def take_tanh(b):
                act.wait_ge(s["v_ready"], b + 1)
                nc.scalar.activation(th, v, ACT.Tanh).then_inc(s["th_ready"], 1)

            def prepare(b):
                last_but = lambda n: not isinstance(b, int) or b < BATCH - n
                wait(act, s["c_out"], 16 * b)
                for d in range(ND):
                    act.wait_ge(s["xd_ps"], ND * b + d + 1)
                    nc.scalar.copy(xdbl[0:BR + NR, d], ps[0:BR + NR, 4 + d, :]).then_inc(s["xd_sb"], 1)
                nc.scalar.copy(part1[0:BR], ps[0:BR, 4:6, :]).then_inc(s["part1_ready"], 1)
                wait(act, s["fit_ready"], ND * b)
                for q in range(DH):
                    act.wait_ge(s["dt_ps"], ND * b + q // NH + 1)
                    last = nc.scalar.activation(mag[:, q, :], ps[:, DT_BANKS[q], :], ACT.Abs, bias=chan[:, q, KC + 1:KC + 2])
                last.then_inc(s["mag_ready"], 1)
                nc.scalar.add_instruction(mybir.InstLoadActFuncSet(name=nc.get_next_instruction_name(), act_func_set_id=EXP_LN_SET))
                act.wait_ge(s["mag_ready"], b + 1)
                nc.scalar.activation(mag, mag, ACT.Exp, scale=-1.0).then_inc(s["exp_ready"], 1)
                act.wait_ge(s["rest_ready"], b + 1)
                nc.scalar.copy(part2[0:BR], rest[0:BR]).then_inc(s["part2_ready"], 1)
                act.wait_ge(s["exp_ready"], b + 1)
                nc.scalar.activation(ln1p, mag, ACT.Ln, bias=1.0)
                wait(act, s["delta_out"], 16 * b)
                for d in range(ND):
                    for q in range(d * NH, (d + 1) * NH):
                        last = nc.scalar.activation(pos_part[:, q, :], ps[:, DT_BANKS[q], :], ACT.Relu, bias=chan[:, q, KC + 1:KC + 2])
                    last.then_inc(s["relu_ready"], 1)
                    act.wait_ge(s["small_ready"], b + 1)
                    way = slice(d * NH, (d + 1) * NH)
                    nc.scalar.activation(fit[:, way], small[:, way], ACT.Square, scale=SQ_SCALE, bias=fit_bias[:, 0:1])\
                        .then_inc(s["square_ready"], 1)
                if last_but(1):
                    take_tanh(b + 1)
                act.wait_ge(s["skip_ps"], b + 1)
                wait(act, s["skip_out"], 16 * b)
                nc.scalar.copy(skip_p.rearrange("p t c -> p (t c)"), ps[:, 2:4, :].rearrange("p a n -> p (a n)")).then_inc(s["skip_sb"], 1)
                if last_but(2):
                    take_projected(b + 2)

            take_projected(0)
            for g in range(BATCH):
                act.wait_ge(s["mixT_ps"], g + 1)
                wait(act, s["base_ps"], g - 1)
                nc.scalar.copy(mix_wT[0:E, g % 2, :], ps[0:E, 2 + g % 2, :]).then_inc(s["mixT_sb"], 1)
                if g == 1:
                    take_tanh(0)
            take_projected(1)
            act.wait_ge(s["base_sb"], BATCH)
            prepare(0)
            with act.Fori(1, BATCH - 2) as b:
                prepare(b)
            for b in range(BATCH - 2, BATCH):
                prepare(b)
            act.wait_ge(s["decay_free"], 1)

            def empty(b, q):
                for what, j, m, before in events(b, q):
                    bank = m_ps[m]
                    if what == "O":
                        continue
                    bank_written(act, s, b, what, j, m)
                    if what == "T":
                        last = nc.scalar.copy(rowsT[:, :], bank[:, 0:S])
                    elif what in ("U0", "U1"):
                        for f in range(2):
                            c = 2 * (what == "U1") + f
                            last = nc.scalar.activation(hidden[:, j, c, :], bank[:, f * S:(f + 1) * S], ACT.Identity,
                                                        bias=w1[:, j % W_RING, FF + c:FF + c + 1])
                    elif what == "D":
                        wait(act, y_out[j % W_RING], 16 * SH * (MPB // W_RING * (b - before) + j // W_RING))
                        last = nc.scalar.copy(yrows[:, j % W_RING, :, :].rearrange("p a d -> p (a d)"), bank[:, 0:S])
                    elif what == "G":
                        last = nc.scalar.copy(gatedT[:, j, :], bank)
                    last.then_inc(s[f"m{m}_free"], 1)

            def gelus(b, n, now):
                for k in range(GROUP):
                    if isinstance(b, int) and not 0 <= b < BATCH:
                        pass
                    else:
                        if k == 0:
                            for what, m in (("U0", 1), ("U1", 0)):
                                bank_emptied(act, s, b, what, GROUP * (n + 1) - 1, m)
                        h = hidden[:, GROUP * n + k, :, :].rearrange("p f s -> p (f s)")
                        nc.scalar.activation(h, h, ACT.Gelu).then_inc(s["gelu_done"], 1)
                    if k in (1, 3):
                        empty(now, BURST_STEPS[n][k // 2])

            def besides(b, q):
                if not (isinstance(b, int) and b == 0):
                    for p in EMPTY_AFTER[q]:
                        empty(b - 1, p)
                for p in EMPTY[q]:
                    empty(b, p)
                if q in GELU_STEP:
                    n = GELU_STEP.index(q)
                    gelus(b - n, n, b)

            def batch(b, par, i):
                act.wait_ge(s[f"early_in{par}"], 48 * i + 48)
                for q in range(PAIRS):
                    g, dh = q // DH, q % DH
                    wait(act, s["scan_done"], DECAYS * b + 2 * (q - DA_RING) + 2)
                    lo = 1 if dh < NH else 0
                    for j in range(2):
                        nc.scalar.activation(decay[:, q % DA_RING, j, lo:lo + L - 1], delta[:, par, dh, lo:lo + L - 1], ACT.Exp,
                                             scale=a_neg[:, dh, 2 * g + j:2 * g + j + 1]).then_inc(s["decay_ready"], 1)
                    if isinstance(b, int) and b == 0 and q == EMPTY_LAG - 1:
                        act.wait_ge(s["prepared"], 1)
                    besides(b, q)

            batch(0, 0, 0)
            batch(1, 1, 0)
            with act.Fori(1, BATCH // 2) as i:
                batch(2 * i, 0, i)
                batch(2 * i + 1, 1, i)
            for q in range(PAIRS):
                besides(BATCH, q)

        @block.tensor
        def _(pe):
            for g in range(BATCH + 1):
                if g < BATCH:
                    pe.wait_ge(s["xn_ready"], TPB * (g + 1))
                    wait(pe, s["xnT_ready"], g - 3)
                    for t in range(TPB):
                        last = nc.tensor.transpose(ps[:, 2 + g % 4, t * P:(t + 1) * P], xn[:, g * TPB + t, 0:D], ident[:, :])
                    last.then_inc(s["xnT_ps"], 1)
                if g == 1:
                    pe.wait_ge(s["kw_ready"], 1)
                    nc.tensor.matmul(ps[:, 6, 0:E], ones_f, keys_sq, start=True, stop=True).then_inc(s["keys_ps"], 1)
                if g > 0:
                    pe.wait_ge(s["xnT_ready"], g)
                    for t in range((g - 1) * TPB, g * TPB):
                        last = nc.tensor.matmul(ps[:, 7, t * E:(t + 1) * E], xnT[:, t * P:(t + 1) * P], route_w,
                                                start=True, stop=True)
            last.then_inc(s["logit_ps"], 1)
            pe.wait_ge(s["chosen_ready"], 1)
            nc.tensor.matmul(ps[:, 0, :], tri, chosen, start=True, stop=True)
            nc.tensor.matmul(ps[:, 1, :], ones_b, chosen, start=True, stop=True).then_inc(s["rank_ps"], 1)

            def project_in(b):
                pe.wait_ge(s["xb_ready"], b + 1)
                wait(pe, s["relu_ready"], ND * (b - 1))
                wait(pe, s["xpad_ready"], b)
                for h in range(NH):
                    last = nc.tensor.matmul(ps[:, h, :], inw[:, h * P:(h + 1) * P], xb, start=True, stop=True)
                last.then_inc(s["xz_ps"], 1)
                wait(pe, s["part1_ready"], b - 1)
                wait(pe, s["z_sb"], b)
                for t in range(TPB):
                    last = nc.tensor.matmul(ps[:, 4 + t // 2, t % 2 * DIN:(t % 2 + 1) * DIN], xb[:, t * P:(t + 1) * P],
                                            inw[:, DIN:2 * DIN], start=True, stop=True)
                last.then_inc(s["z_ps"], 1)

            def prepare(b):
                ahead = min(b + 2, BATCH) if isinstance(b, int) else b + 2
                pe.wait_ge(s["z_sb"], ahead)
                for d in range(ND):
                    pe.wait_ge(s["u_ready"], ND * b + d + 1)
                    for h in range(NH):
                        last = nc.tensor.matmul(ps[0:BR + NR, 4 + d, :], xproj[:, d, h, :], u[:, d * NH + h, :],
                                                start=h == 0, stop=h == NH - 1)
                    last.then_inc(s["xd_ps"], 1)
                wait(pe, s["skip_sb"], b)
                def skip_tile(t):
                    for h in range(NH):
                        for d in range(ND):
                            o = t % 2 * DIN + h * P
                            last = nc.tensor.matmul(ps[:, 2 + t // 2, o:o + P], u[:, d * NH + h, t * P:(t + 1) * P],
                                                    diag[:, d * NH + h, :], start=d == 0, stop=d == ND - 1)
                    return last
                wait(pe, s["relu_ready"], ND * b)
                pe.wait_ge(s["xpad_ready"], ahead)
                for d in range(ND):
                    pe.wait_ge(s["xd_sb"], ND * b + d + 1)
                    for h in range(NH):
                        last = nc.tensor.matmul(ps[:, DT_BANKS[d * NH + h], :], dtw[BR:BR + NR, d, h * P:(h + 1) * P],
                                                xdbl[BR:BR + NR, d, :], start=True, stop=True)
                    last.then_inc(s["dt_ps"], 1)
                for t in range(TPB):
                    last = skip_tile(t)
                last.then_inc(s["skip_ps"], 1)
                if not isinstance(b, int) or b < BATCH - 2:
                    project_in(b + 2)

            project_in(0)
            pe.wait_ge(s["mix_ready"], 1)
            for g in range(BATCH + 1):
                if g < BATCH:
                    wait(pe, s["mixT_sb"], g - 1)
                    for t in range(TPB):
                        tt = g * TPB + t
                        last = nc.tensor.transpose(ps[0:E, 2 + g % 2, t * P:(t + 1) * P], mix_w[:, tt * E:(tt + 1) * E], ident[:, :])
                    last.then_inc(s["mixT_ps"], 1)
                if g > 0:
                    k = g - 1
                    pe.wait_ge(s["mixT_sb"], k + 1)
                    wait(pe, s["base_sb"], k - 1)
                    for t in range(TPB):
                        last = nc.tensor.matmul(ps[:, 6 + k % 2, t * P:(t + 1) * P], mix_wT[0:E, k % 2, t * P:(t + 1) * P], b2[0:E, :],
                                                start=True, stop=True)
                    last.then_inc(s["base_ps"], 1)
                if g == 3:
                    project_in(1)
            prepare(0)
            with pe.Fori(1, BATCH - 2) as b:
                prepare(b)
            for b in range(BATCH - 2, BATCH):
                prepare(b)
            for n, per in (("skip_sb", 1), ("part1_ready", 1), ("relu_ready", ND)):
                pe.wait_ge(s[n], per * BATCH)

            def sum_states(b, q):
                g, d, h = q // DH, q // NH % ND, q % NH
                product_done(pe, b, q)
                if q < NH:
                    wait(pe, s["y_free"], NH * (b - 1) + h + 1)
                for j in range(2):
                    for t in range(TPB):
                        last = nc.tensor.matmul(y_ps[:, h, t * P:(t + 1) * P], state[:, q % H_RING, j, t * P:(t + 1) * P], ident[:, :],
                                                is_transpose=True, start=q < NH and j == 0 and t == 0,
                                                stop=q >= PAIRS - NH and j == 1, skip_group_check=True)
                last.then_inc(s["summed"], 1)

            def besides(b, q):
                for what, j, m, before in events(b, q):
                    bank, slot = m_ps[m], j % W_RING
                    loads = MPB // W_RING * (b - before) + j // W_RING + 1
                    bank_empty(pe, s, b, what, j, m)
                    if what == "T":
                        pe.wait_ge(rows_in[slot], 16 * loads)
                        for a in range(SH):
                            last = nc.tensor.transpose(bank[:, a * P:(a + 1) * P], rows[:, slot, a, 0:D], ident[:, :])
                    elif what in ("U0", "U1"):
                        if what == "U0":
                            bank_emptied(pe, s, b, "T", j, 0)
                            pe.wait_ge(w1_in_s[slot], 16 * loads)
                        for f in range(2):
                            c = 2 * (what == "U1") + f
                            last = nc.tensor.matmul(bank[:, f * S:(f + 1) * S], w1[:, slot, c * P:(c + 1) * P], rowsT[:, :],
                                                    start=True, stop=True)
                    elif what == "D":
                        pe.wait_ge(w2_in_s[slot], 16 * loads)
                        pe.wait_ge(s["gelu_done"], MPB * (b - before) + j + 1)
                        for a in range(SH):
                            for c in range(FC):
                                last = nc.tensor.matmul(bank[:, a * P:(a + 1) * P], hidden[:, j, c, a * P:(a + 1) * P], w2[:, slot, c, :],
                                                        start=c == 0, stop=c == FC - 1)
                    elif what == "G":
                        pe.wait_ge(s["gated_ready"], NH * (b - 1) + j + 1)
                        for t in range(TPB):
                            last = nc.tensor.transpose(bank[:, t * P:(t + 1) * P], gated[:, j, t, :], ident[:, :])
                    else:
                        for k in range(NH):
                            bank_emptied(pe, s, b, "G", k, k)
                        for t in range(TPB):
                            for h in range(NH):
                                last = nc.tensor.matmul(bank[:, t * P:(t + 1) * P], gatedT[:, h, t * P:(t + 1) * P], outw[:, h, :],
                                                        start=h == 0, stop=h == NH - 1)
                    last.then_inc(s[f"m{m}_ready"], 1)

            def batch(b, par, i):
                first = isinstance(b, int) and b == 0
                pe.wait_ge(s[f"early_in{par}"], 48 * i + 48)
                for q in range(PAIRS):
                    g, d = q // DH, q // NH % ND
                    for j in range(2):
                        tau = 2 * q + j
                        wait(pe, s["scan_done"], DECAYS * b + tau - B_RING + 1)
                        nc.tensor.matmul(b_ps[:, tau % B_RING, :], sel[:, 2 * g + j, :], parts[:, par, d, :],
                                         start=True, stop=True).then_inc(s["b_ready"], 1)
                    besides(b, q)
                    if not first:
                        for k in SUMS_AFTER[q]:
                            sum_states(b - 1, k)
                    for k in SUMS[q]:
                        sum_states(b, k)

            batch(0, 0, 0)
            batch(1, 1, 0)
            with pe.Fori(1, BATCH // 2) as i:
                batch(2 * i, 0, i)
                batch(2 * i + 1, 1, i)
            for q in range(PAIRS):
                for k in SUMS_AFTER[q]:
                    sum_states(BATCH - 1, k)
                besides(BATCH, q)

        @block.vector
        def _(dve):
            done = [0]

            def link(ins):
                done[0] += 1
                ins.then_inc(s["v_chain"], 1)
                dve.wait_ge(s["v_chain"], done[0])

            dve.wait_ge(s["consts_in"], 16)
            nc.vector.tensor_copy(ident[:, :], consts[:, C_ID:C_ID + P])
            nc.vector.tensor_copy(tri, consts[:, C_TRI:C_TRI + P])
            nc.vector.memset(ones_f, 1.0)
            nc.vector.memset(ones_b, 1.0)
            nc.vector.memset(fit_bias[:, :], SQ_BIAS)
            per = NT // XQ
            for k in range(XQ + 1):
                if k < XQ:
                    own = slice(k * per, (k + 1) * per)
                    dve.wait_ge(x_loaded[k], 16)
                    for t in range(k * per, (k + 1) * per):
                        last = nc.vector.bn_stats(stats[:, t, :], x_all[:, t, :])
                    link(last)
                    for t in range(k * per, (k + 1) * per):
                        last = nc.vector.bn_aggr(mv[:, t, :], stats[:, t, :])
                    link(last)
                    nc.vector.tensor_scalar(var_eps[:, own], mv[:, own, 1], EPS, None, ALU.add).then_inc(s["var_ready"], 1)
                if k > 0:
                    own = slice((k - 1) * per, k * per)
                    dve.wait_ge(s["std_ready"], k)
                    link(nc.vector.reciprocal(rstd[:, own], std[:, own]))
                    for t in range((k - 1) * per, k * per):
                        nc.vector.tensor_scalar(xn[:, t, 0:D], x_all[:, t, :], mv[:, t, 0:1], rstd[:, t:t + 1],
                                                ALU.subtract, ALU.mult).then_inc(s["xn_ready"], 1)
                if k == 1:
                    dve.wait_ge(s["route_in"], 32)
                    keysT, rwT, rb = (route[:, n * E:(n + 1) * E] for n in range(3))
                    nc.vector.scalar_tensor_tensor(route_w, keysT, 2.0, rwT, ALU.mult, ALU.add)
                    nc.vector.tensor_tensor(keys_sq, keysT, keysT, ALU.mult).then_inc(s["kw_ready"], 1)
            dve.wait_ge(s["wts_in"], 16 * WTS_DMAS)
            nc.vector.tensor_copy(sel[:, :, :].rearrange("p n m -> p (n m)"), consts[:, C_SEL:C_END])
            nc.vector.tensor_copy(unused[:, :, :].rearrange("p j a -> p (j a)"), consts[:, C_UNUSED:C_SEL])
            nc.vector.tensor_scalar(half_taps[:, :, :], chan[:, :, 0:KC + 1], 0.5, None, ALU.mult)
            for q in range(DH):
                nc.vector.tensor_scalar(diag[:, q, :], consts[:, C_ID:C_ID + P], chan[:, q, KC + 2:KC + 3], None, ALU.mult)
            dve.wait_ge(s["keys_ps"], 1)
            link(nc.vector.tensor_tensor(route_b, rb, ps[:, 6, 0:E], ALU.subtract))
            dve.wait_ge(s["logit_ps"], 1)
            te = lambda ap: ap.rearrange("p (t e) -> p t e", e=E)
            link(nc.vector.tensor_tensor(te(logits), te(ps[:, 7, :]), bc(route_b.unsqueeze(1), [P, NT, E]), ALU.add))
            for t in range(NT):
                last = nc.vector.max(top8[:, t, :], te(logits)[:, t, :])
            link(last)
            for t in range(NT):
                last = nc.vector.max_index(idx8[:, t, :], top8[:, t, :], te(logits)[:, t, :])
            link(last)
            tk = lambda ap: ap.rearrange("p (t k) -> p t k", k=TOPK)
            link(nc.vector.tensor_copy(tk(idxf), idx8[:, :, 0:TOPK]))
            iota = consts[:, C_IOTA:C_IOTA + E]
            tke = lambda ap: ap.rearrange("p (n e) -> p n e", e=E)
            link(nc.vector.tensor_tensor(tke(onehot), bc(idxf.unsqueeze(2), [P, NT * TOPK, E]),
                                         bc(iota.unsqueeze(1), [P, NT * TOPK, E]), ALU.is_equal))
            oh4 = onehot.rearrange("p (t k e) -> p t k e", k=TOPK, e=E)
            with nc.allow_low_precision(reason="zeros and ones"):
                nc.vector.tensor_reduce(te(chosen), oh4.rearrange("p t k e -> p t e k"), AXX, ALU.add).then_inc(s["chosen_ready"], 1)
            dve.wait_ge(s["rank_ps"], 1)
            link(nc.vector.tensor_copy(totals, ps[:, 1, :].rearrange("p (t e) -> p e t", e=E)))
            flat = lambda ap: ap.rearrange("p e t -> p (e t)")
            link(nc.vector.tensor_tensor_scan(flat(upto), consts[:, C_MASK:C_MASK + NT * E], flat(totals), 0.0, ALU.mult, ALU.add))
            cmp1 = compare[:, 0:E * E].rearrange("p (e j) -> p e j", j=E)
            link(nc.vector.tensor_tensor(cmp1, bc(upto[:, :, NT - 1:NT], [P, E, E]),
                                         bc(consts[:, C_THR:C_THR + E].unsqueeze(1), [P, E, E]), ALU.is_gt))
            link(nc.vector.tensor_reduce(n_tiles, cmp1, AXX, ALU.add))
            link(nc.vector.tensor_tensor_scan(end_tile, ones_f[:, 0:E], n_tiles, 0.0, ALU.mult, ALU.add))
            link(nc.vector.tensor_tensor(slot0, end_tile, n_tiles, ALU.subtract))
            link(nc.vector.tensor_scalar(slot0, slot0, float(S), None, ALU.mult))
            link(nc.vector.tensor_tensor(upto, upto, totals, ALU.subtract))
            link(nc.vector.tensor_tensor(upto, upto, bc(slot0.unsqueeze(2), [P, E, NT]), ALU.add))
            link(nc.vector.tensor_tensor(te(place), te(ps[:, 0, :]), upto.rearrange("p e t -> p t e"), ALU.add))
            pr4 = product.rearrange("p (t k e) -> p t k e", k=TOPK, e=E)
            link(nc.vector.tensor_tensor(pr4, oh4, bc(te(place).unsqueeze(2), [P, NT, TOPK, E]), ALU.mult))
            link(nc.vector.tensor_reduce(posf, tke(product), AXX, ALU.add))
            nc.vector.tensor_copy(pos[:, :], posf).then_inc(s["pos_ready"], 1)
            nc.vector.tensor_tensor(tk(idxf), top8[:, :, 0:TOPK], bc(top8[:, :, 0:1], [P, NT, TOPK]),
                                    ALU.subtract).then_inc(s["gdiff_ready"], 1)
            dve.wait_ge(s["gdiff_ready"], 1)
            link(nc.vector.memset(xpad[:, :, :], 0.0))
            nc.vector.tensor_copy(xb, xnT[:, 0:L]).then_inc(s["xb_ready"], 1)
            cmp2 = compare.rearrange("p (t e) -> p t e", e=E)
            link(nc.vector.tensor_tensor(cmp2, bc(end_tile.unsqueeze(1), [P, NTILE, E]),
                                         bc(consts[:, C_TILE:C_TILE + NTILE].unsqueeze(2), [P, NTILE, E]), ALU.is_le))
            link(nc.vector.tensor_reduce(texp, cmp2, AXX, ALU.add))
            link(nc.vector.tensor_scalar(tile_expert[:, :], texp, float(E - 1), None, ALU.min))
            dve.wait_ge(s["gexp_ready"], 1)
            link(nc.vector.tensor_reduce(gsum, tk(gexp), AXX, ALU.add))
            link(nc.vector.reciprocal(grec, gsum))
            link(nc.vector.tensor_tensor(gates[:, :, :], tk(gexp), bc(grec.unsqueeze(2), [P, NT, TOPK]), ALU.mult))
            link(nc.vector.tensor_tensor(tke(product), tke(onehot),
                                         bc(gates[:, :, :].rearrange("p t k -> p (t k)").unsqueeze(2), [P, NT * TOPK, E]), ALU.mult))
            nc.vector.tensor_reduce(te(mix_w), pr4.rearrange("p t k e -> p t e k"), AXX, ALU.add).then_inc(s["mix_ready"], 1)
            dve.wait_ge(s["a_exp"], 1)
            nc.vector.tensor_scalar(a_neg[:, :, :], a_neg[:, :, :], -1.0, None, ALU.mult)

            def residual(g):
                dve.wait_ge(s["base_ps"], g + 1)
                held = (base_lo, base_hi)[g * 2 // BATCH][:, g % (BATCH // 2)]
                nc.vector.tensor_tensor(held, ps[:, 6 + g % 2, :], x_all[:, g * TPB:(g + 1) * TPB, :].rearrange("p t d -> p (t d)"),
                                        ALU.add).then_inc(s["base_sb"], 1)

            def copy_x(b):
                wait(dve, s["z_ps"], b)
                nc.vector.tensor_copy(xb, xnT[:, bass.ds(b * L, L)]).then_inc(s["xb_ready"], 1)

            def convolve(b, between=None):
                dve.wait_ge(s["xpad_ready"], b + 1)
                wait(dve, s["u_ready"], ND * b)
                for k in range(KC):
                    if k == KC - 1 and between is not None:
                        between()
                    for q in range(DH):
                        d, h = q // NH, q % NH
                        o = k if d == 0 else 2 * (KC - 1) - k
                        src = xpad[:, h, o:o + L]
                        if k == 0:
                            ins = nc.vector.tensor_scalar(v[:, q, :], src, half_taps[:, q, 0:1], half_taps[:, q, KC:KC + 1],
                                                          ALU.mult, ALU.add)
                        else:
                            dve.wait_ge(s["v_chain"], start + (KC - 1) * DH * b + (k - 1) * DH + q + 1)
                            ins = nc.vector.scalar_tensor_tensor(v[:, q, :], src, half_taps[:, q, k:k + 1], v[:, q, :],
                                                                 ALU.mult, ALU.add)
                        if k < KC - 1:
                            ins.then_inc(s["v_chain"], 1)
                ins.then_inc(s["v_ready"], 1)

            def take_rest(b):
                dve.wait_ge(s["part1_ready"], b + 1)
                nc.vector.scalar_tensor_tensor(rest[0:BR], part1[0:BR], consts[0:BR, C_PART:C_PART + 1], xdbl[0:BR],
                                               ALU.mult, ALU.add).then_inc(s["rest_ready"], 1)

            def gate_z(b):
                dve.wait_ge(s["z_sb"], b + 1)
                nc.vector.scalar_tensor_tensor(zth, zth, 1.0, zhalf, ALU.add, ALU.mult).then_inc(s["gate_ready"], 1)

            def take_u(b, d):
                way = slice(d * NH, (d + 1) * NH)
                dve.wait_ge(s["th_ready"], b + 1)
                dve.wait_ge(s["v_ready"], b + 1)
                wait(dve, s["skip_ps"], b)
                wait(dve, s["du_ready"], ND * (b - 1) + d + 1)
                nc.vector.scalar_tensor_tensor(u[:, way], th[:, way], 1.0, v[:, way], ALU.add, ALU.mult).then_inc(s["u_ready"], 1)

            def prepare(b):
                last_but = lambda n: not isinstance(b, int) or b < BATCH - n
                if last_but(1):
                    convolve(b + 1, lambda: take_rest(b))
                else:
                    take_rest(b)
                if last_but(2):
                    copy_x(b + 2)
                if last_but(1):
                    gate_z(b + 1)
                dve.wait_ge(s["exp_ready"], b + 1)
                nc.vector.tensor_scalar(small, mag, SMALL, None, ALU.min).then_inc(s["small_ready"], 1)
                dve.wait_ge(s["part2_ready"], b + 1)
                dve.wait_ge(s["rest_ready"], b + 1)
                wait(dve, s["parts_out"], 16 * b)
                nc.vector.scalar_tensor_tensor(parts_p[0:BR], part2[0:BR], consts[0:BR, C_PART + 1:C_PART + 2], rest[0:BR],
                                               ALU.mult, ALU.add).then_inc(s["parts_ready"], 1)
                for d in range(ND):
                    way, n = slice(d * NH, (d + 1) * NH), ND * b + d + 1
                    dve.wait_ge(s["relu_ready"], n)
                    nc.vector.scalar_tensor_tensor(pos_part[:, way], ln1p[:, way], LOG_SMALL, pos_part[:, way], ALU.max, ALU.add)\
                        .then_inc(s["sum_ready"], 1)
                    dve.wait_ge(s["square_ready"], n)
                    dve.wait_ge(s["small_ready"], b + 1)
                    nc.vector.scalar_tensor_tensor(fit[:, way], fit[:, way], SQ_REST, small[:, way], ALU.add, ALU.mult)\
                        .then_inc(s["fit_ready"], 1)
                    dve.wait_ge(s["fit_ready"], n)
                    dve.wait_ge(s["sum_ready"], n)
                    nc.vector.scalar_tensor_tensor(pos_part[:, way], pos_part[:, way], -LOG_SMALL, fit[:, way], ALU.add, ALU.add)\
                        .then_inc(s["delta_ready"], 1)
                    dve.wait_ge(s["delta_ready"], n)
                    dve.wait_ge(s["u_ready"], n)
                    wait(dve, s["du_out"], 16 * b)
                    nc.vector.tensor_tensor(du_p[:, way], pos_part[:, way], u[:, way], ALU.mult).then_inc(s["du_ready"], 1)
                    if last_but(1):
                        take_u(b + 1, d)
                if not last_but(1):
                    dve.wait_ge(s["parts_ready"], BATCH)
                    dve.wait_ge(s["fit_ready"], ND * BATCH)
                    dve.wait_ge(s["dest_free"], TOPK)
                    for r in range(DA_RING):
                        at = 0 if r % DH < NH else L - 1
                        last = nc.vector.memset(decay[:, r, :, at:at + 1], 0.0)
                    last.then_inc(s["decay_free"], 1)

            start = done[0]
            copy_x(1)
            convolve(0)
            gate_z(0)
            for g in range(BATCH):
                residual(g)
            dve.wait_ge(s["base_sb"], BATCH)
            nc.vector.memset(parts_p[BR:P], 0.0)
            for d in range(ND):
                take_u(0, d)
            prepare(0)
            with dve.Fori(1, BATCH - 2) as b:
                prepare(b)
            for b in range(BATCH - 2, BATCH):
                prepare(b)

            for n in ("gate_out", "c_out", "parts_out", "delta_out"):
                dve.wait_ge(s[n], 16 * BATCH)
            dve.wait_ge(s["scattered"], 16 * NT * TOPK)
            dve.wait_ge(s["skip_sb"], BATCH)
            dve.wait_ge(s["du_ready"], ND * BATCH)
            dve.sem_inc(s["prepared"], 1)

            def gate_batch(b, par, i):
                dve.wait_ge(s[f"late_in{par}"], 80 * i + 80)
                for h in range(NH):
                    dve.wait_ge(s["summed"], PAIRS * b + PAIRS - NH + h + 1)
                    nc.vector.tensor_tensor(gated[:, h], y_ps[:, h, :].rearrange("p (t c) -> p t c", t=TPB), skip[:, par, h],
                                            ALU.add).then_inc(s["y_free"], 1)
                for h in range(NH):
                    dve.wait_ge(s["y_free"], NH * b + h + 1)
                    nc.vector.tensor_tensor(gated[:, h], gated[:, h], gate[:, par, h], ALU.mult).then_inc(s["gated_ready"], 1)

            def mix_batch(b, par):
                bank_written(dve, s, b + 1, "O", 0, 1)
                if isinstance(b, int) and b == BATCH - 1:
                    to = acc[:, b * TPB * D:(b + 1) * TPB * D]
                    dve.wait_ge(s["summed"], PAIRS * BATCH)
                else:
                    to = mixed[:, :]
                    wait(dve, s["mixed_out"], 16 * b)
                nc.vector.tensor_tensor(to, m_ps[1], base[:, par, :], ALU.add).then_inc(s["m1_free"], 1)

            def save_dest(b, j):
                slot, before = j % W_RING, MPB // W_RING * b + j // W_RING
                dve.wait_ge(rows_in[slot], 16 * (before + 1))
                wait(dve, y_out[slot], 16 * SH * (before - MPB // W_RING + 1))
                nc.vector.tensor_tensor(dest[:, j, :], rows[:, slot, :, D], unused[:, j, :], ALU.max).then_inc(s["dest_saved"], 1)

            def batch(b, par, i):
                first = isinstance(b, int) and b == 0
                dve.wait_ge(s[f"early_in{par}"], 48 * i + 48)

                def dbx(tau):
                    dve.wait_ge(s["b_ready"], DECAYS * b + tau + 1)
                    bank = b_ps[:, tau % B_RING, :]
                    nc.vector.tensor_tensor(bank, du[:, par, tau // 2 % DH, :], bank, ALU.mult).then_inc(s["dbx_done"], 1)

                dbx(0)
                for q in range(PAIRS):
                    if q == GATE_STEP and not first:
                        gate_batch(b - 1, 1 - par, i if par else i - 1)
                    if q == MIX_STEP and not first:
                        mix_batch(b - 1, 1 - par)
                    if q in T_STEP:
                        save_dest(b, T_STEP.index(q))
                    if q - 1 in VECTOR_PAIRS:
                        r = (q - 1) // NH
                        dve.wait_ge(s["scan_done"], DECAYS * b + 2 * q)
                        dve.wait_ge(c_in[r % C_RING], 16 * (CPB // C_RING * b + r // C_RING + 1))
                        nc.vector.tensor_tensor(state[:, (q - 1) % H_RING], state[:, (q - 1) % H_RING], c_rows[:, r % C_RING],
                                                ALU.mult).then_inc(s["v_prod_done"], 1)
                    for j in range(2):
                        tau = 2 * q + j
                        if tau + 1 < DECAYS:
                            dbx(tau + 1)
                        if j == 0:
                            wait(dve, s["summed"], PAIRS * b + q - H_RING + 1)
                        dve.wait_ge(s["decay_ready"], DECAYS * b + tau + 1)
                        dve.wait_ge(s["dbx_done"], DECAYS * b + tau + 1)
                        way = slice(None) if q % DH < NH else slice(None, None, -1)
                        nc.vector.tensor_tensor_scan(state[:, q % H_RING, j, way], decay[:, q % DA_RING, j, way],
                                                     b_ps[:, tau % B_RING, way], 0.0, ALU.mult, ALU.add).then_inc(s["scan_done"], 1)

            batch(0, 0, 0)
            batch(1, 1, 0)
            with dve.Fori(1, BATCH // 2) as i:
                batch(2 * i, 0, i)
                batch(2 * i + 1, 1, i)
            gate_batch(BATCH - 1, 1, BATCH // 2 - 1)
            mix_batch(BATCH - 1, 1)
            dve.wait_ge(s["acc_in"], 16)
            for g in range(BATCH):
                dve.wait_ge(y_in[g], 16)
                for k in range(TOPK):
                    for t in range(TPB):
                        wait(dve, s["f_chain"], TPB * ((TOPK - 1) * g + k - 1) + t + 1 if k else 0)
                        at = slice((g * TPB + t) * D, (g * TPB + t + 1) * D)
                        nc.vector.scalar_tensor_tensor(acc[:, at], y_tok[g][:, t, k, :], gates[:, g * TPB + t, k:k + 1], acc[:, at],
                                                       ALU.mult, ALU.add).then_inc(s["f_chain" if k < TOPK - 1 else "acc_ready"], 1)


def kernel(**inputs):
    import numpy as np
    import concourse.bacc as bacc
    from concourse.bass_utils import run_bass_kernel_spmd

    a = {k[3:]: np.asarray(v) for k, v in inputs.items()}
    f = lambda n: a["attn_" + n]

    def by_channel(m):
        return np.stack([w.reshape(NH, P, -1) for w in m]).transpose(2, 0, 1, 3).reshape(P, DH, -1)

    consts = np.zeros((P, C_END), np.float32)
    p = np.arange(P)
    consts[:, C_ID:C_ID + P] = np.eye(P)
    consts[:, C_TRI:C_TRI + P] = p[:, None] < p[None, :]
    consts[:, C_IOTA:C_IOTA + E] = np.arange(E)
    consts[:, C_THR:C_THR + E] = S * np.arange(E)
    consts[:, C_TILE:C_TILE + NTILE] = np.arange(NTILE)
    consts[:, C_MASK:C_MASK + NT * E] = np.tile(np.arange(NT) > 0, E)
    consts[:, C_UNUSED:C_SEL] = P * np.arange(MPB * SH)[None, :] + p[:, None]
    consts[:, C_DEST:C_UNUSED] = UNUSED + TOPK * (P * np.arange(NT)[None, :] + p[:, None])
    consts[:, C_PART] = -1.0 * (p >= BR // 3)
    consts[:, C_PART + 1] = -1.0 * (p >= 2 * BR // 3)
    sel = (p[:, None] % (2 * NS) == np.arange(NS)[None, :]) & (p[:, None] < BR)
    consts[:, C_SEL:C_END] = np.repeat(sel, P, axis=1)

    chan = np.concatenate([by_channel([f("conv_w")[:, 0], f("convb_w")[:, 0]]),
                           by_channel([f("conv_bias"), f("convb_bias")]),
                           by_channel([f("dt_proj_bias"), f("dt_proj_b_bias")]),
                           by_channel([f("D_skip"), f("D_b_skip")]),
                           by_channel([f("A_log"), f("A_b_log")])], axis=2)
    xproj = []
    for w in (f("x_proj_w"), f("x_proj_b_w")):
        rows = np.concatenate([w[NR:]] * 3 + [w[:NR]])
        xproj.append(rows.T.reshape(NH, P, BR + NR).transpose(1, 0, 2))
    w1 = a["ffn_w1"].transpose(0, 2, 1)
    b1 = a["ffn_b1"].reshape(E, FC, P).transpose(0, 2, 1)
    arrays = {
        "x": f("hidden_states").reshape(TOK, D),
        "consts": consts,
        "chan": chan,
        "in_w": f("in_proj_w").T,
        "xproj": np.stack(xproj, axis=1),
        "dt_w": np.stack([f("dt_proj_w").T, f("dt_proj_b_w").T], axis=1),
        "out_w": f("out_proj_w").T.reshape(NH, P, D).transpose(1, 0, 2),
        "route": np.concatenate([a["ffn_keys"].T, a["ffn_rw"].T, np.broadcast_to(a["ffn_rb"], (P, E))], axis=1),
        "b2": a["ffn_b2"],
        "w1": np.concatenate([w1, b1], axis=2),
        "w2": a["ffn_w2"].transpose(0, 2, 1).reshape(E, FC, P, D).transpose(0, 2, 1, 3).reshape(E, P, FC * D),
    }
    arrays = {k: np.ascontiguousarray(v) for k, v in arrays.items()}
    nc = bacc.Bacc("TRN2", target_bir_lowering=False, num_devices=1)
    aps = [nc.dram_tensor(k + "_dram", v.shape, mybir.dt.from_np(v.dtype), kind="ExternalInput").ap()
           for k, v in arrays.items()]
    out = nc.dram_tensor("out_dram", (TOK, D), F32, kind="ExternalOutput").ap()
    build_kernel(nc, *aps, out)
    r = run_bass_kernel_spmd(nc, [{k + "_dram": v for k, v in arrays.items()}], core_ids=[0])
    return r.results[0]["out_dram"].reshape(BATCH, L, D)
```
